# Optimizing a Trainium2 kernel written in Bass

```python
import numpy as np
import jax
import jax.numpy as jnp

def _softmax(x, axis=-1):
    return jax.nn.softmax(x, axis=axis)

def _gelu(x):
    return jax.nn.gelu(x, approximate=True)

def _silu(x):
    return jax.nn.silu(x)

def _sigmoid(x):
    return jax.nn.sigmoid(x)

def _layernorm(x, axis=-1, eps=1e-05):
    m = jnp.mean(x, axis=axis, keepdims=True)
    v = jnp.var(x, axis=axis, keepdims=True)
    return (x - m) / jnp.sqrt(v + eps)

def _scatter_add(tgt, idx, src, axis=0):
    return tgt.at[idx].add(src)

def _segment_sum(src, seg, n):
    return jax.ops.segment_sum(src, seg, n)
kernel_name = 'mk_adaln_d1_jaxref_r4_29a58e'

def setup_inputs(seed: int=0):
    np.random.seed(seed)
    _w = jnp.asarray

    def _L0_attn_setup():
        import jax, jax.numpy as jnp
        import numpy as np
        B, S, D = (4, 512, 256)
        KD, VD = (256, 256)
        key = jax.random.key(seed)
        ks = jax.random.split(key, 9)
        sc_in = 1.0 / np.sqrt(D)
        sc_v = 1.0 / np.sqrt(VD)
        return {'x': jax.random.normal(ks[0], (B, S, D), dtype=jnp.float32), 'Wq': jax.random.normal(ks[1], (KD, D), dtype=jnp.float32) * sc_in, 'bq': jax.random.normal(ks[2], (KD,), dtype=jnp.float32) * 0.01, 'Wk': jax.random.normal(ks[3], (KD, D), dtype=jnp.float32) * sc_in, 'bk': jax.random.normal(ks[4], (KD,), dtype=jnp.float32) * 0.01, 'Wv': jax.random.normal(ks[5], (VD, D), dtype=jnp.float32) * sc_in, 'bv': jax.random.normal(ks[6], (VD,), dtype=jnp.float32) * 0.01, 'Wo': jax.random.normal(ks[7], (D, VD), dtype=jnp.float32) * sc_v, 'bo': jax.random.normal(ks[8], (D,), dtype=jnp.float32) * 0.01}
    _L0_attn_in = _L0_attn_setup()

    def _L0_ffn_setup():
        import jax, jax.numpy as jnp
        import numpy as np
        D_MODEL = 256
        NUM_TILES = 64
        TPC = 8
        NUM_CLUSTERS = NUM_TILES // TPC
        GRID = 16
        COMP_H = 64
        NUM_KNOTS = 8
        EPS_LN = 1e-05

        def _calibrate(scores, knots, temperature):
            K = knots.shape[0]
            normalized = jax.nn.sigmoid(scores / (temperature[0] + 1e-06))
            idx_float = normalized * (K - 1)
            idx_low = jnp.clip(idx_float.astype(jnp.int32), 0, K - 2)
            idx_high = idx_low + 1
            t = idx_float - idx_low.astype(scores.dtype)
            val_low = knots[idx_low]
            val_high = knots[idx_high]
            return val_low + t * (val_high - val_low)

        def _forward(x, signatures_raw, knot_values, temperature, compress_w1, compress_b1, compress_w2, compress_b2, spline_w1, spline_b1, spline_w2, spline_b2, directions, norm_gamma, norm_beta, output_scale):
            B, T, D = x.shape
            xf = x.reshape(-1, D)
            q = jnp.where(signatures_raw > 0.3, 1.0, jnp.where(signatures_raw < -0.3, -1.0, 0.0)).astype(signatures_raw.dtype)
            sigs = signatures_raw + jax.lax.stop_gradient(q - signatures_raw)
            cluster_sigs = jnp.sign(sigs.reshape(NUM_CLUSTERS, TPC, D).mean(axis=1))
            cluster_scores = xf @ cluster_sigs.T
            cluster_gates = _calibrate(cluster_scores, knot_values, temperature)
            cluster_idx = jnp.argmax(cluster_gates, axis=-1)
            tile_scores = xf @ sigs.T
            tile_gates = _calibrate(tile_scores, knot_values, temperature)
            gates_by_cluster = tile_gates.reshape(-1, NUM_CLUSTERS, TPC)
            sel_gates = jnp.take_along_axis(gates_by_cluster, cluster_idx[:, None, None], axis=1)[:, 0, :]
            local_idx = jnp.argmax(sel_gates, axis=-1)
            tile_idx = cluster_idx * TPC + local_idx
            h = jax.nn.gelu(xf @ compress_w1 + compress_b1, approximate=False)
            comp = jnp.tanh(h @ compress_w2 + compress_b2)
            w1 = spline_w1[tile_idx]
            b1 = spline_b1[tile_idx]
            hh = jax.nn.relu(jnp.einsum('ni,nig->ng', comp, w1) + b1)
            w2 = spline_w2[tile_idx]
            b2 = spline_b2[tile_idx]
            mag = jnp.einsum('ng,ngo->no', hh, w2) + b2
            ffn_out = mag * directions[tile_idx] * output_scale[0]
            y = xf + ffn_out
            mu = y.mean(axis=-1, keepdims=True)
            var = ((y - mu) ** 2).mean(axis=-1, keepdims=True)
            y = (y - mu) / jnp.sqrt(var + EPS_LN) * norm_gamma + norm_beta
            return y.reshape(B, T, D)
        key = jax.random.key(seed)
        ks = jax.random.split(key, 12)
        B, T = (4, 1024)
        x = jax.random.normal(ks[0], (B, T, D_MODEL), dtype=jnp.float32)
        signatures_raw = jax.random.normal(ks[1], (NUM_TILES, D_MODEL), dtype=jnp.float32) * 0.5
        knot_values = jax.nn.sigmoid(jnp.linspace(-3.0, 3.0, NUM_KNOTS).astype(jnp.float32))
        temperature = jnp.ones((1,), dtype=jnp.float32)
        compress_w1 = jax.random.normal(ks[2], (D_MODEL, COMP_H), dtype=jnp.float32) * (1.0 / np.sqrt(D_MODEL))
        compress_b1 = jnp.zeros((COMP_H,), dtype=jnp.float32)
        compress_w2 = jax.random.normal(ks[3], (COMP_H, 2), dtype=jnp.float32) * (1.0 / np.sqrt(COMP_H))
        compress_b2 = jnp.zeros((2,), dtype=jnp.float32)
        spline_w1 = jax.random.normal(ks[4], (NUM_TILES, 2, GRID), dtype=jnp.float32) * (1.0 / np.sqrt(2.0))
        spline_b1 = jnp.zeros((NUM_TILES, GRID), dtype=jnp.float32)
        spline_w2 = jax.random.normal(ks[5], (NUM_TILES, GRID, 1), dtype=jnp.float32) * (1.0 / np.sqrt(GRID))
        spline_b2 = jnp.zeros((NUM_TILES, 1), dtype=jnp.float32)
        directions = jax.random.normal(ks[6], (NUM_TILES, D_MODEL), dtype=jnp.float32) * 0.02
        norm_gamma = jnp.ones((D_MODEL,), dtype=jnp.float32)
        norm_beta = jnp.zeros((D_MODEL,), dtype=jnp.float32)
        output_scale = jnp.ones((1,), dtype=jnp.float32) * 0.1
        return dict(x=x, signatures_raw=signatures_raw, knot_values=knot_values, temperature=temperature, compress_w1=compress_w1, compress_b1=compress_b1, compress_w2=compress_w2, compress_b2=compress_b2, spline_w1=spline_w1, spline_b1=spline_b1, spline_w2=spline_w2, spline_b2=spline_b2, directions=directions, norm_gamma=norm_gamma, norm_beta=norm_beta, output_scale=output_scale)
    _L0_ffn_in = _L0_ffn_setup()
    _L0_c = _w((lambda *s: np.random.randn(*s).astype(np.float32) * 0.05)(16, 256))
    _L0_wmod = _w((lambda *s: np.random.randn(*s).astype(np.float32) * 0.05)(256, 6 * 256) * 256 ** (-0.5))
    _d = {'L0_attn_x': _L0_attn_in['x'], 'L0_attn_Wq': _L0_attn_in['Wq'], 'L0_attn_bq': _L0_attn_in['bq'], 'L0_attn_Wk': _L0_attn_in['Wk'], 'L0_attn_bk': _L0_attn_in['bk'], 'L0_attn_Wv': _L0_attn_in['Wv'], 'L0_attn_bv': _L0_attn_in['bv'], 'L0_attn_Wo': _L0_attn_in['Wo'], 'L0_attn_bo': _L0_attn_in['bo'], 'L0_ffn_signatures_raw': _L0_ffn_in['signatures_raw'], 'L0_ffn_knot_values': _L0_ffn_in['knot_values'], 'L0_ffn_temperature': _L0_ffn_in['temperature'], 'L0_ffn_compress_w1': _L0_ffn_in['compress_w1'], 'L0_ffn_compress_b1': _L0_ffn_in['compress_b1'], 'L0_ffn_compress_w2': _L0_ffn_in['compress_w2'], 'L0_ffn_compress_b2': _L0_ffn_in['compress_b2'], 'L0_ffn_spline_w1': _L0_ffn_in['spline_w1'], 'L0_ffn_spline_b1': _L0_ffn_in['spline_b1'], 'L0_ffn_spline_w2': _L0_ffn_in['spline_w2'], 'L0_ffn_spline_b2': _L0_ffn_in['spline_b2'], 'L0_ffn_directions': _L0_ffn_in['directions'], 'L0_ffn_norm_gamma': _L0_ffn_in['norm_gamma'], 'L0_ffn_norm_beta': _L0_ffn_in['norm_beta'], 'L0_ffn_output_scale': _L0_ffn_in['output_scale'], 'L0_c': _L0_c, 'L0_wmod': _L0_wmod}
    _x0 = _d['L0_attn_x']
    _d['L0_attn_x'] = jax.random.normal(jax.random.fold_in(jax.random.key(seed), 1), (16, 512, 256), dtype=_x0.dtype)
    del _x0
    return _d

def reference(L0_attn_x, L0_attn_Wq, L0_attn_bq, L0_attn_Wk, L0_attn_bk, L0_attn_Wv, L0_attn_bv, L0_attn_Wo, L0_attn_bo, L0_ffn_signatures_raw, L0_ffn_knot_values, L0_ffn_temperature, L0_ffn_compress_w1, L0_ffn_compress_b1, L0_ffn_compress_w2, L0_ffn_compress_b2, L0_ffn_spline_w1, L0_ffn_spline_b1, L0_ffn_spline_w2, L0_ffn_spline_b2, L0_ffn_directions, L0_ffn_norm_gamma, L0_ffn_norm_beta, L0_ffn_output_scale, L0_c, L0_wmod):

    def _L0_attn_ref(x, Wq, bq, Wk, bk, Wv, bv, Wo, bo):
        import jax, jax.numpy as jnp
        import numpy as np
        B, S, D = (4, 512, 256)
        KD, VD = (256, 256)
        q = jnp.einsum('bsd,kd->bsk', x, Wq) + bq
        k = jnp.einsum('bsd,kd->bsk', x, Wk) + bk
        v = jnp.einsum('bsd,vd->bsv', x, Wv) + bv
        scores = jnp.einsum('bqk,bsk->bqs', q, k) / jnp.sqrt(jnp.float32(KD))
        sign_mask = jnp.sign(scores)
        sign_mask = sign_mask + (sign_mask == 0).astype(jnp.float32)
        seq = scores.shape[-1]
        causal = jnp.tril(jnp.ones((seq, seq), dtype=bool))
        masked = jnp.where(causal, scores * sign_mask, -jnp.inf)
        weights = jax.nn.softmax(masked, axis=2)
        out = jnp.einsum('bqs,bsv->bqv', weights, v)
        return jnp.einsum('bqv,dv->bqd', out, Wo) + bo

    def _L0_ffn_ref(x, signatures_raw, knot_values, temperature, compress_w1, compress_b1, compress_w2, compress_b2, spline_w1, spline_b1, spline_w2, spline_b2, directions, norm_gamma, norm_beta, output_scale):
        import jax, jax.numpy as jnp
        import numpy as np
        D_MODEL = 256
        NUM_TILES = 64
        TPC = 8
        NUM_CLUSTERS = NUM_TILES // TPC
        GRID = 16
        COMP_H = 64
        NUM_KNOTS = 8
        EPS_LN = 1e-05

        def _calibrate(scores, knots, temperature):
            K = knots.shape[0]
            normalized = jax.nn.sigmoid(scores / (temperature[0] + 1e-06))
            idx_float = normalized * (K - 1)
            idx_low = jnp.clip(idx_float.astype(jnp.int32), 0, K - 2)
            idx_high = idx_low + 1
            t = idx_float - idx_low.astype(scores.dtype)
            val_low = knots[idx_low]
            val_high = knots[idx_high]
            return val_low + t * (val_high - val_low)

        def _forward(x, signatures_raw, knot_values, temperature, compress_w1, compress_b1, compress_w2, compress_b2, spline_w1, spline_b1, spline_w2, spline_b2, directions, norm_gamma, norm_beta, output_scale):
            B, T, D = x.shape
            xf = x.reshape(-1, D)
            q = jnp.where(signatures_raw > 0.3, 1.0, jnp.where(signatures_raw < -0.3, -1.0, 0.0)).astype(signatures_raw.dtype)
            sigs = signatures_raw + jax.lax.stop_gradient(q - signatures_raw)
            cluster_sigs = jnp.sign(sigs.reshape(NUM_CLUSTERS, TPC, D).mean(axis=1))
            cluster_scores = xf @ cluster_sigs.T
            cluster_gates = _calibrate(cluster_scores, knot_values, temperature)
            cluster_idx = jnp.argmax(cluster_gates, axis=-1)
            tile_scores = xf @ sigs.T
            tile_gates = _calibrate(tile_scores, knot_values, temperature)
            gates_by_cluster = tile_gates.reshape(-1, NUM_CLUSTERS, TPC)
            sel_gates = jnp.take_along_axis(gates_by_cluster, cluster_idx[:, None, None], axis=1)[:, 0, :]
            local_idx = jnp.argmax(sel_gates, axis=-1)
            tile_idx = cluster_idx * TPC + local_idx
            h = jax.nn.gelu(xf @ compress_w1 + compress_b1, approximate=False)
            comp = jnp.tanh(h @ compress_w2 + compress_b2)
            w1 = spline_w1[tile_idx]
            b1 = spline_b1[tile_idx]
            hh = jax.nn.relu(jnp.einsum('ni,nig->ng', comp, w1) + b1)
            w2 = spline_w2[tile_idx]
            b2 = spline_b2[tile_idx]
            mag = jnp.einsum('ng,ngo->no', hh, w2) + b2
            ffn_out = mag * directions[tile_idx] * output_scale[0]
            y = xf + ffn_out
            mu = y.mean(axis=-1, keepdims=True)
            var = ((y - mu) ** 2).mean(axis=-1, keepdims=True)
            y = (y - mu) / jnp.sqrt(var + EPS_LN) * norm_gamma + norm_beta
            return y.reshape(B, T, D)
        return _forward(x, signatures_raw, knot_values, temperature, compress_w1, compress_b1, compress_w2, compress_b2, spline_w1, spline_b1, spline_w2, spline_b2, directions, norm_gamma, norm_beta, output_scale)
    x = L0_attn_x
    mod = (_silu(L0_c) @ L0_wmod).reshape(L0_c.shape[0], 6, 1, -1)
    sa, ca, ga, sb, cb, gb = (mod[:, 0], mod[:, 1], mod[:, 2], mod[:, 3], mod[:, 4], mod[:, 5])
    ga = (2 * (ga >= 0) - 1) * jnp.maximum(jnp.abs(ga), 0.25)
    gb = (2 * (gb >= 0) - 1) * jnp.maximum(jnp.abs(gb), 0.25)
    h = _layernorm(x, axis=-1) * (1 + ca) + sa
    x = x + ga * _L0_attn_ref(h, L0_attn_Wq, L0_attn_bq, L0_attn_Wk, L0_attn_bk, L0_attn_Wv, L0_attn_bv, L0_attn_Wo, L0_attn_bo)
    h = _layernorm(x, axis=-1) * (1 + cb) + sb
    x = x + gb * _L0_ffn_ref(h, L0_ffn_signatures_raw, L0_ffn_knot_values, L0_ffn_temperature, L0_ffn_compress_w1, L0_ffn_compress_b1, L0_ffn_compress_w2, L0_ffn_compress_b2, L0_ffn_spline_w1, L0_ffn_spline_b1, L0_ffn_spline_w2, L0_ffn_spline_b2, L0_ffn_directions, L0_ffn_norm_gamma, L0_ffn_norm_beta, L0_ffn_output_scale)
    return x

_drawn_inputs = setup_inputs


def setup_inputs(seed=0):
    import zlib

    import numpy as np

    out = dict(_drawn_inputs(seed))
    spreads = {'L0_ffn_compress_b1': (0.0, 0.8),
     'L0_ffn_compress_b2': (0.0, 2.0),
     'L0_ffn_spline_b1': (0.0, 2.0),
     'L0_ffn_spline_b2': (0.0, 2.0),
     'L0_ffn_norm_gamma': (1.0, 0.2),
     'L0_ffn_norm_beta': (0.0, 0.325)}
    factors = {'L0_attn_bq': 44.344,
     'L0_attn_bk': 50.528,
     'L0_attn_bv': 8.0,
     'L0_attn_bo': 8.0,
     'L0_ffn_signatures_raw': 8.0,
     'L0_ffn_knot_values': 8.0,
     'L0_ffn_compress_w1': 8.0,
     'L0_ffn_compress_w2': 8.0,
     'L0_ffn_spline_w1': 8.0,
     'L0_ffn_spline_w2': 8.0,
     'L0_ffn_directions': 8.0}
    for name, (base, spread) in spreads.items():
        noise = np.random.default_rng([zlib.crc32(name.encode()), seed]).standard_normal(out[name].shape)
        drawn = base * np.exp(spread * noise) if base else spread * noise
        out[name] = jnp.asarray(drawn.astype(out[name].dtype))
    for name, factor in factors.items():
        out[name] = (out[name] * factor).astype(out[name].dtype)
    return out
```

```python
from contextlib import ExitStack

import concourse.bass as bass
from concourse import mybir

F32 = mybir.dt.float32
F32R = mybir.dt.float32r
BF16 = mybir.dt.bfloat16
ALU = mybir.AluOpType
ACT = mybir.ActivationFunctionType
X = mybir.AxisListType.X

P = 128
EPS = 1e-5
TEMP_EPS = 1e-6
Z_MIN = -88.0
MASKED = -1e30
GATE_MIN = 0.25


LOADS_SP, LOADS_ACT = 21, 10
SIG_READY, SILU_READY, CT_READY, ROWS_READY, DVE_SETUP = 21, 24, 25, 32, 62
WOT_READY = ACT_SETUP = 2
POOL_SETUP = 4
DVE_C = 82


class Chain:

    def __init__(self, sem, per):
        self.sem, self.per, self.n = sem, per, 0

    def start(self, i):
        assert self.n in (0, self.per), (str(self.sem), self.n, self.per)
        self.i, self.n = i, 0

    def mark(self, ins):
        self.n += 1
        ins.then_inc(self.sem, 1)

    def wait(self, eng):
        eng.wait_ge(self.sem, self.per * self.i + self.n)

    def link(self, eng, ins):
        self.mark(ins)
        self.wait(eng)


def need(eng, sem, count):
    if isinstance(count, int) and count <= 0:
        return
    eng.wait_ge(sem, count)


def adaln_kernel(nc, ins, out):
    x_in, wq_in, wo_in = ins["L0_attn_x"], ins["L0_attn_Wq"], ins["L0_attn_Wo"]
    B, S, D = x_in.shape
    NT = S // P
    KC = D // P
    PAIRS = B // 2
    PT = 2 * NT
    NTILES = ins["L0_ffn_signatures_raw"].shape[0]
    K = ins["L0_ffn_knot_values"].shape[0]
    H = ins["L0_ffn_compress_w1"].shape[1]
    GRID = ins["L0_ffn_spline_b1"].shape[1]
    TPC = 8
    NCL = NTILES // TPC
    NCOMP = ins["L0_ffn_compress_w2"].shape[1]
    VW = D + 2
    FW = NCL + NTILES + H
    PAR = NCOMP * GRID + 2 * GRID + 2
    GW = PAR + D
    SCALE = float(D) ** -0.5
    assert NT == 4 and KC == 2 and NCL == 8 and 2 * NTILES == P and SCALE == 0.0625

    gate_rows = nc.dram_tensor("gate_rows", (B, 3 * D), F32, kind="Internal").ap()

    with ExitStack() as ctx:
        def sb(name, shape, dt=F32):
            return ctx.enter_context(nc.sbuf_tensor(name, shape, dt))

        def sem(name):
            return ctx.enter_context(nc.semaphore(name))

        banks = [ctx.enter_context(nc.psum_tensor(f"bank{i}", [P, 512], F32)) for i in range(8)]
        turn_ps = banks[0:2]
        mix_ps = banks[2:5]
        score_ps = banks[5:7]
        attn_ps = banks[7]
        TURN = dict(H2T0=0, H2T1=1, PTe0=0, XTo0=1, XTo1=0, PTe1=1, H2T2=0, H2T3=1, PTe2=0, PTe3=1,
                    PTo0=0, PTo1=1, XTe0=0, XTe1=1, OHT0=0, PTo2=1, OHT1=0, PTo3=1)
        mix_order = ([f"Ge{c}" for c in range(KC)] + [f"Ve{t}" for t in range(NT)]
                     + [f"FS{u}" for u in range(3)] + [f"BT{u}" for u in range(NT)]
                     + [f"Go{c}" for c in range(KC)] + [f"Vo{t}" for t in range(NT)]
                     + [f"GA{t}" for t in range(PT)])
        MIX = {name: i % 3 for i, name in enumerate(mix_order)}
        SEQ = "eo"

        ident = sb("ident", [P, P])
        identb = sb("identb", [P, P], BF16)
        causal = sb("causal", [P, P])
        ones2 = sb("ones2", [2, P], F32R)
        a_hi = sb("a_hi", [P, KC, D], F32R)
        a_lo = sb("a_lo", [P, KC, D], F32R)
        m_hi = sb("m_hi", [P, KC, VW], F32R)
        m_lo = sb("m_lo", [P, KC, VW], F32R)
        vbias = sb("vbias", [2, VW], F32R)
        g_bias = sb("g_bias", [P, KC])
        f_hi = sb("f_hi", [P, KC, FW], F32R)
        f_lo = sb("f_lo", [P, KC, FW], F32R)
        table = sb("table", [P, GW], F32R)
        sa_col = sb("sa_col", [P, KC, B])
        ca_col = sb("ca_col", [P, KC, B])
        sb_col = sb("sb_col", [P, KC, B])
        cb_col = sb("cb_col", [P, KC, B])
        b1_row = sb("b1_row", [P, H])
        w2_rows = sb("w2_rows", [P, H, NCOMP])
        b2_row = sb("b2_row", [P, NCOMP])
        knots = sb("knots", [P, K])
        knot_step = sb("knot_step", [P, K - 1])
        inv_temp = sb("inv_temp", [P, 1])
        out_scale = sb("out_scale", [P, 1])
        steps = sb("steps", [P, K])
        falling = sb("falling", [P, TPC])

        x_sb = [sb(f"x{s}", [P, NT, D]) for s in range(2)]
        st1 = sb("st1", [P, NT, 6])
        sum1, dif1, var1, guess1, newt1, rstd1, nmr1 = (
            sb(n, [P, NT]) for n in ("sum1", "dif1", "var1", "guess1", "newt1", "rstd1", "nmr1"))
        xhat = sb("xhat", [P, NT, D])
        h_full = sb("h_full", [P, KC, S])
        h_hi = [sb(f"h_hi{s}", [P, KC, S], F32R) for s in range(2)]
        h_lo = [sb(f"h_lo{s}", [P, KC, S], F32R) for s in range(2)]
        ga_row = [sb(f"ga_row{s}", [P, D]) for s in range(2)]
        g_hi = sb("g_hi", [P, KC, S], F32R)
        g_lo = sb("g_lo", [P, KC, S], F32R)
        v_sb = [sb(f"v{s}", [P, NT, VW]) for s in range(2)]
        absc = [sb(f"absc{j}", [P, S]) for j in range(2)]
        probs = [sb(f"probs{j}", [P, S]) for j in range(2)]
        probsT = [sb(f"probsT{j}", [P, S]) for j in range(2)]
        negmax = sb("negmax", [P, NT])
        rowsum = [sb(f"rowsum{s}", [P, NT]) for s in range(2)]
        rinv = sb("rinv", [P, NT])
        gated = [sb(f"gated{j}", [P, D]) for j in range(2)]
        x2 = [sb(f"x2_{s}", [P, NT, D]) for s in range(2)]
        st2 = sb("st2", [P, PT, 6])
        gb_row = [sb(f"gb_row{s}", [P, 2, D]) for s in range(2)]
        sum2, dif2, var2, guess2, newt2, rstd2, nmr2 = (
            sb(n, [P, PT]) for n in ("sum2", "dif2", "var2", "guess2", "newt2", "rstd2", "nmr2"))
        wide = sb("wide", [P, 4 * KC * S])
        xhat2 = wide[:, 0:PT * D].rearrange("p (t d) -> p t d", t=PT)
        h2_full = wide[:, PT * D:].rearrange("p (s c t) -> p s c t", s=2, c=KC)
        h2_hi = sb("h2_hi", [P, 2, KC, S], F32R)
        h2_lo = sb("h2_lo", [P, 2, KC, S], F32R)
        h2_tok = sb("h2_tok", [P, PT, D])
        fs = sb("fs", [P, PT, FW])
        hid = sb("hid", [P, PT, H])
        w2prod = sb("w2prod", [P, PT, NCOMP, H])
        comp = sb("comp", [P, PT, NCOMP])
        cmp_t = sb("cmp_t", [P, PT, NCOMP])
        E8 = PT * TPC
        z_cl = sb("z_cl", [P, E8])
        z_lo = sb("z_lo", [P, E8])
        cal = [sb(f"cal{j}", [P, E8]) for j in range(5)]
        cal7 = [sb(f"cal7_{j}", [P, E8, K - 1]) for j in range(2)]
        best = sb("best", [P, PT])
        oh_cl = sb("oh_cl", [P, PT, NCL])
        oh_lo = sb("oh_lo", [P, PT, TPC])
        picked = sb("picked", [P, PT, NTILES])
        onehot = sb("onehot", [P, PT, P], BF16)
        onehotT = sb("onehotT", [P, PT * P], F32R)
        gath = sb("gath", [P, PT, GW])
        sp0 = sb("sp0", [P, PT, GRID])
        sp1 = sb("sp1", [P, PT, GRID])
        mag = sb("mag", [P, PT])
        y = sb("y", [P, PT, D])
        st3 = sb("st3", [P, PT, 6])
        sum3, dif3, var3, guess3, newt3, rstd3, nmr3 = (
            sb(n, [P, PT]) for n in ("sum3", "dif3", "var3", "guess3", "newt3", "rstd3", "nmr3"))
        res = sb("res", [P, PT, D])

        w_in = sem("w_in")
        x_ld = [sem(f"x_loaded{s}") for s in range(2)]
        ga_ld = [sem(f"ga_loaded{s}") for s in range(2)]
        gb_ld = [sem(f"gb_loaded{s}") for s in range(2)]
        sent = [sem(f"out_sent{s}") for s in range(2)]
        rows_sent = sem("rows_sent")
        id_ready = sem("ident_ready")
        s_pe, s_dve, s_act, s_pool = sem("setup_pe"), sem("setup_dve"), sem("setup_act"), sem("setup_pool")
        ln1_var, ln1_guess, ln1_ready = sem("ln1_var"), sem("ln1_guess"), sem("ln1_ready")
        xhat_ready = sem("xhat_ready")
        xt_done = sem("xhat_turned")
        h_ready = sem("h_ready")
        h_hi_rdy = sem("h_hi_ready")
        h_lo_rdy = sem("h_lo_ready")
        g_done = sem("g_done")
        g_hi_rdy, g_lo_rdy = sem("g_hi_ready"), sem("g_lo_ready")
        vproj_done = sem("v_done")
        v_ready = sem("v_ready")
        scores_done = sem("scores_done")
        absc_ready = sem("abs_scores_ready")
        masked = sem("diag_masked")
        rowmax = sem("rowmax_ready")
        probs_rdy = sem("probs_ready")
        pt_done = sem("probs_turned")
        pt_rdy = sem("probsT_ready")
        pv_done = sem("pv_done")
        st2_rdy = sem("x2_stats_ready")
        gated_rdy = sem("gated_ready")
        x2_rdy = sem("x2_ready")
        ln2_var = sem("ln2_var")
        ln2_guess, ln2_ready = sem("ln2_guess"), sem("ln2_ready")
        xhat2_rdy = sem("xhat2_ready")
        h2t_done = sem("xhat2_turned")
        h2_rdy = sem("h2_ready")
        h2_hi_rdy, h2_lo_rdy = sem("h2_hi_ready"), sem("h2_lo_ready")
        fs_done = sem("ffn_scores_done")
        fs_rdy = sem("ffn_scores_ready")
        bt_done = sem("h2_turned_back")
        h2_tok_rdy = sem("h2_tok_ready")
        zc_rdy, ec_rdy = sem("cluster_z_ready"), sem("cluster_exp_ready")
        zl_rdy, el_rdy = sem("local_z_ready"), sem("local_exp_ready")
        pregelu, gelu_rdy = sem("pregelu_ready"), sem("gelu_ready")
        pretanh, tanh_rdy = sem("pretanh_ready"), sem("tanh_ready")
        onehot_rdy = sem("onehot_ready")
        oht_done = sem("onehot_turned")
        oht_rdy = sem("onehotT_ready")
        ga_done = sem("gather_done")
        gath_rdy = sem("gathered_ready")
        ln3_var, ln3_guess, ln3_ready = sem("ln3_var"), sem("ln3_guess"), sem("ln3_ready")
        yhat_rdy = sem("yhat_ready")
        res_rdy = sem("result_ready")
        y_sem = sem("y_ready")
        act_guess1 = Chain(sem("act_chain_a"), 1)
        act_guess2 = Chain(sem("act_chain_c"), 2)
        dve_a = Chain(sem("dve_chain_a"), NT + 5 + 3)
        dve_b = Chain(sem("dve_chain_b"), NT)
        dve_c = Chain(sem("dve_chain_c"), DVE_C)
        pool_c = Chain(sem("pool_chain_c"), 4)

        wq, wk, wv, wo = (res[:, KC * i:KC * (i + 1), :] for i in range(4))
        woT = sb("woT", [P, KC, D])
        wmod_sb = wide[:, 0:KC * 6 * D].rearrange("p (c n) -> p c n", c=KC)
        bq, bk, bv = (sb(n, [P, KC]) for n in ("bq", "bk", "bv"))
        bo2 = sb("bo2", [2, D])
        c_sb = sb("c_sb", [B, D])
        c_exp = sb("c_exp", [B, D])
        c_T = sb("c_T", [P, KC, B])
        mod = sb("mod", [B, 3, D])
        rows = sb("rows", [B, 3, D])
        gamma_r, beta_r = sb("gamma_r", [B, D]), sb("beta_r", [B, D])
        sraw = sb("sraw", [NTILES, D])
        sraw8 = h2_tok[0:NCL, :, :]
        sq = sb("sq", [NTILES, D])
        sq8 = y[0:NCL, :, :]
        stmp = sb("stmp", [NTILES, D])
        stmp8 = gath[0:NCL, :, 0:D]
        f_full = sb("f_full", [P, KC, FW])
        t_full = sb("t_full", [P, GW])
        vb2 = sb("vb2", [2, VW])
        vb2_hi, vb2_lo = sb("vb2_hi", [2, VW], F32R), sb("vb2_lo", [2, VW])

        block = ctx.enter_context(nc.Block())

        def seq(k, s):
            return 2 * k + s

        @block.sync
        def _(sp):
            def col(a):
                return a.rearrange("(c p) -> p c", p=P)

            def row(a, n):
                return a.rearrange("(o d) -> o d", o=1).broadcast_to([n, a.shape[0]])

            n = [0]

            def load(dst, src, **kw):
                sp.dma_start(dst, src, **kw).then_inc(w_in, 16)
                n[0] += 1

            x_v = x_in.rearrange("b (t p) d -> b p t d", p=P)
            out_v = out.rearrange("b (t p) d -> b p t d", p=P)

            sp.dma_start(x_sb[0][:, :, :], x_v[0]).then_inc(x_ld[0], 16)
            sp.dma_start(x_sb[1][:, :, :], x_v[1]).then_inc(x_ld[1], 16)
            load(c_sb[:, :], ins["L0_c"])
            load(wmod_sb[:, :, :], ins["L0_wmod"].rearrange("(c p) n -> p c n", p=P))
            for w, name in ((wq, "Wq"), (wk, "Wk"), (wo, "Wo"), (wv, "Wv")):
                load(w[:, :, :], ins[f"L0_attn_{name}"].rearrange("(c p) n -> p c n", p=P))
            for w, name in ((bq, "bq"), (bk, "bk"), (bv, "bv")):
                load(w[:, :], col(ins[f"L0_attn_{name}"]), allow_slow_non_contiguous=True)
            load(bo2[:, :], row(ins["L0_attn_bo"], 2))
            raw = ins["L0_ffn_signatures_raw"]
            load(sraw[:, :], raw)
            load(sraw8[:, :, :], raw.rearrange("(c j) d -> c j d", j=TPC))
            load(f_full[:, :, NCL + NTILES:FW], ins["L0_ffn_compress_w1"].rearrange("(c p) n -> p c n", p=P))
            load(b1_row[:, :], row(ins["L0_ffn_compress_b1"], P))
            load(w2_rows[:, :, :].rearrange("p h o -> p (h o)"),
                 ins["L0_ffn_compress_w2"].rearrange("(a h) o -> a (h o)", a=1).broadcast_to([P, H * NCOMP]))
            load(b2_row[:, :], row(ins["L0_ffn_compress_b2"], P))
            load(knots[:, :], row(ins["L0_ffn_knot_values"], P))
            load(inv_temp[:, :], row(ins["L0_ffn_temperature"], P))
            load(out_scale[:, :], row(ins["L0_ffn_output_scale"], P))
            load(gamma_r[:, :], row(ins["L0_ffn_norm_gamma"], B))
            load(beta_r[:, :], row(ins["L0_ffn_norm_beta"], B))
            assert n[0] == LOADS_SP

            sp.wait_ge(s_dve, ROWS_READY)
            sp.dma_start(gate_rows, rows[:, :, :].rearrange("b a d -> b (a d)")).then_inc(rows_sent, 16)
            sp.wait_ge(rows_sent, 16)

            def gate_row(i, a, n_rows):
                r = gate_rows[bass.ds(i, 1), a * D:(a + n_rows) * D]
                return r.broadcast_to([P, n_rows * D])

            def load_ga(k, s):
                sp.dma_start(ga_row[s][:, :], gate_row(seq(k, s), 0, 1)).then_inc(ga_ld[s], 16)

            load_ga(0, 0)
            load_ga(0, 1)

            def superstep(k, c, nxt):
                if c is not None:
                    for s in range(2):
                        need(sp, res_rdy, 2 * c)
                        sp.dma_start(gb_row[s][:, :, :].rearrange("p a d -> p (a d)"),
                                     gate_row(seq(c, s), 1, 2)).then_inc(gb_ld[s], 16)
                for s in range(2):
                    if nxt:
                        sp.wait_ge(x2_rdy, NT * seq(k, s) + NT)
                        sp.dma_start(x_sb[s][:, :, :], x_v[bass.ds(seq(k + 1, s), 1)].rearrange("o p t d -> (o p) t d")
                                     ).then_inc(x_ld[s], 16)
                        load_ga(k + 1, s)
                    if c is not None:
                        sp.wait_ge(res_rdy, 2 * c + s + 1)
                        sp.dma_start(out_v[bass.ds(seq(c, s), 1)].rearrange("o p t d -> (o p) t d"),
                                     res[:, NT * s:NT * (s + 1), :]).then_inc(sent[s], 16)

            superstep(0, None, True)
            superstep(1, 0, True)
            with sp.Fori(2, PAIRS - 1) as k:
                superstep(k, k - 1, True)
            superstep(PAIRS - 1, PAIRS - 2, False)
            superstep(PAIRS, PAIRS - 1, False)
            for s in range(2):
                sp.wait_ge(sent[s], 16 * PAIRS)

        @block.tensor
        def _(pe):
            mm, tr = nc.tensor.matmul, nc.tensor.transpose
            pe.wait_ge(id_ready, 1)
            pe.wait_ge(w_in, 16 * (LOADS_SP + LOADS_ACT))
            for m in range(KC):
                for c in range(KC):
                    last = mm(banks[0][:, m * D:(m + 1) * D], wq[:, c, m * P:(m + 1) * P], wk[:, c, :],
                              start=(c == 0), stop=(c == KC - 1))
            last.then_inc(s_pe, 1)
            for v in range(KC):
                for o in range(KC):
                    last = tr(banks[1][:, v * D + o * P:v * D + (o + 1) * P], wo[:, o, v * P:(v + 1) * P], ident[:, :])
            last.then_inc(s_pe, 1)
            for m in range(KC):
                for c in range(KC):
                    mm(banks[3][:, m:m + 1], wq[:, c, m * P:(m + 1) * P], bk[:, c:c + 1],
                       start=(c == 0), stop=(c == KC - 1))
                for c in range(KC):
                    last = mm(banks[3][:, KC + m:KC + m + 1], wk[:, c, m * P:(m + 1) * P], bq[:, c:c + 1],
                              start=(c == 0), stop=(c == KC - 1))
            last.then_inc(s_pe, 1)
            pe.wait_ge(s_dve, SIG_READY)
            for c in range(KC):
                tr(banks[7][:, c * FW + NCL:c * FW + NCL + NTILES], sq[:, c * P:(c + 1) * P], ident[0:NTILES, 0:NTILES])
                last = tr(banks[7][:, c * FW:c * FW + NCL], sq8[:, 0, c * P:(c + 1) * P], ident[0:NCL, 0:NCL])
            last.then_inc(s_pe, 1)
            pe.wait_ge(s_dve, SILU_READY)
            for c in range(KC):
                last = tr(banks[5][:, c * B:(c + 1) * B], c_sb[:, c * P:(c + 1) * P], ident[0:B, 0:B])
            last.then_inc(s_pe, 1)
            pe.wait_ge(s_act, WOT_READY)
            for m in range(KC):
                for v in range(KC):
                    last = mm(banks[2][:, m * D:(m + 1) * D], wv[:, v, m * P:(m + 1) * P], woT[:, v, :],
                              start=(v == 0), stop=(v == KC - 1))
            last.then_inc(s_pe, 1)
            for v in range(KC):
                mm(banks[4][0:2, 0:D], bv[:, v:v + 1].broadcast_to([P, 2]), woT[:, v, :],
                   start=(v == 0), stop=(v == KC - 1))
            for c in range(KC):
                last = mm(banks[4][0:2, D:D + 1], bq[:, c:c + 1].broadcast_to([P, 2]), bk[:, c:c + 1],
                          start=(c == 0), stop=(c == KC - 1))
            last.then_inc(s_pe, 1)
            pe.wait_ge(s_dve, CT_READY)
            for i, j in enumerate((0, 1, 3, 4)):
                for m in range(KC):
                    o = (i * KC + m) * B
                    for c in range(KC):
                        last = mm(banks[6][:, o:o + B], wmod_sb[:, c, j * D + m * P:j * D + (m + 1) * P], c_T[:, c, :],
                                  start=(c == 0), stop=(c == KC - 1))
            last.then_inc(s_pe, 1)
            for i, j in enumerate((2, 5)):
                for c in range(KC):
                    last = mm(banks[5][0:B, i * D:(i + 1) * D], c_T[:, c, :], wmod_sb[:, c, j * D:(j + 1) * D],
                              start=(c == 0), stop=(c == KC - 1))
            last.then_inc(s_pe, 1)
            pe.wait_ge(s_dve, DVE_SETUP)
            pe.wait_ge(s_act, ACT_SETUP)

            reader = {}

            def free(name, k, reads, count):
                bank = TURN[name] if name in TURN else 2 + MIX[name]
                if bank in reader:
                    before, at, when = reader[bank]
                    pe.wait_ge(before, at(when))
                reader[bank] = (reads, count, k)
                return banks[bank]

            def split3(ps, lhs_hi, lhs_lo, rhs_hi, rhs_lo, start=True, stop=True):
                ops = [(a(c), b(c)) for c in range(KC)
                       for a, b in ((lhs_hi, rhs_hi), (lhs_hi, rhs_lo), (lhs_lo, rhs_hi))]
                for i, (a, b) in enumerate(ops):
                    last = mm(ps, a, b, start=start and i == 0, stop=stop and i == len(ops) - 1)
                return last

            def x_turn(k, s):
                for c in range(KC):
                    ps = free(f"XT{SEQ[s]}{c}", k, h_ready, lambda kk, c=c: KC * seq(kk, s) + c + 1)
                    if c == 0:
                        pe.wait_ge(xhat_ready, NT * seq(k, s) + NT)
                    for t in range(NT):
                        last = tr(ps[:, t * P:(t + 1) * P], xhat[:, t, c * P:(c + 1) * P], ident[:, :])
                    last.then_inc(xt_done, 1)

            def project(k, s):
                pe.wait_ge(h_lo_rdy, KC * seq(k, s) + KC)
                for m in range(KC):
                    ps = free(f"G{SEQ[s]}{m}", k, g_lo_rdy, lambda kk, m=m: KC * seq(kk, s) + m + 1)
                    split3(ps[:, 0:S], lambda c: a_hi[:, c, m * P:(m + 1) * P], lambda c: a_lo[:, c, m * P:(m + 1) * P],
                           lambda c: h_hi[s][:, c, :], lambda c: h_lo[s][:, c, :]).then_inc(g_done, 1)
                for t in range(NT):
                    ps = free(f"V{SEQ[s]}{t}", k, v_ready, lambda kk, t=t: NT * seq(kk, s) + t + 1)
                    mm(ps[:, 0:VW], ones2[:, :], vbias[:, :], start=True, stop=False)
                    split3(ps[:, 0:VW], lambda c: h_hi[s][:, c, t * P:(t + 1) * P], lambda c: h_lo[s][:, c, t * P:(t + 1) * P],
                           lambda c: m_hi[:, c, :], lambda c: m_lo[:, c, :], start=False).then_inc(vproj_done, 1)

            def scores(k, s, t):
                b = seq(k, s)
                if t == 0:
                    pe.wait_ge(g_lo_rdy, KC * b + KC)
                need(pe, absc_ready, NT * b + t - 1)
                w = (t + 1) * P
                split3(score_ps[t % 2][:, 0:w], lambda c: g_hi[:, c, t * P:(t + 1) * P], lambda c: g_lo[:, c, t * P:(t + 1) * P],
                       lambda c: h_hi[s][:, c, 0:w], lambda c: h_lo[s][:, c, 0:w]).then_inc(scores_done, 1)

            def p_turn(k, s, t):
                b = seq(k, s)
                ps = free(f"PT{SEQ[s]}{t}", k, pt_rdy, lambda kk: NT * seq(kk, s) + t + 1)
                pe.wait_ge(probs_rdy, NT * b + t + 1)
                for j in range(t + 1):
                    last = tr(ps[:, j * P:(j + 1) * P], probs[t % 2][:, j * P:(j + 1) * P], ident[:, :])
                last.then_inc(pt_done, 1)

            def attend(k, s, t):
                b = seq(k, s)
                need(pe, gated_rdy, NT * b + t)
                pe.wait_ge(pt_rdy, NT * b + t + 1)
                for j in range(t + 1):
                    last = mm(attn_ps[:, 0:D], probsT[t % 2][:, j * P:(j + 1) * P], v_sb[s][:, j, 0:D],
                              start=(j == 0), stop=(j == t))
                last.then_inc(pv_done, 1)

            def h2_turn(c, k, u):
                s, m = u // KC, u % KC
                ps = free(f"H2T{u}", k, h2_rdy, lambda kk: 2 * KC * (kk - 1) + u + 1)
                pe.wait_ge(xhat2_rdy, PT * c + NT * (s + 1))
                for t in range(NT):
                    last = tr(ps[:, t * P:(t + 1) * P], xhat2[:, NT * s + t, m * P:(m + 1) * P], ident[:, :])
                last.then_inc(h2t_done, 1)

            def ffn_scores(c, k, u):
                ps = free(f"FS{u}", k, fs_rdy, lambda kk: 3 * (kk - 1) + u + 1)
                tiles = range(3 * u, min(3 * u + 3, PT))
                pe.wait_ge(h2_lo_rdy, 2 * KC * c + KC * (tiles[-1] // NT + 1))
                for i, t in enumerate(tiles):
                    s, q = t // NT, (t % NT) * P
                    last = split3(ps[:, i * FW:(i + 1) * FW], lambda m: h2_hi[:, s, m, q:q + P], lambda m: h2_lo[:, s, m, q:q + P],
                                  lambda m: f_hi[:, m, :], lambda m: f_lo[:, m, :])
                last.then_inc(fs_done, 1)

            def turn_back(c, k, u):
                ps = free(f"BT{u}", k, h2_tok_rdy, lambda kk: NT * (kk - 1) + u + 1)
                pe.wait_ge(h2_rdy, 2 * KC * c + KC * (u // 2 + 1))
                for i in range(2):
                    t = 2 * u + i
                    for m in range(KC):
                        q = (t % NT) * P
                        last = tr(ps[:, i * D + m * P:i * D + (m + 1) * P], h2_full[:, t // NT, m, q:q + P], ident[:, :])
                last.then_inc(bt_done, 1)

            def onehot_turn(c, k, u):
                ps = free(f"OHT{u}", k, oht_rdy, lambda kk: 2 * (kk - 1) + u + 1)[:, :].bitcast(BF16)
                pe.wait_ge(onehot_rdy, c + 1)
                for i in range(NT):
                    last = tr(ps[:, i * P:(i + 1) * P], onehot[:, NT * u + i, :], identb[:, :])
                last.then_inc(oht_done, 1)

            def gather(c, k, t):
                ps = free(f"GA{t}", k, gath_rdy, lambda kk: PT * (kk - 1) + t + 1)
                pe.wait_ge(oht_rdy, 2 * c + t // NT + 1)
                mm(ps[:, 0:GW], onehotT[:, t * P:(t + 1) * P], table[:, :], start=True, stop=True).then_inc(ga_done, 1)

            def superstep(k, c, b, nxt):
                C = c is not None
                if b:
                    project(k, 0)
                    scores(k, 0, 0)
                    scores(k, 0, 1)
                if C:
                    h2_turn(c, k, 0)
                    h2_turn(c, k, 1)
                if b:
                    scores(k, 0, 2)
                    p_turn(k, 0, 0)
                    x_turn(k, 1)
                    attend(k, 0, 0)
                    p_turn(k, 0, 1)
                    scores(k, 0, 3)
                if C:
                    h2_turn(c, k, 2)
                    h2_turn(c, k, 3)
                if b:
                    attend(k, 0, 1)
                    p_turn(k, 0, 2)
                    attend(k, 0, 2)
                if C:
                    for u in range(3):
                        ffn_scores(c, k, u)
                if b:
                    p_turn(k, 0, 3)
                if C:
                    for u in range(NT):
                        turn_back(c, k, u)
                if b:
                    attend(k, 0, 3)
                    project(k, 1)
                    scores(k, 1, 0)
                    scores(k, 1, 1)
                    p_turn(k, 1, 0)
                    scores(k, 1, 2)
                    attend(k, 1, 0)
                    p_turn(k, 1, 1)
                    scores(k, 1, 3)
                if b and nxt:
                    x_turn(k + 1, 0)
                if b:
                    attend(k, 1, 1)
                if C:
                    onehot_turn(c, k, 0)
                if b:
                    p_turn(k, 1, 2)
                    attend(k, 1, 2)
                if C:
                    onehot_turn(c, k, 1)
                if b:
                    p_turn(k, 1, 3)
                if C:
                    for t in range(PT):
                        gather(c, k, t)
                if b:
                    attend(k, 1, 3)

            x_turn(0, 0)
            superstep(0, None, True, True)
            superstep(1, 0, True, True)
            with pe.Fori(2, PAIRS - 1) as k:
                for bank, (r, at, when) in list(reader.items()):
                    reader[bank] = (r, at, k if when == 2 else k - 1)
                superstep(k, k - 1, True, True)
            for bank, (r, at, when) in list(reader.items()):
                reader[bank] = (r, at, PAIRS - 2)
            superstep(PAIRS - 1, PAIRS - 2, True, False)
            superstep(PAIRS, PAIRS - 1, False, False)

        @block.scalar
        def _(act):
            A = nc.scalar.activation
            n = [0]

            def load(dst, src):
                act.dma_start(dst, src).then_inc(w_in, 16)
                n[0] += 1

            G = GRID
            for h in range(2):
                r = slice(h * NTILES, (h + 1) * NTILES)
                load(t_full[r, 0:2 * G], ins["L0_ffn_spline_w1"].rearrange("n i g -> n (i g)"))
                load(t_full[r, 2 * G:3 * G], ins["L0_ffn_spline_b1"])
                load(t_full[r, 3 * G:4 * G], ins["L0_ffn_spline_w2"].rearrange("n g o -> n (g o)"))
                load(t_full[r, 4 * G:4 * G + 1], ins["L0_ffn_spline_b2"])
                load(t_full[r, PAR:GW], ins["L0_ffn_directions"])
            assert n[0] == LOADS_ACT
            nc.scalar.preload_act_table_set("natural_log_exp_and_others")
            act.wait_ge(w_in, 16 * (LOADS_SP + LOADS_ACT))
            A(c_exp[:, :], c_sb[:, :], ACT.Exp, scale=-1.0).then_inc(s_act, 1)
            act.wait_ge(s_pe, 2)
            A(woT[:, :, :].rearrange("p c d -> p (c d)"), banks[1][:, :], ACT.Copy).then_inc(s_act, 1)

            def ln_guess(out_, var, ready, chain, i, signal):
                act.wait_ge(ready, i + 1)
                chain.link(act, A(out_, var, ACT.Ln))
                A(out_, out_, ACT.Exp, scale=-0.5).then_inc(signal, 1)

            def a_norm(k, s):
                b = seq(k, s)
                act_guess1.start(b)
                ln_guess(guess1[:, :], var1[:, :], ln1_var, act_guess1, b, ln1_guess)

            def a_xhat(k, s):
                b = seq(k, s)
                act.wait_ge(ln1_ready, b + 1)
                for t in range(NT):
                    A(xhat[:, t, :], x_sb[s][:, t, :], ACT.Identity, bias=nmr1[:, t:t + 1],
                      scale=rstd1[:, t:t + 1]).then_inc(xhat_ready, 1)

            def a_evict(k, s):
                b = seq(k, s)
                for c in range(KC):
                    act.wait_ge(xt_done, KC * b + c + 1)
                    need(act, h_lo_rdy, KC * (b - 1) + c + 1)
                    A(h_full[:, c, :], turn_ps[TURN[f"XT{SEQ[s]}{c}"]][:, :], ACT.Identity,
                      bias=sa_col[:, c, bass.ds(b, 1)], scale=ca_col[:, c, bass.ds(b, 1)]).then_inc(h_ready, 1)

            def b_evict(k, s):
                b = seq(k, s)
                for c in range(KC):
                    act.wait_ge(g_done, KC * b + c + 1)
                    need(act, scores_done, NT * b)
                    A(g_hi[:, c, :], mix_ps[MIX[f"G{SEQ[s]}{c}"]][:, :], ACT.Identity,
                      bias=g_bias[:, c:c + 1]).then_inc(g_hi_rdy, 1)
                for t in range(NT):
                    act.wait_ge(vproj_done, NT * b + t + 1)
                    need(act, pv_done, NT * (b - 1))
                    A(v_sb[s][:, t, :], mix_ps[MIX[f"V{SEQ[s]}{t}"]][:, 0:VW], ACT.Identity).then_inc(v_ready, 1)

            def b_abs(k, s, t):
                b, w = seq(k, s), (t + 1) * P
                act.wait_ge(scores_done, NT * b + t + 1)
                act.wait_ge(v_ready, NT * b + t + 1)
                A(absc[t % 2][:, 0:w], score_ps[t % 2][:, 0:w], ACT.Abs, bias=v_sb[s][:, t, D:D + 1],
                  scale=SCALE).then_inc(absc_ready, 1)

            def b_exp(k, s, t):
                b, w = seq(k, s), (t + 1) * P
                act.wait_ge(rowmax, NT * b + t + 1)
                A(probs[t % 2][:, 0:w], absc[t % 2][:, 0:w], ACT.Exp, bias=negmax[:, t:t + 1],
                  accum_out=rowsum[s][:, t:t + 1]).then_inc(probs_rdy, 1)

            def b_pt(k, s, t):
                b, w = seq(k, s), (t + 1) * P
                act.wait_ge(pt_done, NT * b + t + 1)
                need(act, pv_done, NT * b + t - 1)
                A(probsT[t % 2][:, 0:w], turn_ps[TURN[f"PT{SEQ[s]}{t}"]][:, 0:w], ACT.Identity).then_inc(pt_rdy, 1)

            def c_guess2(c):
                act_guess2.start(c)
                ln_guess(guess2[:, :], var2[:, :], ln2_var, act_guess2, c, ln2_guess)

            def c_xhat2(c, s):
                act.wait_ge(ln2_ready, c + 1)
                for t in range(NT * s, NT * (s + 1)):
                    A(xhat2[:, t, :], x2[s][:, t % NT, :], ACT.Identity, bias=nmr2[:, t:t + 1],
                      scale=rstd2[:, t:t + 1]).then_inc(xhat2_rdy, 1)

            def c_h2(c, u):
                s, m = u // KC, u % KC
                b = seq(c, s)
                act.wait_ge(h2t_done, 2 * KC * c + u + 1)
                need(act, h2_lo_rdy, 2 * KC * (c - 1) + u + 1)
                A(h2_full[:, s, m, :], turn_ps[TURN[f"H2T{u}"]][:, :], ACT.Identity,
                  bias=sb_col[:, m, bass.ds(b, 1)], scale=cb_col[:, m, bass.ds(b, 1)]).then_inc(h2_rdy, 1)

            def c_fs(c, u):
                n_ = min(3, PT - 3 * u)
                act.wait_ge(fs_done, 3 * c + u + 1)
                need(act, onehot_rdy, c)
                A(fs[:, 3 * u:3 * u + n_, :].rearrange("p t f -> p (t f)"), mix_ps[MIX[f"FS{u}"]][:, 0:n_ * FW],
                  ACT.Identity).then_inc(fs_rdy, 1)

            def c_back(c, u):
                act.wait_ge(bt_done, NT * c + u + 1)
                need(act, ln3_var, c)
                A(h2_tok[:, 2 * u:2 * u + 2, :].rearrange("p t d -> p (t d)"), mix_ps[MIX[f"BT{u}"]][:, :],
                  ACT.Identity).then_inc(h2_tok_rdy, 1)

            def c_exp_cl(c):
                act.wait_ge(zc_rdy, c + 1)
                A(z_cl[:, :], z_cl[:, :], ACT.Exp, scale=-1.0).then_inc(ec_rdy, 1)

            def c_exp_lo(c):
                act.wait_ge(zl_rdy, c + 1)
                A(z_lo[:, :], z_lo[:, :], ACT.Exp, scale=-1.0).then_inc(el_rdy, 1)

            def c_gelu(c):
                act.wait_ge(pregelu, c + 1)
                A(hid[:, :, :], hid[:, :, :], ACT.Gelu).then_inc(gelu_rdy, 1)

            def c_tanh(c):
                act.wait_ge(pretanh, c + 1)
                A(comp[:, :, :], cmp_t[:, :, :], ACT.Tanh).then_inc(tanh_rdy, 1)
                nc.scalar.preload_act_table_set("natural_log_exp_and_others")

            def c_onehot(c, u):
                act.wait_ge(oht_done, 2 * c + u + 1)
                need(act, ga_done, PT * (c - 1) + NT * (u + 1))
                A(onehotT[:, u * S:(u + 1) * S], turn_ps[TURN[f"OHT{u}"]][:, :].bitcast(BF16)[:, 0:S],
                  ACT.Identity).then_inc(oht_rdy, 1)

            def c_gath(c, t):
                act.wait_ge(ga_done, PT * c + t + 1)
                need(act, ln3_var, c)
                A(gath[:, t, :], mix_ps[MIX[f"GA{t}"]][:, 0:GW], ACT.Identity).then_inc(gath_rdy, 1)

            def c_guess3(c):
                ln_guess(guess3[:, :], var3[:, :], ln3_var, act_guess2, c, ln3_guess)

            def c_yhat(c):
                act.wait_ge(ln3_ready, c + 1)
                for t in range(PT):
                    A(y[:, t, :], y[:, t, :], ACT.Identity, bias=nmr3[:, t:t + 1],
                      scale=rstd3[:, t:t + 1]).then_inc(yhat_rdy, 1)

            act.wait_ge(s_dve, DVE_SETUP)

            def superstep(k, c, b, nxt):
                C = c is not None
                if b:
                    b_evict(k, 0)
                if C:
                    c_guess2(c)
                if b:
                    b_abs(k, 0, 0)
                if C:
                    c_xhat2(c, 0)
                if b:
                    b_abs(k, 0, 1)
                    b_exp(k, 0, 0)
                    a_norm(k, 1)
                if C:
                    c_h2(c, 0)
                    c_h2(c, 1)
                if b:
                    b_exp(k, 0, 1)
                    b_abs(k, 0, 2)
                    a_xhat(k, 1)
                    b_pt(k, 0, 0)
                if C:
                    c_xhat2(c, 1)
                if b:
                    a_evict(k, 1)
                    b_exp(k, 0, 2)
                    b_pt(k, 0, 1)
                    b_abs(k, 0, 3)
                if C:
                    c_h2(c, 2)
                    c_h2(c, 3)
                if b:
                    b_exp(k, 0, 3)
                    b_pt(k, 0, 2)
                if C:
                    for u in range(3):
                        c_fs(c, u)
                if b:
                    b_pt(k, 0, 3)
                if C:
                    c_exp_cl(c)
                    for u in range(NT):
                        c_back(c, u)
                if b:
                    b_evict(k, 1)
                    b_abs(k, 1, 0)
                    b_abs(k, 1, 1)
                    b_exp(k, 1, 0)
                    b_exp(k, 1, 1)
                    b_pt(k, 1, 0)
                    b_abs(k, 1, 2)
                    if nxt:
                        a_norm(k + 1, 0)
                if C:
                    c_exp_lo(c)
                if b:
                    b_exp(k, 1, 2)
                    b_pt(k, 1, 1)
                    b_abs(k, 1, 3)
                    b_exp(k, 1, 3)
                if b and nxt:
                    a_xhat(k + 1, 0)
                    a_evict(k + 1, 0)
                if C:
                    c_gelu(c)
                    c_tanh(c)
                    c_onehot(c, 0)
                if b:
                    b_pt(k, 1, 2)
                if C:
                    c_onehot(c, 1)
                if b:
                    b_pt(k, 1, 3)
                if C:
                    for t in range(PT):
                        c_gath(c, t)
                    c_guess3(c)
                    c_yhat(c)

            a_norm(0, 0)
            a_xhat(0, 0)
            a_evict(0, 0)
            superstep(0, None, True, True)
            superstep(1, 0, True, True)
            with act.Fori(2, PAIRS - 1) as k:
                superstep(k, k - 1, True, True)
            superstep(PAIRS - 1, PAIRS - 2, True, False)
            superstep(PAIRS, PAIRS - 1, False, False)

        @block.gpsimd
        def _(pool):
            gp = nc.gpsimd
            n = [0]

            def link(ins_):
                n[0] += 1
                ins_.then_inc(s_pool, 1)
                pool.wait_ge(s_pool, n[0])

            link(gp.memset(ident[:, :], 0.0))
            gp.affine_select(out=ident[:, :], in_=ident[:, :], compare_op=ALU.not_equal, fill=1.0, base=0,
                             pattern=[[-1, P]], channel_multiplier=1).then_inc(id_ready, 1)
            link(gp.memset(causal[:, :], 0.0))
            gp.affine_select(out=causal[:, :], in_=causal[:, :], compare_op=ALU.is_ge, fill=MASKED, base=0,
                             pattern=[[-1, P]], channel_multiplier=1)
            for j in range(K):
                gp.memset(steps[:, j:j + 1], float(j))
            for j in range(TPC):
                gp.memset(falling[:, j:j + 1], float(TPC - j))
            link(gp.memset(t_full[:, PAR - 1:PAR], 0.0))
            link(gp.memset(vb2[:, :], 0.0))
            assert n[0] == POOL_SETUP

            def split_h(k, s):
                b = seq(k, s)
                for c in range(KC):
                    pool.wait_ge(h_hi_rdy, KC * b + c + 1)
                    gp.tensor_tensor(h_lo[s][:, c, :], h_full[:, c, :], h_hi[s][:, c, :].bitcast(F32),
                                     ALU.subtract).then_inc(h_lo_rdy, 1)

            def mask(k, s, t):
                pool.wait_ge(absc_ready, NT * seq(k, s) + t + 1)
                d = absc[t % 2][:, t * P:(t + 1) * P]
                gp.tensor_tensor(d, d, causal[:, :], ALU.add).then_inc(masked, 1)

            def residual(k, s, t):
                b = seq(k, s)
                pool.wait_ge(gated_rdy, NT * b + t + 1)
                if s == 0 and t == 0:
                    need(pool, xhat2_rdy, PT * k)
                gp.tensor_tensor(x2[s][:, t, :], gated[t % 2][:, :], x_sb[s][:, t, :], ALU.add).then_inc(x2_rdy, 1)

            def split_h2(c, u):
                s, m = u // KC, u % KC
                pool.wait_ge(h2_hi_rdy, 2 * KC * c + u + 1)
                gp.tensor_tensor(h2_lo[:, s, m, :], h2_full[:, s, m, :], h2_hi[:, s, m, :].bitcast(F32),
                                 ALU.subtract).then_inc(h2_lo_rdy, 1)

            def base(c, s):
                if s == 0:
                    pool_c.start(c)
                pool.wait_ge(gb_ld[s], 16 * (c + 1))
                pool.wait_ge(x2_rdy, NT * seq(c, s) + NT)
                need(pool, sent[s], 16 * c)
                pool_c.mark(gp.tensor_tensor(res[:, NT * s:NT * (s + 1), :], x2[s][:, :, :],
                                             gb_row[s][:, 1:2, :].broadcast_to([P, NT, D]), ALU.add))

            def finish(c, s):
                pool.wait_ge(yhat_rdy, PT * c + NT * (s + 1))
                ys = y[:, NT * s:NT * (s + 1), :]
                pool_c.link(pool, gp.tensor_tensor(ys, ys, gb_row[s][:, 0:1, :].broadcast_to([P, NT, D]), ALU.mult))
                rs = res[:, NT * s:NT * (s + 1), :]
                gp.tensor_tensor(rs, rs, ys, ALU.add).then_inc(res_rdy, 1)

            def superstep(k, c, b, nxt):
                C = c is not None
                if C:
                    base(c, 0)
                if b:
                    mask(k, 0, 0)
                    mask(k, 0, 1)
                if C:
                    split_h2(c, 0)
                    split_h2(c, 1)
                if b:
                    mask(k, 0, 2)
                    split_h(k, 1)
                    mask(k, 0, 3)
                if C:
                    split_h2(c, 2)
                    split_h2(c, 3)
                    base(c, 1)
                if b:
                    for t in range(NT):
                        residual(k, 0, t)
                    mask(k, 1, 0)
                    mask(k, 1, 1)
                    mask(k, 1, 2)
                    mask(k, 1, 3)
                    residual(k, 1, 0)
                if b and nxt:
                    split_h(k + 1, 0)
                if b:
                    for t in range(1, NT):
                        residual(k, 1, t)
                if C:
                    finish(c, 0)
                    finish(c, 1)

            split_h(0, 0)
            superstep(0, None, True, True)
            superstep(1, 0, True, True)
            with pool.Fori(2, PAIRS - 1) as k:
                superstep(k, k - 1, True, True)
            superstep(PAIRS - 1, PAIRS - 2, True, False)
            superstep(PAIRS, PAIRS - 1, False, False)

        @block.vector
        def _(dve):
            v = nc.vector
            tt, ts, stt, red = v.tensor_tensor, v.tensor_scalar, v.scalar_tensor_tensor, v.tensor_reduce
            n = [0]

            def mark(ins_):
                n[0] += 1
                ins_.then_inc(s_dve, 1)

            def link(ins_):
                mark(ins_)
                dve.wait_ge(s_dve, n[0])

            dve.wait_ge(id_ready, 1)
            dve.wait_ge(s_pool, POOL_SETUP)
            link(v.tensor_copy(identb[:, :], ident[:, :]))
            dve.wait_ge(w_in, 16 * (LOADS_SP + LOADS_ACT))
            for raw_, q_, tmp in ((sraw[:, :], sq[:, :], stmp[:, :]),
                                  (sraw8[:, :, :], sq8[:, :, :], stmp8[:, :, :])):
                link(ts(q_, raw_, 0.3, None, ALU.is_gt))
                link(ts(tmp, raw_, -0.3, None, ALU.is_lt))
                link(tt(q_, q_, tmp, ALU.subtract))
                link(tt(q_, q_, raw_, ALU.subtract))
                link(tt(q_, raw_, q_, ALU.add))
            for j in range(1, TPC):
                link(tt(sq8[:, 0, :], sq8[:, 0, :], sq8[:, j, :], ALU.add))
            link(ts(sq8[:, 1, :], sq8[:, 0, :], 0.0, None, ALU.is_gt))
            link(ts(sq8[:, 2, :], sq8[:, 0, :], 0.0, None, ALU.is_lt))
            link(tt(sq8[:, 0, :], sq8[:, 1, :], sq8[:, 2, :], ALU.subtract))
            assert n[0] == SIG_READY, n
            dve.wait_ge(s_act, 1)
            link(ts(c_exp[:, :], c_exp[:, :], 1.0, None, ALU.add))
            link(v.reciprocal(c_exp[:, :], c_exp[:, :]))
            link(tt(c_sb[:, :], c_sb[:, :], c_exp[:, :], ALU.mult))
            assert n[0] == SILU_READY, n
            dve.wait_ge(s_pe, 5)
            link(v.tensor_copy(c_T[:, :, :].rearrange("p c b -> p (c b)"), banks[5][:, 0:KC * B]))
            assert n[0] == CT_READY, n
            dve.wait_ge(s_pe, 9)
            g = mod[:, 0:2, :].rearrange("b a d -> b (a d)")
            r = rows[:, 0:2, :].rearrange("b a d -> b (a d)")
            link(v.tensor_copy(g, banks[5][0:B, :]))
            link(stt(out=r, in0=g, scalar=-1.0, in1=g, op0=ALU.mult, op1=ALU.max))
            link(ts(g, g, 0.0, None, ALU.is_ge))
            link(ts(g, g, 2.0, -1.0, ALU.mult, ALU.add))
            link(stt(out=r, in0=r, scalar=GATE_MIN, in1=g, op0=ALU.max, op1=ALU.mult))
            link(tt(rows[:, 2, :], rows[:, 1, :], beta_r[:, :], ALU.mult))
            link(tt(rows[:, 1, :], rows[:, 1, :], gamma_r[:, :], ALU.mult))
            assert n[0] == ROWS_READY, n
            flat = lambda a: a[:, :, :].rearrange("p c d -> p (c d)")
            dve.wait_ge(s_pe, 9)
            link(v.tensor_copy(flat(a_hi), banks[0][:, :]))
            mark(tt(flat(a_lo), banks[0][:, :], flat(a_hi).bitcast(F32), ALU.subtract))
            bank2 = banks[2][:, :].rearrange("p (c d) -> p c d", c=KC)
            mark(v.tensor_copy(m_hi[:, :, 0:D], bank2))
            link(v.tensor_copy(m_hi[:, :, D:VW], steps[:, 0:1].unsqueeze(1).broadcast_to([P, KC, 2])))
            mark(tt(m_lo[:, :, 0:D], bank2, m_hi[:, :, 0:D].bitcast(F32), ALU.subtract))
            mark(v.tensor_copy(m_lo[:, :, D:VW], steps[:, 0:1].unsqueeze(1).broadcast_to([P, KC, 2])))
            tcol = comp[:, 0:KC, 0]
            link(ts(tcol, banks[3][:, 0:KC], SCALE, None, ALU.mult))
            link(v.tensor_copy(m_hi[:, :, D], tcol))
            link(tt(m_lo[:, :, D], tcol, m_hi[:, :, D].bitcast(F32), ALU.subtract))
            mark(v.tensor_copy(g_bias[:, :], banks[3][:, KC:2 * KC]))
            mark(tt(vb2[:, 0:D], banks[4][0:2, 0:D], bo2[:, :], ALU.add))
            link(ts(vb2[:, D:D + 1], banks[4][0:2, D:D + 1], SCALE, None, ALU.mult))
            link(v.tensor_copy(vb2_hi[:, :], vb2[:, :]))
            link(tt(vb2_lo[:, :], vb2[:, :], vb2_hi[:, :].bitcast(F32), ALU.subtract))
            link(ts(vb2_lo[:, :], vb2_lo[:, :], ident[0:2, 1:2], None, ALU.mult))
            link(stt(out=vbias[:, :], in0=vb2_hi[:, :].bitcast(F32), scalar=ident[0:2, 0:1], in1=vb2_lo[:, :],
                     op0=ALU.mult, op1=ALU.add))
            mark(ts(ones2[:, :], ident[0:2, :], 0.0, 1.0, ALU.mult, ALU.add))
            for i, (dst, add) in enumerate(((sa_col, 0.0), (ca_col, 1.0), (sb_col, 0.0), (cb_col, 1.0))):
                mark(ts(flat(dst), banks[6][:, i * KC * B:(i + 1) * KC * B], add, None, ALU.add))
            link(v.tensor_copy(f_full[:, :, 0:NCL + NTILES],
                               banks[7][:, 0:KC * FW].rearrange("p (c f) -> p c f", c=KC)[:, :, 0:NCL + NTILES]))
            link(v.tensor_copy(flat(f_hi), flat(f_full)))
            mark(tt(flat(f_lo), flat(f_full), flat(f_hi).bitcast(F32), ALU.subtract))
            lo = slice(NTILES, P)
            link(v.tensor_copy(table[:, :], t_full[:, :]))
            link(tt(t_full[lo, :], t_full[lo, :], table[lo, :].bitcast(F32), ALU.subtract))
            link(v.tensor_copy(table[lo, :], t_full[lo, :]))
            mark(tt(knot_step[:, :], knots[:, 1:K], knots[:, 0:K - 1], ALU.subtract))
            link(ts(inv_temp[:, :], inv_temp[:, :], TEMP_EPS, None, ALU.add))
            link(v.reciprocal(inv_temp[:, :], inv_temp[:, :]))
            assert n[0] == DVE_SETUP, n

            def variance(chain, st, sums, dif, var, signal):
                chain.mark(tt(sums, st[:, :, 1], st[:, :, 4], ALU.add))
                chain.mark(tt(var, st[:, :, 2], st[:, :, 5], ALU.add))
                chain.link(dve, tt(dif, st[:, :, 1], st[:, :, 4], ALU.subtract))
                chain.mark(tt(dif, dif, dif, ALU.mult))
                chain.link(dve, ts(var, var, 1.0 / D, EPS, ALU.mult, ALU.add))
                stt(out=var, in0=dif, scalar=0.25, in1=var, op0=ALU.mult, op1=ALU.add).then_inc(signal, 1)

            def newton(chain, var, guess, tmp, rstd, nmr, sums, signal):
                chain.link(dve, tt(tmp, guess, guess, ALU.mult))
                chain.link(dve, stt(out=tmp, in0=tmp, scalar=-0.5, in1=var, op0=ALU.mult, op1=ALU.mult))
                chain.link(dve, stt(out=rstd, in0=tmp, scalar=1.5, in1=guess, op0=ALU.add, op1=ALU.mult))
                stt(out=nmr, in0=sums, scalar=-0.5, in1=rstd, op0=ALU.mult, op1=ALU.mult).then_inc(signal, 1)

            def a_stats(k, s):
                dve.wait_ge(x_ld[s], 16 * (k + 1))
                dve_a.start(seq(k, s))
                for t in range(NT):
                    dve_a.mark(v.bn_stats(st1[:, t, :], x_sb[s][:, t, :]))
                dve_a.wait(dve)
                variance(dve_a, st1, sum1[:, :], dif1[:, :], var1[:, :], ln1_var)

            def a_norm(k, s):
                dve.wait_ge(ln1_guess, seq(k, s) + 1)
                newton(dve_a, var1[:, :], guess1[:, :], newt1[:, :], rstd1[:, :], nmr1[:, :], sum1[:, :], ln1_ready)

            def a_split(k, s):
                b = seq(k, s)
                need(dve, scores_done, NT * (b - 1))
                for c in range(KC):
                    dve.wait_ge(h_ready, KC * b + c + 1)
                    v.tensor_copy(h_hi[s][:, c, :], h_full[:, c, :]).then_inc(h_hi_rdy, 1)

            def b_split(k, s):
                b = seq(k, s)
                for c in range(KC):
                    dve.wait_ge(g_hi_rdy, KC * b + c + 1)
                    stt(out=g_lo[:, c, :], in0=mix_ps[MIX[f"G{SEQ[s]}{c}"]][:, :], scalar=g_bias[:, c:c + 1],
                        in1=g_hi[:, c, :].bitcast(F32), op0=ALU.add, op1=ALU.subtract).then_inc(g_lo_rdy, 1)

            def b_max(k, s, t):
                dve.wait_ge(masked, NT * seq(k, s) + t + 1)
                red(negmax[:, t:t + 1], absc[t % 2][:, 0:(t + 1) * P], X, ALU.max, negate=True).then_inc(rowmax, 1)

            def b_gate(k, s, t):
                b = seq(k, s)
                if t == 0:
                    dve_b.start(b)
                    dve.wait_ge(ga_ld[s], 16 * (k + 1))
                dve.wait_ge(pv_done, NT * b + t + 1)
                dve_b.link(dve, v.reciprocal(rinv[:, t:t + 1], rowsum[s][:, t:t + 1]))
                need(dve, x2_rdy, NT * b + t - 1)
                stt(out=gated[t % 2][:, :], in0=attn_ps[:, 0:D], scalar=rinv[:, t:t + 1], in1=ga_row[s][:, :],
                    op0=ALU.mult, op1=ALU.mult).then_inc(gated_rdy, 1)

            def b_stats(k, s):
                b = seq(k, s)
                for t in range(NT):
                    dve.wait_ge(x2_rdy, NT * b + t + 1)
                    v.bn_stats(st2[:, NT * s + t, :], x2[s][:, t, :]).then_inc(st2_rdy, 1)

            def c_var(c):
                dve_c.start(c)
                dve.wait_ge(st2_rdy, PT * (c + 1))
                variance(dve_c, st2, sum2[:, :], dif2[:, :], var2[:, :], ln2_var)

            def c_norm(c):
                dve.wait_ge(ln2_guess, c + 1)
                newton(dve_c, var2[:, :], guess2[:, :], newt2[:, :], rstd2[:, :], nmr2[:, :], sum2[:, :], ln2_ready)

            def c_split(c, u):
                s, m = u // KC, u % KC
                dve.wait_ge(h2_rdy, 2 * KC * c + u + 1)
                v.tensor_copy(h2_hi[:, s, m, :], h2_full[:, s, m, :]).then_inc(h2_hi_rdy, 1)

            def link_c(ins_):
                dve_c.link(dve, ins_)

            def c_hidden(c):
                dve.wait_ge(fs_rdy, 3 * (c + 1))
                ts_z(z_cl[:, :].rearrange("p (t j) -> p t j", t=PT), fs[:, :, 0:NCL]).then_inc(zc_rdy, 1)
                tt(hid[:, :, :], fs[:, :, NCL + NTILES:FW], b1_row[:, :].unsqueeze(1).broadcast_to([P, PT, H]),
                   ALU.add).then_inc(pregelu, 1)

            def ts_z(dst, src):
                return ts(dst, src, inv_temp[:, 0:1], Z_MIN, ALU.mult, ALU.max)

            def calibrate(e):
                ix, fl, vl, vd, gate = (a[:, :] for a in cal)
                K1 = K - 1
                row7 = lambda a: a.unsqueeze(1).broadcast_to([P, E8, K1])
                col7 = lambda a: a.unsqueeze(2).broadcast_to([P, E8, K1])
                link_c(ts(e, e, 1.0, None, ALU.add))
                link_c(v.reciprocal(ix, e))
                link_c(ts(ix, ix, float(K1), None, ALU.mult))
                m6 = cal7[0][:, :, 0:K1 - 1]
                link_c(tt(m6, ix.unsqueeze(2).broadcast_to([P, E8, K1 - 1]),
                          steps[:, 1:K1].unsqueeze(1).broadcast_to([P, E8, K1 - 1]), ALU.is_ge))
                link_c(red(fl, m6, X, ALU.add))
                link_c(tt(cal7[0][:, :, :], col7(fl), row7(steps[:, 0:K1]), ALU.is_equal))
                link_c(tt(cal7[1][:, :, :], cal7[0][:, :, :], row7(knots[:, 0:K1]), ALU.mult))
                link_c(red(vl, cal7[1][:, :, :], X, ALU.add))
                link_c(tt(cal7[1][:, :, :], cal7[0][:, :, :], row7(knot_step[:, :]), ALU.mult))
                link_c(red(vd, cal7[1][:, :, :], X, ALU.add))
                link_c(tt(ix, ix, fl, ALU.subtract))
                link_c(tt(ix, ix, vd, ALU.mult))
                link_c(tt(gate, vl, ix, ALU.add))

            def first_best(onehot_):
                gate = cal[4][:, :].rearrange("p (t j) -> p t j", t=PT)
                rank = cal[0][:, :].rearrange("p (t j) -> p t j", t=PT)
                spread = best[:, :].unsqueeze(2).broadcast_to([P, PT, TPC])
                link_c(red(best[:, :], gate, X, ALU.max))
                link_c(tt(rank, gate, spread, ALU.is_equal))
                link_c(tt(rank, rank, falling[:, :].unsqueeze(1).broadcast_to([P, PT, TPC]), ALU.mult))
                link_c(red(best[:, :], rank, X, ALU.max))
                link_c(tt(onehot_, rank, spread, ALU.is_equal))

            def c_cluster(c):
                dve.wait_ge(ec_rdy, c + 1)
                calibrate(z_cl[:, :])
                first_best(oh_cl[:, :, :])
                pick = picked[:, :, :].rearrange("p t (c j) -> p t c j", c=NCL)
                for q in range(2):
                    tiles = slice(NT * q, NT * (q + 1))
                    link_c(tt(pick[:, tiles], fs[:, tiles, NCL:NCL + NTILES].rearrange("p t (c j) -> p t c j", c=NCL),
                              oh_cl[:, tiles, :].unsqueeze(3).broadcast_to([P, NT, NCL, TPC]), ALU.mult))
                zl = z_lo[:, :].rearrange("p (t j) -> p t j", t=PT)
                link_c(red(zl, pick.rearrange("p t c j -> p t j c"), X, ALU.add))
                ts_z(zl, zl).then_inc(zl_rdy, 1)

            def c_local(c):
                dve.wait_ge(el_rdy, c + 1)
                calibrate(z_lo[:, :])
                first_best(oh_lo[:, :, :])
                for q in range(PT):
                    dve_c.mark(tt(onehot[:, q, 0:NTILES].rearrange("p (c j) -> p c j", c=NCL),
                                  oh_cl[:, q, :].unsqueeze(2).broadcast_to([P, NCL, TPC]),
                                  oh_lo[:, q, :].unsqueeze(1).broadcast_to([P, NCL, TPC]), ALU.mult))
                dve_c.wait(dve)
                v.tensor_copy(onehot[:, :, NTILES:P], onehot[:, :, 0:NTILES]).then_inc(onehot_rdy, 1)

            def c_comp(c):
                dve.wait_ge(gelu_rdy, c + 1)
                for o in range(NCOMP):
                    dve_c.mark(tt(w2prod[:, :, o, :], hid[:, :, :],
                                  w2_rows[:, :, o].unsqueeze(1).broadcast_to([P, PT, H]), ALU.mult))
                dve_c.wait(dve)
                link_c(red(cmp_t[:, :, :], w2prod[:, :, :, :], X, ALU.add))
                tt(cmp_t[:, :, :], cmp_t[:, :, :], b2_row[:, :].unsqueeze(1).broadcast_to([P, PT, NCOMP]),
                   ALU.add).then_inc(pretanh, 1)

            def c_spline(c):
                G = GRID
                dve.wait_ge(tanh_rdy, c + 1)
                dve.wait_ge(gath_rdy, PT * (c + 1))
                cb = lambda i: comp[:, :, i:i + 1].broadcast_to([P, PT, G])
                dve_c.mark(tt(sp0[:, :, :], gath[:, :, 0:G], cb(0), ALU.mult))
                link_c(tt(sp1[:, :, :], gath[:, :, G:2 * G], cb(1), ALU.mult))
                link_c(tt(sp0[:, :, :], sp0[:, :, :], sp1[:, :, :], ALU.add))
                link_c(tt(sp0[:, :, :], sp0[:, :, :], gath[:, :, 2 * G:3 * G], ALU.add))
                link_c(stt(out=sp0[:, :, :], in0=sp0[:, :, :], scalar=0.0, in1=gath[:, :, 3 * G:4 * G],
                           op0=ALU.max, op1=ALU.mult))
                link_c(red(mag[:, :], sp0[:, :, :], X, ALU.add))
                link_c(tt(mag[:, :], mag[:, :], gath[:, :, 4 * G], ALU.add))
                link_c(ts(mag[:, :], mag[:, :], out_scale[:, 0:1], None, ALU.mult))
                dve.wait_ge(h2_tok_rdy, NT * (c + 1))
                need(dve, res_rdy, 2 * c)
                for t in range(PT):
                    stt(out=y[:, t, :], in0=gath[:, t, PAR:GW], scalar=mag[:, t:t + 1], in1=h2_tok[:, t, :],
                        op0=ALU.mult, op1=ALU.add).then_inc(y_sem, 1)
                for t in range(PT):
                    dve.wait_ge(y_sem, PT * c + t + 1)
                    dve_c.mark(v.bn_stats(st3[:, t, :], y[:, t, :]))
                dve_c.wait(dve)
                variance(dve_c, st3, sum3[:, :], dif3[:, :], var3[:, :], ln3_var)

            def c_norm3(c):
                dve.wait_ge(ln3_guess, c + 1)
                newton(dve_c, var3[:, :], guess3[:, :], newt3[:, :], rstd3[:, :], nmr3[:, :], sum3[:, :], ln3_ready)

            def superstep(k, c, b, nxt):
                C = c is not None
                if C:
                    c_var(c)
                if b:
                    b_split(k, 0)
                if C:
                    c_norm(c)
                if b:
                    a_stats(k, 1)
                    b_max(k, 0, 0)
                    b_max(k, 0, 1)
                    a_norm(k, 1)
                if C:
                    c_split(c, 0)
                    c_split(c, 1)
                if b:
                    b_max(k, 0, 2)
                    a_split(k, 1)
                    b_gate(k, 0, 0)
                    b_max(k, 0, 3)
                if C:
                    c_split(c, 2)
                    c_split(c, 3)
                if b:
                    b_gate(k, 0, 1)
                    b_gate(k, 0, 2)
                if C:
                    c_hidden(c)
                if b:
                    b_gate(k, 0, 3)
                if C:
                    c_cluster(c)
                if b:
                    b_split(k, 1)
                    b_stats(k, 0)
                    b_max(k, 1, 0)
                    b_max(k, 1, 1)
                    if nxt:
                        a_stats(k + 1, 0)
                    b_max(k, 1, 2)
                    b_max(k, 1, 3)
                    if nxt:
                        a_norm(k + 1, 0)
                    b_gate(k, 1, 0)
                if C:
                    c_local(c)
                if b and nxt:
                    a_split(k + 1, 0)
                if b:
                    b_gate(k, 1, 1)
                if C:
                    c_comp(c)
                if b:
                    b_gate(k, 1, 2)
                    b_gate(k, 1, 3)
                    b_stats(k, 1)
                if C:
                    c_spline(c)
                    c_norm3(c)

            a_stats(0, 0)
            a_norm(0, 0)
            a_split(0, 0)
            superstep(0, None, True, True)
            superstep(1, 0, True, True)
            with dve.Fori(2, PAIRS - 1) as k:
                superstep(k, k - 1, True, True)
            superstep(PAIRS - 1, PAIRS - 2, True, False)
            superstep(PAIRS, PAIRS - 1, False, False)


_INS = ['L0_attn_x', 'L0_attn_Wq', 'L0_attn_bq', 'L0_attn_Wk', 'L0_attn_bk', 'L0_attn_Wv', 'L0_attn_bv', 'L0_attn_Wo',
        'L0_attn_bo', 'L0_ffn_signatures_raw', 'L0_ffn_knot_values', 'L0_ffn_temperature', 'L0_ffn_compress_w1',
        'L0_ffn_compress_b1', 'L0_ffn_compress_w2', 'L0_ffn_compress_b2', 'L0_ffn_spline_w1', 'L0_ffn_spline_b1',
        'L0_ffn_spline_w2', 'L0_ffn_spline_b2', 'L0_ffn_directions', 'L0_ffn_norm_gamma', 'L0_ffn_norm_beta',
        'L0_ffn_output_scale', 'L0_c', 'L0_wmod']


def kernel(**inputs):
    import numpy as np
    import concourse.bacc as bacc
    from concourse.bass_utils import run_bass_kernel_spmd

    nc = bacc.Bacc("TRN2", target_bir_lowering=False, num_devices=1)
    arrays, args = {}, {}
    for name in _INS:
        a = np.ascontiguousarray(inputs[name])
        arrays[f"in_{name}"] = a
        args[name] = nc.dram_tensor(f"in_{name}", a.shape, mybir.dt.from_np(a.dtype), kind="ExternalInput").ap()
    shape = arrays["in_L0_attn_x"].shape
    out = nc.dram_tensor("out", shape, F32, kind="ExternalOutput").ap()
    adaln_kernel(nc, args, out)
    r = run_bass_kernel_spmd(nc, [arrays], core_ids=[0])
    return r.results[0]["out"]
```

```python
from contextlib import ExitStack

import concourse.bass as bass
from concourse import mybir

F32 = mybir.dt.float32
F32R = mybir.dt.float32r
BF16 = mybir.dt.bfloat16
ALU = mybir.AluOpType
ACT = mybir.ActivationFunctionType
X = mybir.AxisListType.X

P = 128
EPS = 1e-5
TEMP_EPS = 1e-6
Z_MIN = -88.0
MASKED = -1e30
GATE_MIN = 0.25


LOADS_SP, LOADS_ACT = 21, 10
SIG_READY, SILU_READY, CT_READY, ROWS_READY, DVE_SETUP = 21, 24, 25, 32, 62
WOT_READY = ACT_SETUP = 2
POOL_SETUP = 4


class Chain:

    def __init__(self, sem, per):
        self.sem, self.per, self.n, self.i = sem, per, 0, 0

    def at(self, i):
        self.i = i

    def mark(self, ins):
        self.n = self.n % self.per + 1
        ins.then_inc(self.sem, 1)

    def wait(self, eng):
        eng.wait_ge(self.sem, self.per * self.i + self.n)

    def link(self, eng, ins):
        self.mark(ins)
        self.wait(eng)


def need(eng, sem, count):
    if isinstance(count, int) and count <= 0:
        return
    eng.wait_ge(sem, count)


def adaln_kernel(nc, ins, out):
    x_in, wq_in, wo_in = ins["L0_attn_x"], ins["L0_attn_Wq"], ins["L0_attn_Wo"]
    B, S, D = x_in.shape
    NT = S // P
    KC = D // P
    PAIRS = B // 2
    LAG = 3
    PT = 2 * NT
    NTILES = ins["L0_ffn_signatures_raw"].shape[0]
    K = ins["L0_ffn_knot_values"].shape[0]
    H = ins["L0_ffn_compress_w1"].shape[1]
    GRID = ins["L0_ffn_spline_b1"].shape[1]
    TPC = 8
    NCL = NTILES // TPC
    NCOMP = ins["L0_ffn_compress_w2"].shape[1]
    VW = D + 2
    FW = NCL + NTILES + H
    PAR = NCOMP * GRID + 2 * GRID + 2
    GW = PAR + D
    SCALE = float(D) ** -0.5
    assert NT == 4 and KC == 2 and NCL == 8 and 2 * NTILES == P and SCALE == 0.0625

    gate_rows = nc.dram_tensor("gate_rows", (B, 3 * D), F32, kind="Internal").ap()

    with ExitStack() as ctx:
        def sb(name, shape, dt=F32):
            return ctx.enter_context(nc.sbuf_tensor(name, shape, dt))

        def sem(name):
            return ctx.enter_context(nc.semaphore(name))

        banks = [ctx.enter_context(nc.psum_tensor(f"bank{i}", [P, 512], F32)) for i in range(8)]
        turn_ps = banks[0:2]
        mix_ps = banks[2:5]
        score_ps = banks[5:7]
        attn_ps = banks[7]
        turn_order = """XT10 XT11 PT00 PT01 PT02 PT03 PT10 OHT0 OHT1 PT11 PT12 PT13 XT00 XT01 H2T0 H2T1 H2T2 H2T3""".split()
        mix_order = """FS0 G01 FS1 FS2 BT0 V02 V03 BT1 V10 G10 G11 BT2 V11 BT3 V12 V13 GA0 GA1 GA2 GA3 GA4 GA5 GA6 GA7 G00
                        V00 V01""".split()
        TURN = {name: i % 2 for i, name in enumerate(turn_order)}
        MIX = {name: i % 3 for i, name in enumerate(mix_order)}
        SEQ = "eo"

        ident = sb("ident", [P, P])
        identb = sb("identb", [P, P], BF16)
        causal = sb("causal", [P, P])
        ones2 = sb("ones2", [2, P], F32R)
        a_hi = sb("a_hi", [P, KC, D], F32R)
        a_lo = sb("a_lo", [P, KC, D], F32R)
        m_hi = sb("m_hi", [P, KC, VW], F32R)
        m_lo = sb("m_lo", [P, KC, VW], F32R)
        vbias = sb("vbias", [2, VW], F32R)
        g_bias = sb("g_bias", [P, KC])
        f_hi = sb("f_hi", [P, KC, FW], F32R)
        f_lo = sb("f_lo", [P, KC, FW], F32R)
        table = sb("table", [P, GW], F32R)
        sa_col = sb("sa_col", [P, KC, B])
        ca_col = sb("ca_col", [P, KC, B])
        sb_col = sb("sb_col", [P, KC, B])
        cb_col = sb("cb_col", [P, KC, B])
        b1_row = sb("b1_row", [P, H])
        w2_rows = sb("w2_rows", [P, H, NCOMP])
        b2_row = sb("b2_row", [P, NCOMP])
        knots = sb("knots", [P, K])
        knot_step = sb("knot_step", [P, K - 1])
        inv_temp = sb("inv_temp", [P, 1])
        out_scale = sb("out_scale", [P, 1])
        steps = sb("steps", [P, K])
        falling = sb("falling", [P, TPC])

        x_sb = [sb(f"x{s}", [P, NT, D]) for s in range(2)]
        st1 = sb("st1", [P, NT, 6])
        sum1, dif1, var1, guess1, newt1, rstd1, nmr1 = (
            sb(n, [P, NT]) for n in ("sum1", "dif1", "var1", "guess1", "newt1", "rstd1", "nmr1"))
        xhat = sb("xhat", [P, NT, D])
        h_full = sb("h_full", [P, KC, S])
        h_hi = [sb(f"h_hi{s}", [P, KC, S], F32R) for s in range(2)]
        h_lo = [sb(f"h_lo{s}", [P, KC, S], F32R) for s in range(2)]
        ga_row = [sb(f"ga_row{s}", [P, D]) for s in range(2)]
        g_hi = sb("g_hi", [P, KC, S], F32R)
        g_lo = sb("g_lo", [P, KC, S], F32R)
        v_sb = [sb(f"v{s}", [P, NT, VW]) for s in range(2)]
        absc = [sb(f"absc{j}", [P, S]) for j in range(2)]
        probs = [sb(f"probs{j}", [P, S]) for j in range(2)]
        probsT = [sb(f"probsT{j}", [P, S]) for j in range(2)]
        negmax = sb("negmax", [P, NT])
        rowsum = [sb(f"rowsum{s}", [P, NT]) for s in range(2)]
        rinv = sb("rinv", [P, NT])
        gated = [sb(f"gated{j}", [P, D]) for j in range(2)]
        x2 = [sb(f"x2_{s}", [P, NT, D]) for s in range(2)]
        st2 = sb("st2", [P, PT, 6])
        gb_row = [sb(f"gb_row{s}", [P, 2, D]) for s in range(2)]
        sum2, dif2, var2, guess2, newt2, rstd2, nmr2 = (
            sb(n, [P, PT]) for n in ("sum2", "dif2", "var2", "guess2", "newt2", "rstd2", "nmr2"))
        wide = sb("wide", [P, 4 * KC * S])
        xhat2 = wide[:, 0:PT * D].rearrange("p (t d) -> p t d", t=PT)
        h2_full = wide[:, PT * D:].rearrange("p (s c t) -> p s c t", s=2, c=KC)
        h2_hi = sb("h2_hi", [P, 2, KC, S], F32R)
        h2_lo = sb("h2_lo", [P, 2, KC, S], F32R)
        h2_tok = sb("h2_tok", [P, PT, D])
        fs = sb("fs", [P, PT, FW])
        hid = sb("hid", [P, PT, H])
        w2prod = sb("w2prod", [P, PT, NCOMP, H])
        comp = sb("comp", [P, PT, NCOMP])
        cmp_t = sb("cmp_t", [P, PT, NCOMP])
        E8 = PT * TPC
        z_cl = sb("z_cl", [P, E8])
        z_lo = sb("z_lo", [P, E8])
        cal = [sb(f"cal{j}", [P, E8]) for j in range(5)]
        cal7 = [sb(f"cal7_{j}", [P, E8, K - 1]) for j in range(2)]
        best = sb("best", [P, PT])
        oh_cl = sb("oh_cl", [P, PT, NCL])
        oh_lo = sb("oh_lo", [P, PT, TPC])
        picked = sb("picked", [P, PT, NTILES])
        onehot = sb("onehot", [P, PT, P], BF16)
        onehotT = sb("onehotT", [P, PT * P], F32R)
        gath = sb("gath", [P, PT, GW])
        sp0 = sb("sp0", [P, PT, GRID])
        sp1 = sb("sp1", [P, PT, GRID])
        mag = sb("mag", [P, PT])
        y = sb("y", [P, PT, D])
        st3 = sb("st3", [P, PT, 6])
        sum3, dif3, var3, guess3, newt3, rstd3, nmr3 = (
            sb(n, [P, PT]) for n in ("sum3", "dif3", "var3", "guess3", "newt3", "rstd3", "nmr3"))
        res = sb("res", [P, PT, D])

        w_in = sem("w_in")
        x_ld = [sem(f"x_loaded{s}") for s in range(2)]
        ga_ld = [sem(f"ga_loaded{s}") for s in range(2)]
        gb_ld = [sem(f"gb_loaded{s}") for s in range(2)]
        sent = [sem(f"out_sent{s}") for s in range(2)]
        rows_sent = sem("rows_sent")
        id_ready = sem("ident_ready")
        s_pe, s_dve, s_act, s_pool = sem("setup_pe"), sem("setup_dve"), sem("setup_act"), sem("setup_pool")
        ln1_var, ln1_guess, ln1_ready = sem("ln1_var"), sem("ln1_guess"), sem("ln1_ready")
        xhat_ready = sem("xhat_ready")
        xt_done = sem("xhat_turned")
        h_ready = sem("h_ready")
        h_hi_rdy = sem("h_hi_ready")
        h_lo_rdy = sem("h_lo_ready")
        g_done = sem("g_done")
        g_hi_rdy, g_lo_rdy = sem("g_hi_ready"), sem("g_lo_ready")
        vproj_done = sem("v_done")
        v_ready = sem("v_ready")
        scores_done = sem("scores_done")
        absc_ready = sem("abs_scores_ready")
        masked = sem("diag_masked")
        rowmax = sem("rowmax_ready")
        probs_rdy = sem("probs_ready")
        pt_done = sem("probs_turned")
        pt_rdy = sem("probsT_ready")
        pv_done = sem("pv_done")
        st2_rdy = sem("x2_stats_ready")
        gated_rdy = sem("gated_ready")
        x2_rdy = sem("x2_ready")
        ln2_var = sem("ln2_var")
        ln2_guess, ln2_ready = sem("ln2_guess"), sem("ln2_ready")
        xhat2_rdy = sem("xhat2_ready")
        h2t_done = sem("xhat2_turned")
        h2_rdy = sem("h2_ready")
        h2_hi_rdy, h2_lo_rdy = sem("h2_hi_ready"), sem("h2_lo_ready")
        fs_done = sem("ffn_scores_done")
        fs_rdy = sem("ffn_scores_ready")
        bt_done = sem("h2_turned_back")
        h2_tok_rdy = sem("h2_tok_ready")
        zc_rdy, ec_rdy = sem("cluster_z_ready"), sem("cluster_exp_ready")
        zl_rdy, el_rdy = sem("local_z_ready"), sem("local_exp_ready")
        pregelu, gelu_rdy = sem("pregelu_ready"), sem("gelu_ready")
        pretanh, tanh_rdy = sem("pretanh_ready"), sem("tanh_ready")
        onehot_rdy = sem("onehot_ready")
        oht_done = sem("onehot_turned")
        oht_rdy = sem("onehotT_ready")
        ga_done = sem("gather_done")
        gath_rdy = sem("gathered_ready")
        ln3_var, ln3_guess, ln3_ready = sem("ln3_var"), sem("ln3_guess"), sem("ln3_ready")
        yhat_rdy = sem("yhat_ready")
        base_rdy = sem("base_ready")
        res_rdy = sem("result_ready")
        y_sem = sem("y_ready")
        act_guess1 = Chain(sem("act_chain_a"), 1)
        act_guess2 = Chain(sem("act_chain_ln2"), 1)
        act_guess3 = Chain(sem("act_chain_ln3"), 1)
        dve_a = Chain(sem("dve_chain_a"), NT + 5 + 3)
        dve_b = Chain(sem("dve_chain_b"), NT)
        dve_ln2 = Chain(sem("dve_chain_ln2"), 5 + 3)
        dve_route = Chain(sem("dve_chain_route"), 2 * (13 + 5) + 3 + PT)
        dve_comp = Chain(sem("dve_chain_comp"), NCOMP + 1)
        dve_spline = Chain(sem("dve_chain_spline"), 8)
        dve_ln3 = Chain(sem("dve_chain_ln3"), PT + 5 + 3)
        pool_c = Chain(sem("pool_chain_c"), 2)

        wq, wk, wv, wo = (res[:, KC * i:KC * (i + 1), :] for i in range(4))
        woT = sb("woT", [P, KC, D])
        wmod_sb = wide[:, 0:KC * 6 * D].rearrange("p (c n) -> p c n", c=KC)
        bq, bk, bv = (sb(n, [P, KC]) for n in ("bq", "bk", "bv"))
        bo2 = sb("bo2", [2, D])
        c_sb = sb("c_sb", [B, D])
        c_exp = sb("c_exp", [B, D])
        c_T = sb("c_T", [P, KC, B])
        mod = sb("mod", [B, 3, D])
        rows = sb("rows", [B, 3, D])
        gamma_r, beta_r = sb("gamma_r", [B, D]), sb("beta_r", [B, D])
        sraw = sb("sraw", [NTILES, D])
        sraw8 = h2_tok[0:NCL, :, :]
        sq = sb("sq", [NTILES, D])
        sq8 = y[0:NCL, :, :]
        stmp = sb("stmp", [NTILES, D])
        stmp8 = gath[0:NCL, :, 0:D]
        f_full = sb("f_full", [P, KC, FW])
        t_full = sb("t_full", [P, GW])
        vb2 = sb("vb2", [2, VW])
        vb2_hi, vb2_lo = sb("vb2_hi", [2, VW], F32R), sb("vb2_lo", [2, VW])

        block = ctx.enter_context(nc.Block())

        def seq(p, s):
            return 2 * p + s

        def step(f):
            def run(p, *rest, **named):
                if not isinstance(p, int) or 0 <= p < PAIRS:
                    f(p, *rest, **named)
            return run

        def pipeline(eng, superstep):
            for k in range(LAG + 1):
                superstep(k)
            with eng.Fori(LAG + 1, PAIRS) as k:
                superstep(k)
            for k in range(PAIRS, PAIRS + LAG):
                superstep(k)

        @block.sync
        def _(sp):
            def col(a):
                return a.rearrange("(c p) -> p c", p=P)

            def row(a, n):
                return a.rearrange("(o d) -> o d", o=1).broadcast_to([n, a.shape[0]])

            n = [0]

            def load(dst, src, **kw):
                sp.dma_start(dst, src, **kw).then_inc(w_in, 16)
                n[0] += 1

            x_v = x_in.rearrange("b (t p) d -> b p t d", p=P)
            out_v = out.rearrange("b (t p) d -> b p t d", p=P)

            sp.dma_start(x_sb[0][:, :, :], x_v[0]).then_inc(x_ld[0], 16)
            sp.dma_start(x_sb[1][:, :, :], x_v[1]).then_inc(x_ld[1], 16)
            load(c_sb[:, :], ins["L0_c"])
            load(wmod_sb[:, :, :], ins["L0_wmod"].rearrange("(c p) n -> p c n", p=P))
            for w, name in ((wq, "Wq"), (wk, "Wk"), (wo, "Wo"), (wv, "Wv")):
                load(w[:, :, :], ins[f"L0_attn_{name}"].rearrange("(c p) n -> p c n", p=P))
            for w, name in ((bq, "bq"), (bk, "bk"), (bv, "bv")):
                load(w[:, :], col(ins[f"L0_attn_{name}"]), allow_slow_non_contiguous=True)
            load(bo2[:, :], row(ins["L0_attn_bo"], 2))
            raw = ins["L0_ffn_signatures_raw"]
            load(sraw[:, :], raw)
            load(sraw8[:, :, :], raw.rearrange("(c j) d -> c j d", j=TPC))
            load(f_full[:, :, NCL + NTILES:FW], ins["L0_ffn_compress_w1"].rearrange("(c p) n -> p c n", p=P))
            load(b1_row[:, :], row(ins["L0_ffn_compress_b1"], P))
            load(w2_rows[:, :, :].rearrange("p h o -> p (h o)"),
                 ins["L0_ffn_compress_w2"].rearrange("(a h) o -> a (h o)", a=1).broadcast_to([P, H * NCOMP]))
            load(b2_row[:, :], row(ins["L0_ffn_compress_b2"], P))
            load(knots[:, :], row(ins["L0_ffn_knot_values"], P))
            load(inv_temp[:, :], row(ins["L0_ffn_temperature"], P))
            load(out_scale[:, :], row(ins["L0_ffn_output_scale"], P))
            load(gamma_r[:, :], row(ins["L0_ffn_norm_gamma"], B))
            load(beta_r[:, :], row(ins["L0_ffn_norm_beta"], B))
            assert n[0] == LOADS_SP

            sp.wait_ge(s_dve, ROWS_READY)
            sp.dma_start(gate_rows, rows[:, :, :].rearrange("b a d -> b (a d)")).then_inc(rows_sent, 16)
            sp.wait_ge(rows_sent, 16)

            def gate_row(i, a, n_rows):
                r = gate_rows[bass.ds(i, 1), a * D:(a + n_rows) * D]
                return r.broadcast_to([P, n_rows * D])

            def ga_load(p, s):
                sp.dma_start(ga_row[s][:, :], gate_row(seq(p, s), 0, 1)).then_inc(ga_ld[s], 16)

            ga_load(0, 0)
            ga_load(0, 1)

            @step
            def load_x(p, s):
                if isinstance(p, int) and p == 0:
                    return
                sp.wait_ge(x2_rdy, NT * seq(p - 1, s) + NT)
                sp.dma_start(x_sb[s][:, :, :], x_v[bass.ds(seq(p, s), 1)].rearrange("o p t d -> (o p) t d")
                             ).then_inc(x_ld[s], 16)
                ga_load(p, s)

            @step
            def load_gb(p, s):
                need(sp, res_rdy, 2 * (p - 1) + s + 1)
                sp.dma_start(gb_row[s][:, :, :].rearrange("p a d -> p (a d)"),
                             gate_row(seq(p, s), 1, 2)).then_inc(gb_ld[s], 16)

            @step
            def send(p, s):
                sp.wait_ge(res_rdy, 2 * p + s + 1)
                sp.dma_start(out_v[bass.ds(seq(p, s), 1)].rearrange("o p t d -> (o p) t d"),
                             res[:, NT * s:NT * (s + 1), :]).then_inc(sent[s], 16)

            def superstep(k):
                load_gb(k - 3, 1)
                load_x(k - 1, 0)
                load_x(k - 1, 1)
                load_gb(k - 2, 0)
                send(k - 3, 0)
                send(k - 3, 1)

            pipeline(sp, superstep)
            for s in range(2):
                sp.wait_ge(sent[s], 16 * PAIRS)

        @block.tensor
        def _(pe):
            mm, tr = nc.tensor.matmul, nc.tensor.transpose
            pe.wait_ge(id_ready, 1)
            pe.wait_ge(w_in, 16 * (LOADS_SP + LOADS_ACT))
            for m in range(KC):
                for c in range(KC):
                    last = mm(banks[0][:, m * D:(m + 1) * D], wq[:, c, m * P:(m + 1) * P], wk[:, c, :],
                              start=(c == 0), stop=(c == KC - 1))
            last.then_inc(s_pe, 1)
            for v in range(KC):
                for o in range(KC):
                    last = tr(banks[1][:, v * D + o * P:v * D + (o + 1) * P], wo[:, o, v * P:(v + 1) * P], ident[:, :])
            last.then_inc(s_pe, 1)
            for m in range(KC):
                for c in range(KC):
                    mm(banks[3][:, m:m + 1], wq[:, c, m * P:(m + 1) * P], bk[:, c:c + 1],
                       start=(c == 0), stop=(c == KC - 1))
                for c in range(KC):
                    last = mm(banks[3][:, KC + m:KC + m + 1], wk[:, c, m * P:(m + 1) * P], bq[:, c:c + 1],
                              start=(c == 0), stop=(c == KC - 1))
            last.then_inc(s_pe, 1)
            pe.wait_ge(s_dve, SIG_READY)
            for c in range(KC):
                tr(banks[7][:, c * FW + NCL:c * FW + NCL + NTILES], sq[:, c * P:(c + 1) * P], ident[0:NTILES, 0:NTILES])
                last = tr(banks[7][:, c * FW:c * FW + NCL], sq8[:, 0, c * P:(c + 1) * P], ident[0:NCL, 0:NCL])
            last.then_inc(s_pe, 1)
            pe.wait_ge(s_dve, SILU_READY)
            for c in range(KC):
                last = tr(banks[5][:, c * B:(c + 1) * B], c_sb[:, c * P:(c + 1) * P], ident[0:B, 0:B])
            last.then_inc(s_pe, 1)
            pe.wait_ge(s_act, WOT_READY)
            for m in range(KC):
                for v in range(KC):
                    last = mm(banks[2][:, m * D:(m + 1) * D], wv[:, v, m * P:(m + 1) * P], woT[:, v, :],
                              start=(v == 0), stop=(v == KC - 1))
            last.then_inc(s_pe, 1)
            for v in range(KC):
                mm(banks[4][0:2, 0:D], bv[:, v:v + 1].broadcast_to([P, 2]), woT[:, v, :],
                   start=(v == 0), stop=(v == KC - 1))
            for c in range(KC):
                last = mm(banks[4][0:2, D:D + 1], bq[:, c:c + 1].broadcast_to([P, 2]), bk[:, c:c + 1],
                          start=(c == 0), stop=(c == KC - 1))
            last.then_inc(s_pe, 1)
            pe.wait_ge(s_dve, CT_READY)
            for i, j in enumerate((0, 1, 3, 4)):
                for m in range(KC):
                    o = (i * KC + m) * B
                    for c in range(KC):
                        last = mm(banks[6][:, o:o + B], wmod_sb[:, c, j * D + m * P:j * D + (m + 1) * P], c_T[:, c, :],
                                  start=(c == 0), stop=(c == KC - 1))
            last.then_inc(s_pe, 1)
            for i, j in enumerate((2, 5)):
                for c in range(KC):
                    last = mm(banks[5][0:B, i * D:(i + 1) * D], c_T[:, c, :], wmod_sb[:, c, j * D:(j + 1) * D],
                              start=(c == 0), stop=(c == KC - 1))
            last.then_inc(s_pe, 1)
            pe.wait_ge(s_dve, DVE_SETUP)
            pe.wait_ge(s_act, ACT_SETUP)

            reader = {}

            def free(name, p, reads, count):
                bank = TURN[name] if name in TURN else 2 + MIX[name]
                if bank in reader:
                    before, at, when = reader[bank]
                    pe.wait_ge(before, at(when))
                reader[bank] = (reads, count, p)
                return banks[bank]

            def split3(ps, lhs_hi, lhs_lo, rhs_hi, rhs_lo, start=True, stop=True):
                ops = [(a(c), b(c)) for c in range(KC)
                       for a, b in ((lhs_hi, rhs_hi), (lhs_hi, rhs_lo), (lhs_lo, rhs_hi))]
                for i, (a, b) in enumerate(ops):
                    last = mm(ps, a, b, start=start and i == 0, stop=stop and i == len(ops) - 1)
                return last

            @step
            def x_turn(p, s, c):
                ps = free(f"XT{s}{c}", p, h_ready, lambda q: KC * seq(q, s) + c + 1)
                pe.wait_ge(xhat_ready, NT * seq(p, s) + NT)
                for t in range(NT):
                    last = tr(ps[:, t * P:(t + 1) * P], xhat[:, t, c * P:(c + 1) * P], ident[:, :])
                last.then_inc(xt_done, 1)

            @step
            def project_g(p, s, m):
                ps = free(f"G{s}{m}", p, g_lo_rdy, lambda q: KC * seq(q, s) + m + 1)
                pe.wait_ge(h_lo_rdy, KC * seq(p, s) + KC)
                split3(ps[:, 0:S], lambda c: a_hi[:, c, m * P:(m + 1) * P], lambda c: a_lo[:, c, m * P:(m + 1) * P],
                       lambda c: h_hi[s][:, c, :], lambda c: h_lo[s][:, c, :]).then_inc(g_done, 1)

            @step
            def project_v(p, s, t):
                ps = free(f"V{s}{t}", p, v_ready, lambda q: NT * seq(q, s) + t + 1)
                pe.wait_ge(h_lo_rdy, KC * seq(p, s) + KC)
                mm(ps[:, 0:VW], ones2[:, :], vbias[:, :], start=True, stop=False)
                split3(ps[:, 0:VW], lambda c: h_hi[s][:, c, t * P:(t + 1) * P], lambda c: h_lo[s][:, c, t * P:(t + 1) * P],
                       lambda c: m_hi[:, c, :], lambda c: m_lo[:, c, :], start=False).then_inc(vproj_done, 1)

            @step
            def scores(p, s, t):
                b = seq(p, s)
                if t == 0:
                    pe.wait_ge(g_lo_rdy, KC * b + KC)
                need(pe, absc_ready, NT * b + t - 1)
                w = (t + 1) * P
                split3(score_ps[t % 2][:, 0:w], lambda c: g_hi[:, c, t * P:(t + 1) * P], lambda c: g_lo[:, c, t * P:(t + 1) * P],
                       lambda c: h_hi[s][:, c, 0:w], lambda c: h_lo[s][:, c, 0:w]).then_inc(scores_done, 1)

            @step
            def p_turn(p, s, t):
                b = seq(p, s)
                ps = free(f"PT{s}{t}", p, pt_rdy, lambda q: NT * seq(q, s) + t + 1)
                pe.wait_ge(probs_rdy, NT * b + t + 1)
                for j in range(t + 1):
                    last = tr(ps[:, j * P:(j + 1) * P], probs[t % 2][:, j * P:(j + 1) * P], ident[:, :])
                last.then_inc(pt_done, 1)

            @step
            def attend(p, s, t):
                b = seq(p, s)
                need(pe, gated_rdy, NT * b + t)
                pe.wait_ge(pt_rdy, NT * b + t + 1)
                for j in range(t + 1):
                    last = mm(attn_ps[:, 0:D], probsT[t % 2][:, j * P:(j + 1) * P],
                              v_sb[s][:, j, 0:D], start=(j == 0), stop=(j == t))
                last.then_inc(pv_done, 1)

            @step
            def h2_turn(p, u):
                s, m = u // KC, u % KC
                ps = free(f"H2T{u}", p, h2_rdy, lambda q: 2 * KC * q + u + 1)
                pe.wait_ge(xhat2_rdy, PT * p + NT * (s + 1))
                for t in range(NT):
                    last = tr(ps[:, t * P:(t + 1) * P], xhat2[:, NT * s + t, m * P:(m + 1) * P], ident[:, :])
                last.then_inc(h2t_done, 1)

            @step
            def ffn_scores(p, u):
                ps = free(f"FS{u}", p, fs_rdy, lambda q: 3 * q + u + 1)
                tiles = range(3 * u, min(3 * u + 3, PT))
                pe.wait_ge(h2_lo_rdy, 2 * KC * p + KC * (tiles[-1] // NT + 1))
                for i, t in enumerate(tiles):
                    s, q = t // NT, (t % NT) * P
                    last = split3(ps[:, i * FW:(i + 1) * FW], lambda m: h2_hi[:, s, m, q:q + P], lambda m: h2_lo[:, s, m, q:q + P],
                                  lambda m: f_hi[:, m, :], lambda m: f_lo[:, m, :])
                last.then_inc(fs_done, 1)

            @step
            def turn_back(p, u):
                ps = free(f"BT{u}", p, h2_tok_rdy, lambda q: NT * q + u + 1)
                pe.wait_ge(h2_rdy, 2 * KC * p + KC * (u // 2 + 1))
                for i in range(2):
                    t = 2 * u + i
                    for m in range(KC):
                        q = (t % NT) * P
                        last = tr(ps[:, i * D + m * P:i * D + (m + 1) * P], h2_full[:, t // NT, m, q:q + P], ident[:, :])
                last.then_inc(bt_done, 1)

            @step
            def onehot_turn(p, u):
                ps = free(f"OHT{u}", p, oht_rdy, lambda q: 2 * q + u + 1)[:, :].bitcast(BF16)
                pe.wait_ge(onehot_rdy, p + 1)
                for i in range(NT):
                    last = tr(ps[:, i * P:(i + 1) * P], onehot[:, NT * u + i, :], identb[:, :])
                last.then_inc(oht_done, 1)

            @step
            def gather(p, t):
                ps = free(f"GA{t}", p, gath_rdy, lambda q: PT * q + t + 1)
                pe.wait_ge(oht_rdy, 2 * p + t // NT + 1)
                mm(ps[:, 0:GW], onehotT[:, t * P:(t + 1) * P], table[:, :], start=True, stop=True).then_inc(ga_done, 1)

            def superstep(k):
                if not isinstance(k, int):
                    lags = {bank: LAG - p for bank, (_, _, p) in reader.items()}
                    for bank, (r, at, _) in list(reader.items()):
                        reader[bank] = (r, at, k - 1 - lags[bank])
                ffn_scores(k - 3, 0)
                project_g(k - 2, 0, 1)
                ffn_scores(k - 3, 1)
                ffn_scores(k - 3, 2)
                turn_back(k - 3, 0)
                project_v(k - 2, 0, 2)
                scores(k - 2, 0, 0)
                scores(k - 2, 0, 1)
                project_v(k - 2, 0, 3)
                x_turn(k - 2, 1, 0)
                scores(k - 2, 0, 2)
                x_turn(k - 2, 1, 1)
                p_turn(k - 2, 0, 0)
                turn_back(k - 3, 1)
                scores(k - 2, 0, 3)
                attend(k - 2, 0, 0)
                p_turn(k - 2, 0, 1)
                project_v(k - 2, 1, 0)
                project_g(k - 2, 1, 0)
                project_g(k - 2, 1, 1)
                p_turn(k - 2, 0, 2)
                attend(k - 2, 0, 1)
                turn_back(k - 3, 2)
                project_v(k - 2, 1, 1)
                scores(k - 2, 1, 0)
                turn_back(k - 3, 3)
                attend(k - 2, 0, 2)
                scores(k - 2, 1, 1)
                p_turn(k - 2, 0, 3)
                scores(k - 2, 1, 2)
                attend(k - 2, 0, 3)
                project_v(k - 2, 1, 2)
                p_turn(k - 2, 1, 0)
                project_v(k - 2, 1, 3)
                attend(k - 2, 1, 0)
                onehot_turn(k - 3, 0)
                onehot_turn(k - 3, 1)
                scores(k - 2, 1, 3)
                p_turn(k - 2, 1, 1)
                gather(k - 3, 0)
                p_turn(k - 2, 1, 2)
                gather(k - 3, 1)
                attend(k - 2, 1, 1)
                gather(k - 3, 2)
                p_turn(k - 2, 1, 3)
                attend(k - 2, 1, 2)
                gather(k - 3, 3)
                attend(k - 2, 1, 3)
                gather(k - 3, 4)
                gather(k - 3, 5)
                x_turn(k - 1, 0, 0)
                gather(k - 3, 6)
                x_turn(k - 1, 0, 1)
                gather(k - 3, 7)
                h2_turn(k - 2, 0)
                h2_turn(k - 2, 1)
                project_g(k - 1, 0, 0)
                h2_turn(k - 2, 2)
                project_v(k - 1, 0, 0)
                project_v(k - 1, 0, 1)
                h2_turn(k - 2, 3)
                if not isinstance(k, int):
                    for bank, (r, at, _) in list(reader.items()):
                        reader[bank] = (r, at, PAIRS - 1 - lags[bank])

            pipeline(pe, superstep)

        @block.scalar
        def _(act):
            A = nc.scalar.activation
            n = [0]

            def load(dst, src):
                act.dma_start(dst, src).then_inc(w_in, 16)
                n[0] += 1

            G = GRID
            for h in range(2):
                r = slice(h * NTILES, (h + 1) * NTILES)
                load(t_full[r, 0:2 * G], ins["L0_ffn_spline_w1"].rearrange("n i g -> n (i g)"))
                load(t_full[r, 2 * G:3 * G], ins["L0_ffn_spline_b1"])
                load(t_full[r, 3 * G:4 * G], ins["L0_ffn_spline_w2"].rearrange("n g o -> n (g o)"))
                load(t_full[r, 4 * G:4 * G + 1], ins["L0_ffn_spline_b2"])
                load(t_full[r, PAR:GW], ins["L0_ffn_directions"])
            assert n[0] == LOADS_ACT
            nc.scalar.preload_act_table_set("natural_log_exp_and_others")
            act.wait_ge(w_in, 16 * (LOADS_SP + LOADS_ACT))
            A(c_exp[:, :], c_sb[:, :], ACT.Exp, scale=-1.0).then_inc(s_act, 1)
            act.wait_ge(s_pe, 2)
            A(woT[:, :, :].rearrange("p c d -> p (c d)"), banks[1][:, :], ACT.Copy).then_inc(s_act, 1)

            def ln_guess(out_, var, ready, chain, i, signal):
                act.wait_ge(ready, i + 1)
                chain.link(act, A(out_, var, ACT.Ln))
                A(out_, out_, ACT.Exp, scale=-0.5).then_inc(signal, 1)

            @step
            def a_guess(p, s):
                b = seq(p, s)
                act_guess1.at(b)
                ln_guess(guess1[:, :], var1[:, :], ln1_var, act_guess1, b, ln1_guess)

            @step
            def a_xhat(p, s, t):
                b = seq(p, s)
                act.wait_ge(ln1_ready, b + 1)
                need(act, xt_done, KC * b)
                A(xhat[:, t, :], x_sb[s][:, t, :], ACT.Identity, bias=nmr1[:, t:t + 1],
                  scale=rstd1[:, t:t + 1]).then_inc(xhat_ready, 1)

            @step
            def a_evict(p, s, c):
                b = seq(p, s)
                act.wait_ge(xt_done, KC * b + c + 1)
                need(act, h_lo_rdy, KC * (b - 1) + c + 1)
                A(h_full[:, c, :], turn_ps[TURN[f"XT{s}{c}"]][:, :], ACT.Identity,
                  bias=sa_col[:, c, bass.ds(b, 1)], scale=ca_col[:, c, bass.ds(b, 1)]).then_inc(h_ready, 1)

            @step
            def b_g(p, s, c):
                b = seq(p, s)
                act.wait_ge(g_done, KC * b + c + 1)
                need(act, scores_done, NT * b)
                A(g_hi[:, c, :], mix_ps[MIX[f"G{s}{c}"]][:, :], ACT.Identity,
                  bias=g_bias[:, c:c + 1]).then_inc(g_hi_rdy, 1)

            @step
            def b_v(p, s, t):
                b = seq(p, s)
                act.wait_ge(vproj_done, NT * b + t + 1)
                need(act, pv_done, NT * (b - 1))
                A(v_sb[s][:, t, :], mix_ps[MIX[f"V{s}{t}"]][:, 0:VW], ACT.Identity).then_inc(v_ready, 1)

            @step
            def b_abs(p, s, t):
                b, w = seq(p, s), (t + 1) * P
                act.wait_ge(scores_done, NT * b + t + 1)
                act.wait_ge(v_ready, NT * b + t + 1)
                need(act, probs_rdy, NT * b + t - 1)
                A(absc[t % 2][:, 0:w], score_ps[t % 2][:, 0:w], ACT.Abs, bias=v_sb[s][:, t, D:D + 1],
                  scale=SCALE).then_inc(absc_ready, 1)

            @step
            def b_exp(p, s, t):
                b, w = seq(p, s), (t + 1) * P
                act.wait_ge(rowmax, NT * b + t + 1)
                need(act, pt_done, NT * b + t - 1)
                if t == 0:
                    need(act, gated_rdy, NT * (b - 1))
                A(probs[t % 2][:, 0:w], absc[t % 2][:, 0:w], ACT.Exp, bias=negmax[:, t:t + 1],
                  accum_out=rowsum[s][:, t:t + 1]).then_inc(probs_rdy, 1)

            @step
            def b_pt(p, s, t):
                b, w = seq(p, s), (t + 1) * P
                act.wait_ge(pt_done, NT * b + t + 1)
                need(act, pv_done, NT * b + t - 1)
                A(probsT[t % 2][:, 0:w], turn_ps[TURN[f"PT{s}{t}"]][:, 0:w], ACT.Identity).then_inc(pt_rdy, 1)

            @step
            def c_guess2(p):
                act_guess2.at(p)
                ln_guess(guess2[:, :], var2[:, :], ln2_var, act_guess2, p, ln2_guess)

            @step
            def c_xhat2(p, t):
                act.wait_ge(ln2_ready, p + 1)
                need(act, h2t_done, 2 * KC * (p - 1) + KC * (t // NT + 1))
                A(xhat2[:, t, :], x2[t // NT][:, t % NT, :], ACT.Identity, bias=nmr2[:, t:t + 1],
                  scale=rstd2[:, t:t + 1]).then_inc(xhat2_rdy, 1)

            @step
            def c_h2(p, u):
                s, m = u // KC, u % KC
                b = seq(p, s)
                act.wait_ge(h2t_done, 2 * KC * p + u + 1)
                need(act, h2_lo_rdy, 2 * KC * (p - 1) + u + 1)
                need(act, bt_done, NT * (p - 1) + 2 * (s + 1))
                A(h2_full[:, s, m, :], turn_ps[TURN[f"H2T{u}"]][:, :], ACT.Identity,
                  bias=sb_col[:, m, bass.ds(b, 1)], scale=cb_col[:, m, bass.ds(b, 1)]).then_inc(h2_rdy, 1)

            @step
            def c_fs(p, u):
                n_ = min(3, PT - 3 * u)
                act.wait_ge(fs_done, 3 * p + u + 1)
                need(act, onehot_rdy, p)
                need(act, pregelu, p)
                A(fs[:, 3 * u:3 * u + n_, :].rearrange("p t f -> p (t f)"), mix_ps[MIX[f"FS{u}"]][:, 0:n_ * FW],
                  ACT.Identity).then_inc(fs_rdy, 1)

            @step
            def c_back(p, u):
                act.wait_ge(bt_done, NT * p + u + 1)
                need(act, y_sem, PT * (p - 1) + 2 * (u + 1))
                A(h2_tok[:, 2 * u:2 * u + 2, :].rearrange("p t d -> p (t d)"), mix_ps[MIX[f"BT{u}"]][:, :],
                  ACT.Identity).then_inc(h2_tok_rdy, 1)

            @step
            def c_exp_cl(p):
                act.wait_ge(zc_rdy, p + 1)
                A(z_cl[:, :], z_cl[:, :], ACT.Exp, scale=-1.0).then_inc(ec_rdy, 1)

            @step
            def c_exp_lo(p):
                act.wait_ge(zl_rdy, p + 1)
                A(z_lo[:, :], z_lo[:, :], ACT.Exp, scale=-1.0).then_inc(el_rdy, 1)

            @step
            def c_gelu(p):
                act.wait_ge(pregelu, p + 1)
                A(hid[:, :, :], hid[:, :, :], ACT.Gelu).then_inc(gelu_rdy, 1)

            @step
            def c_tanh(p):
                act.wait_ge(pretanh, p + 1)
                need(act, y_sem, PT * (p - 1) + 1)
                A(comp[:, :, :], cmp_t[:, :, :], ACT.Tanh).then_inc(tanh_rdy, 1)
                nc.scalar.preload_act_table_set("natural_log_exp_and_others")

            @step
            def c_onehot(p, u):
                act.wait_ge(oht_done, 2 * p + u + 1)
                need(act, ga_done, PT * (p - 1) + NT * (u + 1))
                A(onehotT[:, u * S:(u + 1) * S], turn_ps[TURN[f"OHT{u}"]][:, :].bitcast(BF16)[:, 0:S],
                  ACT.Identity).then_inc(oht_rdy, 1)

            @step
            def c_gath(p, t):
                act.wait_ge(ga_done, PT * p + t + 1)
                need(act, y_sem, PT * (p - 1) + t + 1)
                A(gath[:, t, :], mix_ps[MIX[f"GA{t}"]][:, 0:GW], ACT.Identity).then_inc(gath_rdy, 1)

            @step
            def c_guess3(p):
                act_guess3.at(p)
                ln_guess(guess3[:, :], var3[:, :], ln3_var, act_guess3, p, ln3_guess)

            @step
            def c_yhat(p, t):
                act.wait_ge(ln3_ready, p + 1)
                A(y[:, t, :], y[:, t, :], ACT.Identity, bias=nmr3[:, t:t + 1],
                  scale=rstd3[:, t:t + 1]).then_inc(yhat_rdy, 1)

            act.wait_ge(s_dve, DVE_SETUP)

            def superstep(k):
                c_exp_lo(k - 3)
                b_exp(k - 2, 0, 2)
                b_g(k - 2, 1, 0)
                b_g(k - 2, 1, 1)
                c_gelu(k - 3)
                b_pt(k - 2, 0, 2)
                b_abs(k - 2, 1, 0)
                b_exp(k - 2, 0, 3)
                b_pt(k - 2, 0, 3)
                b_v(k - 2, 1, 1)
                b_abs(k - 2, 1, 1)
                b_exp(k - 2, 1, 0)
                c_back(k - 3, 2)
                c_back(k - 3, 3)
                b_exp(k - 2, 1, 1)
                b_v(k - 2, 1, 2)
                b_pt(k - 2, 1, 0)
                b_abs(k - 2, 1, 2)
                b_v(k - 2, 1, 3)
                c_onehot(k - 3, 0)
                c_onehot(k - 3, 1)
                b_exp(k - 2, 1, 2)
                b_abs(k - 2, 1, 3)
                b_pt(k - 2, 1, 1)
                c_gath(k - 3, 0)
                c_gath(k - 3, 1)
                b_pt(k - 2, 1, 2)
                b_exp(k - 2, 1, 3)
                c_tanh(k - 3)
                b_pt(k - 2, 1, 3)
                a_guess(k - 1, 0)
                c_gath(k - 3, 2)
                a_xhat(k - 1, 0, 0)
                a_xhat(k - 1, 0, 1)
                a_xhat(k - 1, 0, 2)
                a_xhat(k - 1, 0, 3)
                c_gath(k - 3, 3)
                c_gath(k - 3, 4)
                c_gath(k - 3, 5)
                a_evict(k - 1, 0, 0)
                c_guess2(k - 2)
                c_gath(k - 3, 6)
                c_gath(k - 3, 7)
                a_evict(k - 1, 0, 1)
                c_xhat2(k - 2, 0)
                c_xhat2(k - 2, 1)
                c_xhat2(k - 2, 2)
                c_xhat2(k - 2, 3)
                c_xhat2(k - 2, 4)
                c_xhat2(k - 2, 5)
                c_xhat2(k - 2, 6)
                c_h2(k - 2, 0)
                c_xhat2(k - 2, 7)
                c_h2(k - 2, 1)
                b_g(k - 1, 0, 0)
                c_h2(k - 2, 2)
                b_v(k - 1, 0, 0)
                c_h2(k - 2, 3)
                a_guess(k - 1, 1)
                b_v(k - 1, 0, 1)
                c_fs(k - 2, 0)
                b_g(k - 1, 0, 1)
                a_xhat(k - 1, 1, 0)
                c_fs(k - 2, 1)
                c_guess3(k - 3)
                c_fs(k - 2, 2)
                a_xhat(k - 1, 1, 1)
                c_exp_cl(k - 2)
                c_yhat(k - 3, 0)
                a_xhat(k - 1, 1, 2)
                b_abs(k - 1, 0, 0)
                c_yhat(k - 3, 1)
                c_yhat(k - 3, 2)
                c_yhat(k - 3, 3)
                a_xhat(k - 1, 1, 3)
                c_yhat(k - 3, 4)
                b_abs(k - 1, 0, 1)
                a_evict(k - 1, 1, 0)
                c_back(k - 2, 0)
                b_exp(k - 1, 0, 0)
                b_v(k - 1, 0, 2)
                a_evict(k - 1, 1, 1)
                c_yhat(k - 3, 5)
                b_pt(k - 1, 0, 0)
                b_v(k - 1, 0, 3)
                c_back(k - 2, 1)
                c_yhat(k - 3, 6)
                b_exp(k - 1, 0, 1)
                b_abs(k - 1, 0, 2)
                b_abs(k - 1, 0, 3)
                c_yhat(k - 3, 7)
                b_pt(k - 1, 0, 1)
                b_v(k - 1, 1, 0)

            pipeline(act, superstep)

        @block.gpsimd
        def _(pool):
            gp = nc.gpsimd
            n = [0]

            def link(ins_):
                n[0] += 1
                ins_.then_inc(s_pool, 1)
                pool.wait_ge(s_pool, n[0])

            link(gp.memset(ident[:, :], 0.0))
            gp.affine_select(out=ident[:, :], in_=ident[:, :], compare_op=ALU.not_equal, fill=1.0, base=0,
                             pattern=[[-1, P]], channel_multiplier=1).then_inc(id_ready, 1)
            link(gp.memset(causal[:, :], 0.0))
            gp.affine_select(out=causal[:, :], in_=causal[:, :], compare_op=ALU.is_ge, fill=MASKED, base=0,
                             pattern=[[-1, P]], channel_multiplier=1)
            for j in range(K):
                gp.memset(steps[:, j:j + 1], float(j))
            for j in range(TPC):
                gp.memset(falling[:, j:j + 1], float(TPC - j))
            link(gp.memset(t_full[:, PAR - 1:PAR], 0.0))
            link(gp.memset(vb2[:, :], 0.0))
            assert n[0] == POOL_SETUP

            @step
            def split_h(p, s, c):
                pool.wait_ge(h_hi_rdy, KC * seq(p, s) + c + 1)
                gp.tensor_tensor(h_lo[s][:, c, :], h_full[:, c, :], h_hi[s][:, c, :].bitcast(F32),
                                 ALU.subtract).then_inc(h_lo_rdy, 1)

            @step
            def mask(p, s, t):
                pool.wait_ge(absc_ready, NT * seq(p, s) + t + 1)
                d = absc[t % 2][:, t * P:(t + 1) * P]
                gp.tensor_tensor(d, d, causal[:, :], ALU.add).then_inc(masked, 1)

            @step
            def residual(p, s, t):
                pool.wait_ge(gated_rdy, NT * seq(p, s) + t + 1)
                if t == 0:
                    need(pool, xhat2_rdy, PT * (p - 1) + NT * (s + 1))
                    need(pool, base_rdy, 2 * (p - 1) + s + 1)
                gp.tensor_tensor(x2[s][:, t, :], gated[t % 2][:, :], x_sb[s][:, t, :], ALU.add).then_inc(x2_rdy, 1)

            @step
            def split_h2(p, u):
                s, m = u // KC, u % KC
                pool.wait_ge(h2_hi_rdy, 2 * KC * p + u + 1)
                gp.tensor_tensor(h2_lo[:, s, m, :], h2_full[:, s, m, :], h2_hi[:, s, m, :].bitcast(F32),
                                 ALU.subtract).then_inc(h2_lo_rdy, 1)

            @step
            def base(p, s):
                pool.wait_ge(gb_ld[s], 16 * (p + 1))
                pool.wait_ge(x2_rdy, NT * seq(p, s) + NT)
                need(pool, sent[s], 16 * p)
                gp.tensor_tensor(res[:, NT * s:NT * (s + 1), :], x2[s][:, :, :],
                                 gb_row[s][:, 1:2, :].broadcast_to([P, NT, D]), ALU.add).then_inc(base_rdy, 1)

            @step
            def finish(p, s):
                pool_c.at(p)
                pool.wait_ge(yhat_rdy, PT * p + NT * (s + 1))
                ys = y[:, NT * s:NT * (s + 1), :]
                pool_c.link(pool, gp.tensor_tensor(ys, ys, gb_row[s][:, 0:1, :].broadcast_to([P, NT, D]), ALU.mult))
                pool.wait_ge(base_rdy, 2 * p + s + 1)
                rs = res[:, NT * s:NT * (s + 1), :]
                gp.tensor_tensor(rs, rs, ys, ALU.add).then_inc(res_rdy, 1)

            def superstep(k):
                mask(k - 2, 1, 0)
                residual(k - 2, 0, 0)
                residual(k - 2, 0, 1)
                mask(k - 2, 1, 1)
                residual(k - 2, 0, 2)
                residual(k - 2, 0, 3)
                mask(k - 2, 1, 2)
                base(k - 3, 1)
                mask(k - 2, 1, 3)
                residual(k - 2, 1, 0)
                residual(k - 2, 1, 1)
                residual(k - 2, 1, 2)
                residual(k - 2, 1, 3)
                split_h(k - 1, 0, 0)
                split_h(k - 1, 0, 1)
                split_h2(k - 2, 0)
                split_h2(k - 2, 1)
                split_h2(k - 2, 2)
                split_h2(k - 2, 3)
                mask(k - 1, 0, 0)
                finish(k - 3, 0)
                mask(k - 1, 0, 1)
                split_h(k - 1, 1, 0)
                split_h(k - 1, 1, 1)
                mask(k - 1, 0, 2)
                mask(k - 1, 0, 3)
                finish(k - 3, 1)
                base(k - 2, 0)

            pipeline(pool, superstep)

        @block.vector
        def _(dve):
            v = nc.vector
            tt, ts, stt, red = v.tensor_tensor, v.tensor_scalar, v.scalar_tensor_tensor, v.tensor_reduce
            n = [0]

            def mark(ins_):
                n[0] += 1
                ins_.then_inc(s_dve, 1)

            def link(ins_):
                mark(ins_)
                dve.wait_ge(s_dve, n[0])

            dve.wait_ge(id_ready, 1)
            dve.wait_ge(s_pool, POOL_SETUP)
            link(v.tensor_copy(identb[:, :], ident[:, :]))
            dve.wait_ge(w_in, 16 * (LOADS_SP + LOADS_ACT))
            for raw_, q_, tmp in ((sraw[:, :], sq[:, :], stmp[:, :]),
                                  (sraw8[:, :, :], sq8[:, :, :], stmp8[:, :, :])):
                link(ts(q_, raw_, 0.3, None, ALU.is_gt))
                link(ts(tmp, raw_, -0.3, None, ALU.is_lt))
                link(tt(q_, q_, tmp, ALU.subtract))
                link(tt(q_, q_, raw_, ALU.subtract))
                link(tt(q_, raw_, q_, ALU.add))
            for j in range(1, TPC):
                link(tt(sq8[:, 0, :], sq8[:, 0, :], sq8[:, j, :], ALU.add))
            link(ts(sq8[:, 1, :], sq8[:, 0, :], 0.0, None, ALU.is_gt))
            link(ts(sq8[:, 2, :], sq8[:, 0, :], 0.0, None, ALU.is_lt))
            link(tt(sq8[:, 0, :], sq8[:, 1, :], sq8[:, 2, :], ALU.subtract))
            assert n[0] == SIG_READY, n
            dve.wait_ge(s_act, 1)
            link(ts(c_exp[:, :], c_exp[:, :], 1.0, None, ALU.add))
            link(v.reciprocal(c_exp[:, :], c_exp[:, :]))
            link(tt(c_sb[:, :], c_sb[:, :], c_exp[:, :], ALU.mult))
            assert n[0] == SILU_READY, n
            dve.wait_ge(s_pe, 5)
            link(v.tensor_copy(c_T[:, :, :].rearrange("p c b -> p (c b)"), banks[5][:, 0:KC * B]))
            assert n[0] == CT_READY, n
            dve.wait_ge(s_pe, 9)
            g = mod[:, 0:2, :].rearrange("b a d -> b (a d)")
            r = rows[:, 0:2, :].rearrange("b a d -> b (a d)")
            link(v.tensor_copy(g, banks[5][0:B, :]))
            link(stt(out=r, in0=g, scalar=-1.0, in1=g, op0=ALU.mult, op1=ALU.max))
            link(ts(g, g, 0.0, None, ALU.is_ge))
            link(ts(g, g, 2.0, -1.0, ALU.mult, ALU.add))
            link(stt(out=r, in0=r, scalar=GATE_MIN, in1=g, op0=ALU.max, op1=ALU.mult))
            link(tt(rows[:, 2, :], rows[:, 1, :], beta_r[:, :], ALU.mult))
            link(tt(rows[:, 1, :], rows[:, 1, :], gamma_r[:, :], ALU.mult))
            assert n[0] == ROWS_READY, n
            flat = lambda a: a[:, :, :].rearrange("p c d -> p (c d)")
            dve.wait_ge(s_pe, 9)
            link(v.tensor_copy(flat(a_hi), banks[0][:, :]))
            mark(tt(flat(a_lo), banks[0][:, :], flat(a_hi).bitcast(F32), ALU.subtract))
            bank2 = banks[2][:, :].rearrange("p (c d) -> p c d", c=KC)
            mark(v.tensor_copy(m_hi[:, :, 0:D], bank2))
            link(v.tensor_copy(m_hi[:, :, D:VW], steps[:, 0:1].unsqueeze(1).broadcast_to([P, KC, 2])))
            mark(tt(m_lo[:, :, 0:D], bank2, m_hi[:, :, 0:D].bitcast(F32), ALU.subtract))
            mark(v.tensor_copy(m_lo[:, :, D:VW], steps[:, 0:1].unsqueeze(1).broadcast_to([P, KC, 2])))
            tcol = comp[:, 0:KC, 0]
            link(ts(tcol, banks[3][:, 0:KC], SCALE, None, ALU.mult))
            link(v.tensor_copy(m_hi[:, :, D], tcol))
            link(tt(m_lo[:, :, D], tcol, m_hi[:, :, D].bitcast(F32), ALU.subtract))
            mark(v.tensor_copy(g_bias[:, :], banks[3][:, KC:2 * KC]))
            mark(tt(vb2[:, 0:D], banks[4][0:2, 0:D], bo2[:, :], ALU.add))
            link(ts(vb2[:, D:D + 1], banks[4][0:2, D:D + 1], SCALE, None, ALU.mult))
            link(v.tensor_copy(vb2_hi[:, :], vb2[:, :]))
            link(tt(vb2_lo[:, :], vb2[:, :], vb2_hi[:, :].bitcast(F32), ALU.subtract))
            link(ts(vb2_lo[:, :], vb2_lo[:, :], ident[0:2, 1:2], None, ALU.mult))
            link(stt(out=vbias[:, :], in0=vb2_hi[:, :].bitcast(F32), scalar=ident[0:2, 0:1], in1=vb2_lo[:, :],
                     op0=ALU.mult, op1=ALU.add))
            mark(ts(ones2[:, :], ident[0:2, :], 0.0, 1.0, ALU.mult, ALU.add))
            for i, (dst, add) in enumerate(((sa_col, 0.0), (ca_col, 1.0), (sb_col, 0.0), (cb_col, 1.0))):
                mark(ts(flat(dst), banks[6][:, i * KC * B:(i + 1) * KC * B], add, None, ALU.add))
            link(v.tensor_copy(f_full[:, :, 0:NCL + NTILES],
                               banks[7][:, 0:KC * FW].rearrange("p (c f) -> p c f", c=KC)[:, :, 0:NCL + NTILES]))
            link(v.tensor_copy(flat(f_hi), flat(f_full)))
            mark(tt(flat(f_lo), flat(f_full), flat(f_hi).bitcast(F32), ALU.subtract))
            lo = slice(NTILES, P)
            link(v.tensor_copy(table[:, :], t_full[:, :]))
            link(tt(t_full[lo, :], t_full[lo, :], table[lo, :].bitcast(F32), ALU.subtract))
            link(v.tensor_copy(table[lo, :], t_full[lo, :]))
            mark(tt(knot_step[:, :], knots[:, 1:K], knots[:, 0:K - 1], ALU.subtract))
            link(ts(inv_temp[:, :], inv_temp[:, :], TEMP_EPS, None, ALU.add))
            link(v.reciprocal(inv_temp[:, :], inv_temp[:, :]))
            assert n[0] == DVE_SETUP, n

            def variance(chain, st, sums, dif, var, signal):
                chain.mark(tt(sums, st[:, :, 1], st[:, :, 4], ALU.add))
                chain.mark(tt(var, st[:, :, 2], st[:, :, 5], ALU.add))
                chain.link(dve, tt(dif, st[:, :, 1], st[:, :, 4], ALU.subtract))
                chain.mark(tt(dif, dif, dif, ALU.mult))
                chain.link(dve, ts(var, var, 1.0 / D, EPS, ALU.mult, ALU.add))
                stt(out=var, in0=dif, scalar=0.25, in1=var, op0=ALU.mult, op1=ALU.add).then_inc(signal, 1)

            def newton(chain, var, guess, tmp, rstd, nmr, sums, signal):
                chain.link(dve, tt(tmp, guess, guess, ALU.mult))
                chain.link(dve, stt(out=tmp, in0=tmp, scalar=-0.5, in1=var, op0=ALU.mult, op1=ALU.mult))
                chain.link(dve, stt(out=rstd, in0=tmp, scalar=1.5, in1=guess, op0=ALU.add, op1=ALU.mult))
                stt(out=nmr, in0=sums, scalar=-0.5, in1=rstd, op0=ALU.mult, op1=ALU.mult).then_inc(signal, 1)

            @step
            def a_stats(p, s, t):
                dve_a.at(seq(p, s))
                if t == 0:
                    dve.wait_ge(x_ld[s], 16 * (p + 1))
                dve_a.mark(v.bn_stats(st1[:, t, :], x_sb[s][:, t, :]))

            @step
            def a_var(p, s):
                dve_a.at(seq(p, s))
                dve_a.wait(dve)
                variance(dve_a, st1, sum1[:, :], dif1[:, :], var1[:, :], ln1_var)

            @step
            def a_norm(p, s):
                dve_a.at(seq(p, s))
                dve.wait_ge(ln1_guess, seq(p, s) + 1)
                need(dve, xhat_ready, NT * seq(p, s))
                newton(dve_a, var1[:, :], guess1[:, :], newt1[:, :], rstd1[:, :], nmr1[:, :], sum1[:, :], ln1_ready)

            @step
            def a_split(p, s, c):
                b = seq(p, s)
                need(dve, scores_done, NT * (b - 1))
                dve.wait_ge(h_ready, KC * b + c + 1)
                v.tensor_copy(h_hi[s][:, c, :], h_full[:, c, :]).then_inc(h_hi_rdy, 1)

            @step
            def b_split(p, s, c):
                dve.wait_ge(g_hi_rdy, KC * seq(p, s) + c + 1)
                stt(out=g_lo[:, c, :], in0=mix_ps[MIX[f"G{s}{c}"]][:, :], scalar=g_bias[:, c:c + 1],
                    in1=g_hi[:, c, :].bitcast(F32), op0=ALU.add, op1=ALU.subtract).then_inc(g_lo_rdy, 1)

            @step
            def b_max(p, s, t):
                dve.wait_ge(masked, NT * seq(p, s) + t + 1)
                red(negmax[:, t:t + 1], absc[t % 2][:, 0:(t + 1) * P], X, ALU.max, negate=True).then_inc(rowmax, 1)

            @step
            def b_gate(p, s, t):
                b = seq(p, s)
                dve_b.at(b)
                if t == 0:
                    dve.wait_ge(ga_ld[s], 16 * (p + 1))
                dve.wait_ge(probs_rdy, NT * b + t + 1)
                dve_b.mark(v.reciprocal(rinv[:, t:t + 1], rowsum[s][:, t:t + 1]))
                dve.wait_ge(pv_done, NT * b + t + 1)
                need(dve, x2_rdy, NT * b + t - 1)
                dve_b.wait(dve)
                stt(out=gated[t % 2][:, :], in0=attn_ps[:, 0:D], scalar=rinv[:, t:t + 1],
                    in1=ga_row[s][:, :], op0=ALU.mult, op1=ALU.mult).then_inc(gated_rdy, 1)

            @step
            def b_stats(p, s, t):
                dve.wait_ge(x2_rdy, NT * seq(p, s) + t + 1)
                v.bn_stats(st2[:, NT * s + t, :], x2[s][:, t, :]).then_inc(st2_rdy, 1)

            @step
            def c_var(p):
                dve_ln2.at(p)
                dve.wait_ge(st2_rdy, PT * (p + 1))
                variance(dve_ln2, st2, sum2[:, :], dif2[:, :], var2[:, :], ln2_var)

            @step
            def c_norm(p):
                dve_ln2.at(p)
                dve.wait_ge(ln2_guess, p + 1)
                need(dve, xhat2_rdy, PT * p)
                newton(dve_ln2, var2[:, :], guess2[:, :], newt2[:, :], rstd2[:, :], nmr2[:, :], sum2[:, :], ln2_ready)

            @step
            def c_split(p, u):
                s, m = u // KC, u % KC
                dve.wait_ge(h2_rdy, 2 * KC * p + u + 1)
                need(dve, fs_done, 3 * p)
                v.tensor_copy(h2_hi[:, s, m, :], h2_full[:, s, m, :]).then_inc(h2_hi_rdy, 1)

            @step
            def c_z(p):
                dve.wait_ge(fs_rdy, 3 * (p + 1))
                ts_z(z_cl[:, :].rearrange("p (t j) -> p t j", t=PT), fs[:, :, 0:NCL]).then_inc(zc_rdy, 1)

            @step
            def c_hidden(p):
                dve.wait_ge(fs_rdy, 3 * (p + 1))
                tt(hid[:, :, :], fs[:, :, NCL + NTILES:FW], b1_row[:, :].unsqueeze(1).broadcast_to([P, PT, H]),
                   ALU.add).then_inc(pregelu, 1)

            def ts_z(dst, src):
                return ts(dst, src, inv_temp[:, 0:1], Z_MIN, ALU.mult, ALU.max)

            def link_c(ins_):
                dve_route.link(dve, ins_)

            K1 = K - 1
            row7 = lambda a: a.unsqueeze(1).broadcast_to([P, E8, K1])
            col7 = lambda a: a.unsqueeze(2).broadcast_to([P, E8, K1])
            ix, fl, vl, vd, gates = (a[:, :] for a in cal)

            def knot_below(e):
                link_c(ts(e, e, 1.0, None, ALU.add))
                link_c(v.reciprocal(ix, e))
                link_c(ts(ix, ix, float(K1), None, ALU.mult))
                m6 = cal7[0][:, :, 0:K1 - 1]
                link_c(tt(m6, ix.unsqueeze(2).broadcast_to([P, E8, K1 - 1]),
                          steps[:, 1:K1].unsqueeze(1).broadcast_to([P, E8, K1 - 1]), ALU.is_ge))
                link_c(red(fl, m6, X, ALU.add))

            def knot_values():
                link_c(tt(cal7[0][:, :, :], col7(fl), row7(steps[:, 0:K1]), ALU.is_equal))
                link_c(tt(cal7[1][:, :, :], cal7[0][:, :, :], row7(knots[:, 0:K1]), ALU.mult))
                link_c(red(vl, cal7[1][:, :, :], X, ALU.add))
                link_c(tt(cal7[1][:, :, :], cal7[0][:, :, :], row7(knot_step[:, :]), ALU.mult))
                link_c(red(vd, cal7[1][:, :, :], X, ALU.add))

            def first_best(onehot_):
                link_c(tt(ix, ix, fl, ALU.subtract))
                link_c(tt(ix, ix, vd, ALU.mult))
                link_c(tt(gates, vl, ix, ALU.add))
                gate = gates.rearrange("p (t j) -> p t j", t=PT)
                rank = cal[0][:, :].rearrange("p (t j) -> p t j", t=PT)
                spread = best[:, :].unsqueeze(2).broadcast_to([P, PT, TPC])
                link_c(red(best[:, :], gate, X, ALU.max))
                link_c(tt(rank, gate, spread, ALU.is_equal))
                link_c(tt(rank, rank, falling[:, :].unsqueeze(1).broadcast_to([P, PT, TPC]), ALU.mult))
                link_c(red(best[:, :], rank, X, ALU.max))
                link_c(tt(onehot_, rank, spread, ALU.is_equal))

            @step
            def c_below(p, local):
                dve_route.at(p)
                dve.wait_ge(el_rdy if local else ec_rdy, p + 1)
                knot_below(z_lo[:, :] if local else z_cl[:, :])

            @step
            def c_knots(p, local):
                dve_route.at(p)
                knot_values()

            @step
            def c_best(p, local):
                dve_route.at(p)
                first_best(oh_lo[:, :, :] if local else oh_cl[:, :, :])

            @step
            def c_pick(p):
                dve_route.at(p)
                pick = picked[:, :, :].rearrange("p t (c j) -> p t c j", c=NCL)
                for q in range(2):
                    tiles = slice(NT * q, NT * (q + 1))
                    dve_route.mark(tt(pick[:, tiles], fs[:, tiles, NCL:NCL + NTILES].rearrange("p t (c j) -> p t c j", c=NCL),
                                      oh_cl[:, tiles, :].unsqueeze(3).broadcast_to([P, NT, NCL, TPC]), ALU.mult))
                dve_route.wait(dve)
                zl = z_lo[:, :].rearrange("p (t j) -> p t j", t=PT)
                link_c(red(zl, pick.rearrange("p t c j -> p t j c"), X, ALU.add))
                ts_z(zl, zl).then_inc(zl_rdy, 1)

            @step
            def c_onehot(p):
                dve_route.at(p)
                need(dve, oht_done, 2 * p)
                for q in range(PT):
                    dve_route.mark(tt(onehot[:, q, 0:NTILES].rearrange("p (c j) -> p c j", c=NCL),
                                      oh_cl[:, q, :].unsqueeze(2).broadcast_to([P, NCL, TPC]),
                                      oh_lo[:, q, :].unsqueeze(1).broadcast_to([P, NCL, TPC]), ALU.mult))
                dve_route.wait(dve)
                v.tensor_copy(onehot[:, :, NTILES:P], onehot[:, :, 0:NTILES]).then_inc(onehot_rdy, 1)

            @step
            def c_comp(p):
                dve_comp.at(p)
                dve.wait_ge(gelu_rdy, p + 1)
                for o in range(NCOMP):
                    dve_comp.mark(tt(w2prod[:, :, o, :], hid[:, :, :],
                                     w2_rows[:, :, o].unsqueeze(1).broadcast_to([P, PT, H]), ALU.mult))
                dve_comp.wait(dve)
                need(dve, tanh_rdy, p)
                dve_comp.link(dve, red(cmp_t[:, :, :], w2prod[:, :, :, :], X, ALU.add))
                tt(cmp_t[:, :, :], cmp_t[:, :, :], b2_row[:, :].unsqueeze(1).broadcast_to([P, PT, NCOMP]),
                   ALU.add).then_inc(pretanh, 1)

            @step
            def c_spline(p):
                G = GRID
                dve_spline.at(p)
                dve.wait_ge(tanh_rdy, p + 1)
                dve.wait_ge(gath_rdy, PT * (p + 1))
                cb = lambda i: comp[:, :, i:i + 1].broadcast_to([P, PT, G])
                link_s = lambda ins_: dve_spline.link(dve, ins_)
                dve_spline.mark(tt(sp0[:, :, :], gath[:, :, 0:G], cb(0), ALU.mult))
                link_s(tt(sp1[:, :, :], gath[:, :, G:2 * G], cb(1), ALU.mult))
                link_s(tt(sp0[:, :, :], sp0[:, :, :], sp1[:, :, :], ALU.add))
                link_s(tt(sp0[:, :, :], sp0[:, :, :], gath[:, :, 2 * G:3 * G], ALU.add))
                link_s(stt(out=sp0[:, :, :], in0=sp0[:, :, :], scalar=0.0, in1=gath[:, :, 3 * G:4 * G],
                           op0=ALU.max, op1=ALU.mult))
                link_s(red(mag[:, :], sp0[:, :, :], X, ALU.add))
                link_s(tt(mag[:, :], mag[:, :], gath[:, :, 4 * G], ALU.add))
                link_s(ts(mag[:, :], mag[:, :], out_scale[:, 0:1], None, ALU.mult))

            @step
            def c_y(p, t):
                dve.wait_ge(h2_tok_rdy, NT * p + t // 2 + 1)
                need(dve, res_rdy, 2 * (p - 1) + t // NT + 1)
                stt(out=y[:, t, :], in0=gath[:, t, PAR:GW], scalar=mag[:, t:t + 1], in1=h2_tok[:, t, :],
                    op0=ALU.mult, op1=ALU.add).then_inc(y_sem, 1)

            @step
            def c_stats(p, t):
                dve_ln3.at(p)
                dve.wait_ge(y_sem, PT * p + t + 1)
                dve_ln3.mark(v.bn_stats(st3[:, t, :], y[:, t, :]))

            @step
            def c_var3(p):
                dve_ln3.at(p)
                dve_ln3.wait(dve)
                variance(dve_ln3, st3, sum3[:, :], dif3[:, :], var3[:, :], ln3_var)

            @step
            def c_norm3(p):
                dve_ln3.at(p)
                dve.wait_ge(ln3_guess, p + 1)
                need(dve, yhat_rdy, PT * p)
                newton(dve_ln3, var3[:, :], guess3[:, :], newt3[:, :], rstd3[:, :], nmr3[:, :], sum3[:, :], ln3_ready)

            def superstep(k):
                c_z(k - 3)
                c_hidden(k - 3)
                c_below(k - 3, local=False)
                b_max(k - 2, 0, 0)
                c_knots(k - 3, local=False)
                a_split(k - 2, 1, 0)
                c_best(k - 3, local=False)
                a_split(k - 2, 1, 1)
                b_max(k - 2, 0, 1)
                c_pick(k - 3)
                b_gate(k - 2, 0, 0)
                b_max(k - 2, 0, 2)
                b_max(k - 2, 0, 3)
                c_below(k - 3, local=True)
                b_split(k - 2, 1, 0)
                b_split(k - 2, 1, 1)
                b_gate(k - 2, 0, 1)
                c_knots(k - 3, local=True)
                b_max(k - 2, 1, 0)
                b_gate(k - 2, 0, 2)
                c_best(k - 3, local=True)
                b_max(k - 2, 1, 1)
                b_gate(k - 2, 0, 3)
                c_onehot(k - 3)
                b_gate(k - 2, 1, 0)
                b_max(k - 2, 1, 2)
                c_comp(k - 3)
                b_max(k - 2, 1, 3)
                b_gate(k - 2, 1, 1)
                a_stats(k - 1, 0, 0)
                a_stats(k - 1, 0, 1)
                a_stats(k - 1, 0, 2)
                a_stats(k - 1, 0, 3)
                a_var(k - 1, 0)
                b_gate(k - 2, 1, 2)
                a_norm(k - 1, 0)
                b_stats(k - 2, 0, 0)
                b_stats(k - 2, 0, 1)
                b_stats(k - 2, 0, 2)
                b_stats(k - 2, 0, 3)
                b_gate(k - 2, 1, 3)
                b_stats(k - 2, 1, 0)
                b_stats(k - 2, 1, 1)
                b_stats(k - 2, 1, 2)
                b_stats(k - 2, 1, 3)
                c_var(k - 2)
                a_split(k - 1, 0, 0)
                c_norm(k - 2)
                c_spline(k - 3)
                a_split(k - 1, 0, 1)
                c_y(k - 3, 0)
                a_stats(k - 1, 1, 0)
                c_y(k - 3, 1)
                a_stats(k - 1, 1, 1)
                c_stats(k - 3, 0)
                a_stats(k - 1, 1, 2)
                c_y(k - 3, 2)
                c_split(k - 2, 0)
                a_stats(k - 1, 1, 3)
                c_y(k - 3, 3)
                c_split(k - 2, 1)
                b_split(k - 1, 0, 0)
                c_split(k - 2, 2)
                c_y(k - 3, 4)
                c_y(k - 3, 5)
                c_stats(k - 3, 1)
                a_var(k - 1, 1)
                c_split(k - 2, 3)
                c_y(k - 3, 6)
                c_stats(k - 3, 2)
                c_stats(k - 3, 3)
                c_stats(k - 3, 4)
                c_stats(k - 3, 5)
                c_y(k - 3, 7)
                c_stats(k - 3, 6)
                c_stats(k - 3, 7)
                a_norm(k - 1, 1)
                c_var3(k - 3)
                b_split(k - 1, 0, 1)
                c_norm3(k - 3)

            pipeline(dve, superstep)


_INS = ['L0_attn_x', 'L0_attn_Wq', 'L0_attn_bq', 'L0_attn_Wk', 'L0_attn_bk', 'L0_attn_Wv', 'L0_attn_bv', 'L0_attn_Wo',
        'L0_attn_bo', 'L0_ffn_signatures_raw', 'L0_ffn_knot_values', 'L0_ffn_temperature', 'L0_ffn_compress_w1',
        'L0_ffn_compress_b1', 'L0_ffn_compress_w2', 'L0_ffn_compress_b2', 'L0_ffn_spline_w1', 'L0_ffn_spline_b1',
        'L0_ffn_spline_w2', 'L0_ffn_spline_b2', 'L0_ffn_directions', 'L0_ffn_norm_gamma', 'L0_ffn_norm_beta',
        'L0_ffn_output_scale', 'L0_c', 'L0_wmod']


def kernel(**inputs):
    import numpy as np
    import concourse.bacc as bacc
    from concourse.bass_utils import run_bass_kernel_spmd

    nc = bacc.Bacc("TRN2", target_bir_lowering=False, num_devices=1)
    arrays, args = {}, {}
    for name in _INS:
        a = np.ascontiguousarray(inputs[name])
        arrays[f"in_{name}"] = a
        args[name] = nc.dram_tensor(f"in_{name}", a.shape, mybir.dt.from_np(a.dtype), kind="ExternalInput").ap()
    shape = arrays["in_L0_attn_x"].shape
    out = nc.dram_tensor("out", shape, F32, kind="ExternalOutput").ap()
    adaln_kernel(nc, args, out)
    r = run_bass_kernel_spmd(nc, [arrays], core_ids=[0])
    return r.results[0]["out"]
```

```python
from contextlib import ExitStack

import concourse.bass as bass
from concourse import mybir

F32 = mybir.dt.float32
F32R = mybir.dt.float32r
BF16 = mybir.dt.bfloat16
ALU = mybir.AluOpType
ACT = mybir.ActivationFunctionType
X = mybir.AxisListType.X

P = 128
EPS = 1e-5
TEMP_EPS = 1e-6
Z_MIN = -88.0
MASKED = -1e30
GATE_MIN = 0.25


SILU_READY, CT_READY, ROWS_READY, COLUMNS_READY, DVE_SETUP = 4, 5, 31, 37, 60
WOT_READY = 2
LOADS_REST = 19
POOL_SETUP = 4


class Chain:

    def __init__(self, sem, per):
        self.sem, self.per, self.n, self.i = sem, per, 0, 0

    def at(self, i):
        self.i = i

    def mark(self, ins):
        self.n = self.n % self.per + 1
        ins.then_inc(self.sem, 1)

    def wait(self, eng):
        eng.wait_ge(self.sem, self.per * self.i + self.n)

    def link(self, eng, ins):
        self.mark(ins)
        self.wait(eng)


def need(eng, sem, count):
    if isinstance(count, int) and count <= 0:
        return
    eng.wait_ge(sem, count)


def adaln_kernel(nc, ins, out):
    x_in, wq_in, wo_in = ins["L0_attn_x"], ins["L0_attn_Wq"], ins["L0_attn_Wo"]
    B, S, D = x_in.shape
    NT = S // P
    KC = D // P
    PAIRS = B // 2
    LAG = 3
    PT = 2 * NT
    NTILES = ins["L0_ffn_signatures_raw"].shape[0]
    K = ins["L0_ffn_knot_values"].shape[0]
    H = ins["L0_ffn_compress_w1"].shape[1]
    GRID = ins["L0_ffn_spline_b1"].shape[1]
    TPC = 8
    NCL = NTILES // TPC
    NCOMP = ins["L0_ffn_compress_w2"].shape[1]
    VW = D + 2
    FW = NCL + NTILES + H
    PAR = NCOMP * GRID + 2 * GRID + 2
    GW = PAR + D
    SCALE = float(D) ** -0.5
    assert NT == 4 and KC == 2 and NCL == 8 and 2 * NTILES == P and SCALE == 0.0625

    gate_rows = nc.dram_tensor("gate_rows", (B, 3 * D), F32, kind="Internal").ap()

    with ExitStack() as ctx:
        def sb(name, shape, dt=F32):
            return ctx.enter_context(nc.sbuf_tensor(name, shape, dt))

        def sem(name):
            return ctx.enter_context(nc.semaphore(name))

        banks = [ctx.enter_context(nc.psum_tensor(f"bank{i}", [P, 512], F32)) for i in range(8)]
        turn_ps = banks[0:2]
        mix_ps = banks[2:5]
        score_ps = banks[5:7]
        attn_ps = banks[7]
        turn_order = """H2T2 H2T3 XT10 XT11 PT00 PT01 PT02 PT03 PT10 PT11 PT12 OHT0 OHT1 PT13 XT00 XT01 H2T0 H2T1""".split()
        mix_order = """V00 G00 G01 FS0 FS1 FS2 V01 V02 V03 BT0 G10 G11 V10 V11 V12 V13 BT1 BT2 BT3 GA0 GA1 GA2 GA3 GA4 GA5
                        GA6 GA7""".split()
        TURN = {name: i % 2 for i, name in enumerate(turn_order)}
        MIX = {name: i % 3 for i, name in enumerate(mix_order)}

        ident = sb("ident", [P, P])
        identb = sb("identb", [P, P], BF16)
        causal = sb("causal", [P, P])
        ones2 = sb("ones2", [2, P], F32R)
        a_hi = sb("a_hi", [P, KC, D], F32R)
        a_lo = sb("a_lo", [P, KC, D], F32R)
        m_hi = sb("m_hi", [P, KC, VW], F32R)
        m_lo = sb("m_lo", [P, KC, VW], F32R)
        vbias = sb("vbias", [2, VW], F32R)
        g_bias = sb("g_bias", [P, KC])
        f_hi = sb("f_hi", [P, KC, FW], F32R)
        f_lo = sb("f_lo", [P, KC, FW], F32R)
        table = sb("table", [P, GW], F32R)
        sa_col = sb("sa_col", [P, KC, B])
        ca_col = sb("ca_col", [P, KC, B])
        sa_col2 = sb("sa_col2", [P, KC, B])
        ca_col2 = sb("ca_col2", [P, KC, B])
        sb_col = sb("sb_col", [P, KC, B])
        cb_col = sb("cb_col", [P, KC, B])
        b1_row = sb("b1_row", [P, H])
        w2_rows = sb("w2_rows", [P, H, NCOMP])
        b2_row = sb("b2_row", [P, NCOMP])
        knots = sb("knots", [P, K])
        knot_step = sb("knot_step", [P, K - 1])
        inv_temp = sb("inv_temp", [P, 1])
        out_scale = sb("out_scale", [P, 1])
        steps = sb("steps", [P, K])
        falling = sb("falling", [P, TPC])

        x_sb = [sb(f"x{s}", [P, NT, D]) for s in range(2)]
        st1 = sb("st1", [P, NT, 6])
        sum1, dif1, var1, guess1, newt1, rstd1, nmr1 = (
            sb(n, [P, NT]) for n in ("sum1", "dif1", "var1", "guess1", "newt1", "rstd1", "nmr1"))
        xhat = sb("xhat", [P, NT, D])
        h_full = sb("h_full", [P, KC, S])
        h_hi = [sb(f"h_hi{s}", [P, KC, S], F32R) for s in range(2)]
        h_lo = [sb(f"h_lo{s}", [P, KC, S], F32R) for s in range(2)]
        ga_row = [sb(f"ga_row{s}", [P, D]) for s in range(2)]
        g_hi = sb("g_hi", [P, KC, S], F32R)
        g_lo = sb("g_lo", [P, KC, S], F32R)
        v_sb = [sb(f"v{s}", [P, NT, VW]) for s in range(2)]
        absc = [sb(f"absc{t}", [P, (t + 1) * P]) for t in range(NT)]
        probs = [sb(f"probs{t}", [P, (t + 1) * P]) for t in range(NT)]
        probsT = [sb(f"probsT{t}", [P, (t + 1) * P]) for t in range(NT)]
        negmax = sb("negmax", [P, NT])
        rowsum = [sb(f"rowsum{s}", [P, NT]) for s in range(2)]
        rinv = sb("rinv", [P, NT])
        gated = [sb(f"gated{j}", [P, D]) for j in range(2)]
        x2 = [sb(f"x2_{s}", [P, NT, D]) for s in range(2)]
        st2 = sb("st2", [P, PT, 6])
        gb_row = [sb(f"gb_row{s}", [P, 2, D]) for s in range(2)]
        sum2, dif2, var2, guess2, newt2, rstd2, nmr2 = (
            sb(n, [P, PT]) for n in ("sum2", "dif2", "var2", "guess2", "newt2", "rstd2", "nmr2"))
        wide = sb("wide", [P, 4 * KC * S])
        xhat2 = wide[:, 0:PT * D].rearrange("p (t d) -> p t d", t=PT)
        h2_full = wide[:, PT * D:].rearrange("p (s c t) -> p s c t", s=2, c=KC)
        h2_hi = sb("h2_hi", [P, 2, KC, S], F32R)
        h2_lo = sb("h2_lo", [P, 2, KC, S], F32R)
        h2_tok = sb("h2_tok", [P, PT, D])
        fs = sb("fs", [P, PT, FW])
        hid = sb("hid", [P, PT, H])
        w2prod = sb("w2prod", [P, PT, NCOMP, H])
        comp = sb("comp", [P, PT, NCOMP])
        cmp_t = sb("cmp_t", [P, PT, NCOMP])
        E8 = PT * TPC
        z_cl = sb("z_cl", [P, E8])
        z_lo = sb("z_lo", [P, E8])
        cal = [sb(f"cal{j}", [P, E8]) for j in range(5)]
        cal7 = [sb(f"cal7_{j}", [P, E8, K - 1]) for j in range(3)]
        best = sb("best", [P, PT])
        oh_cl = sb("oh_cl", [P, PT, NCL])
        oh_lo = sb("oh_lo", [P, PT, TPC])
        picked = sb("picked", [P, PT, NTILES])
        onehot = sb("onehot", [P, PT, P], BF16)
        onehotT = sb("onehotT", [P, PT * P], F32R)
        gath = sb("gath", [P, PT, GW])
        sp0 = sb("sp0", [P, PT, GRID])
        sp1 = sb("sp1", [P, PT, GRID])
        mag = sb("mag", [P, PT])
        y = sb("y", [P, PT, D])
        st3 = sb("st3", [P, PT, 6])
        sum3, dif3, var3, guess3, newt3, rstd3, nmr3 = (
            sb(n, [P, PT]) for n in ("sum3", "dif3", "var3", "guess3", "newt3", "rstd3", "nmr3"))
        res = sb("res", [P, PT, D])

        in_c, in_mod, in_sig, in_qk, in_ov, in_bias, in_rest = (
            sem(f"loaded_{n}") for n in ("c", "mod", "signatures", "q_k", "o_v", "biases", "rest"))
        x_ld = [sem(f"x_loaded{s}") for s in range(2)]
        ga_ld = [sem(f"ga_loaded{s}") for s in range(2)]
        gb_ld = [sem(f"gb_loaded{s}") for s in range(2)]
        sent = [sem(f"out_sent{s}") for s in range(2)]
        rows_sent = sem("rows_sent")
        id_ready = sem("ident_ready")
        s_pe, s_dve, s_act, s_pool = sem("setup_pe"), sem("setup_dve"), sem("setup_act"), sem("setup_pool")
        ln1_var, ln1_guess, ln1_ready = sem("ln1_var"), sem("ln1_guess"), sem("ln1_ready")
        xhat_ready = sem("xhat_ready")
        xt_done = sem("xhat_turned")
        h_ready = sem("h_ready")
        h_hi_rdy = sem("h_hi_ready")
        h_lo_rdy = sem("h_lo_ready")
        g_done = sem("g_done")
        g_hi_rdy, g_lo_rdy = sem("g_hi_ready"), sem("g_lo_ready")
        vproj_done = sem("v_done")
        v_ready = sem("v_ready")
        scores_done = sem("scores_done")
        absc_ready = sem("abs_scores_ready")
        masked = sem("diag_masked")
        rowmax = sem("rowmax_ready")
        probs_rdy = sem("probs_ready")
        pt_done = sem("probs_turned")
        pt_rdy = sem("probsT_ready")
        pv_done = sem("pv_done")
        st2_rdy = sem("x2_stats_ready")
        gated_rdy = sem("gated_ready")
        x2_rdy = sem("x2_ready")
        ln2_var = sem("ln2_var")
        ln2_guess, ln2_ready = sem("ln2_guess"), sem("ln2_ready")
        xhat2_rdy = sem("xhat2_ready")
        h2t_done = sem("xhat2_turned")
        h2_rdy = sem("h2_ready")
        h2_hi_rdy, h2_lo_rdy = sem("h2_hi_ready"), sem("h2_lo_ready")
        fs_done = sem("ffn_scores_done")
        fs_rdy = sem("ffn_scores_ready")
        bt_done = sem("h2_turned_back")
        h2_tok_rdy = sem("h2_tok_ready")
        zc_rdy, ec_rdy = sem("cluster_z_ready"), sem("cluster_exp_ready")
        zl_rdy, el_rdy = sem("local_z_ready"), sem("local_exp_ready")
        knot_sel, knot_prod = sem("knot_selected"), sem("knot_products")
        w2_prod = sem("w2_products")
        pregelu, gelu_rdy = sem("pregelu_ready"), sem("gelu_ready")
        pretanh, tanh_rdy = sem("pretanh_ready"), sem("tanh_ready")
        onehot_rdy = sem("onehot_ready")
        oht_done = sem("onehot_turned")
        oht_rdy = sem("onehotT_ready")
        ga_done = sem("gather_done")
        gath_rdy = sem("gathered_ready")
        ln3_var, ln3_guess, ln3_ready = sem("ln3_var"), sem("ln3_guess"), sem("ln3_ready")
        yhat_rdy = sem("yhat_ready")
        base_rdy = sem("base_ready")
        scaled = sem("scaled_yhat")
        res_rdy = sem("result_ready")
        y_sem = sem("y_ready")
        act_guess1 = Chain(sem("act_chain_a"), 1)
        act_guess2 = Chain(sem("act_chain_ln2"), 1)
        act_guess3 = Chain(sem("act_chain_ln3"), 1)
        dve_a = Chain(sem("dve_chain_a"), NT + 5 + 3)
        dve_b = Chain(sem("dve_chain_b"), NT)
        dve_ln2 = Chain(sem("dve_chain_ln2"), 5 + 3)
        dve_route = Chain(sem("dve_chain_route"), 2 * 16 + 3 + 2)
        dve_comp = Chain(sem("dve_chain_comp"), 1)
        dve_spline = Chain(sem("dve_chain_spline"), 8)
        dve_ln3 = Chain(sem("dve_chain_ln3"), PT + 5 + 3)

        wq, wk, wv, wo = (res[:, KC * i:KC * (i + 1), :] for i in range(4))
        woT = sb("woT", [P, KC, D])
        wmod_sb = wide[:, 0:KC * 6 * D].rearrange("p (c n) -> p c n", c=KC)
        bq, bk, bv = (sb(n, [P, KC]) for n in ("bq", "bk", "bv"))
        bo2 = sb("bo2", [2, D])
        c_sb = sb("c_sb", [B, D])
        c_exp = sb("c_exp", [B, D])
        c_T = sb("c_T", [P, KC, B])
        mod = sb("mod", [B, 2, D])
        mod2 = y[0:B, 2:4, :].rearrange("b a d -> b (a d)")
        rows = sb("rows", [B, 3, D])
        gamma_r, beta_r = sb("gamma_r", [B, D]), sb("beta_r", [B, D])
        sraw = y[0:NTILES, 0, :]
        raw_T, sig_T, sig_tmp = (h2_tok[:, i, 0:KC * NTILES] for i in range(3))
        cl_sum = sb("cl_sum", [P, KC * NCL])
        cl_neg = sb("cl_neg", [P, KC * NCL])
        f_full = sb("f_full", [P, KC, FW])
        t_full = sb("t_full", [P, GW])
        vb2 = sb("vb2", [2, VW])
        vb2_hi, vb2_lo = sb("vb2_hi", [2, VW], F32R), sb("vb2_lo", [2, VW])

        block = ctx.enter_context(nc.Block())

        def seq(p, s):
            return 2 * p + s

        ahead = set()

        def step(f):
            def run(p, *rest, **named):
                if not isinstance(p, int) or 0 <= p < PAIRS and (f.__name__, p, rest) not in ahead:
                    f(p, *rest, **named)
            run.__name__ = f.__name__
            return run

        def run_ahead(run, *args):
            run(*args)
            ahead.add((run.__name__, args[0], args[1:]))

        def pipeline(eng, superstep):
            for k in range(LAG + 1):
                superstep(k)
            with eng.Fori(LAG + 1, PAIRS) as k:
                superstep(k)
            for k in range(PAIRS, PAIRS + LAG):
                superstep(k)

        @block.sync
        def _(sp):
            def col(a):
                return a.rearrange("(c p) -> p c", p=P)

            def row(a, n):
                return a.rearrange("(o d) -> o d", o=1).broadcast_to([n, a.shape[0]])

            def load(loaded, dst, src, **kw):
                sp.dma_start(dst, src, **kw).then_inc(loaded, 16)

            x_v = x_in.rearrange("b (t p) d -> b p t d", p=P)
            out_v = out.rearrange("b (t p) d -> b p t d", p=P)

            load(in_sig, sraw[:, :], ins["L0_ffn_signatures_raw"])
            for loaded, w, name in ((in_qk, wq, "Wq"), (in_qk, wk, "Wk"), (in_ov, wo, "Wo"), (in_ov, wv, "Wv")):
                load(loaded, w[:, :, :], ins[f"L0_attn_{name}"].rearrange("(c p) n -> p c n", p=P))
            sp.dma_start(x_sb[0][:, :, :], x_v[0]).then_inc(x_ld[0], 16)
            for w, name in ((bq, "bq"), (bk, "bk"), (bv, "bv")):
                load(in_bias, w[:, :], col(ins[f"L0_attn_{name}"]), allow_slow_non_contiguous=True)
            load(in_bias, bo2[:, :], row(ins["L0_attn_bo"], 2))
            sp.dma_start(x_sb[1][:, :, :], x_v[1]).then_inc(x_ld[1], 16)
            for dst, src in ((b1_row[:, :], row(ins["L0_ffn_compress_b1"], P)),
                             (w2_rows[:, :, :].rearrange("p h o -> p (h o)"),
                              ins["L0_ffn_compress_w2"].rearrange("(a h) o -> a (h o)", a=1).broadcast_to([P, H * NCOMP])),
                             (b2_row[:, :], row(ins["L0_ffn_compress_b2"], P)),
                             (knots[:, :], row(ins["L0_ffn_knot_values"], P)),
                             (inv_temp[:, :], row(ins["L0_ffn_temperature"], P)),
                             (out_scale[:, :], row(ins["L0_ffn_output_scale"], P))):
                load(in_rest, dst, src)

            sp.wait_ge(s_dve, ROWS_READY)
            sp.dma_start(gate_rows, rows[:, :, :].rearrange("b a d -> b (a d)")).then_inc(rows_sent, 16)
            sp.wait_ge(rows_sent, 16)

            def gate_row(i, a, n_rows):
                r = gate_rows[bass.ds(i, 1), a * D:(a + n_rows) * D]
                return r.broadcast_to([P, n_rows * D])

            def ga_load(p, s):
                sp.dma_start(ga_row[s][:, :], gate_row(seq(p, s), 0, 1)).then_inc(ga_ld[s], 16)

            ga_load(0, 0)
            ga_load(0, 1)

            @step
            def load_x(p, s):
                if isinstance(p, int) and p == 0:
                    return
                sp.wait_ge(x2_rdy, NT * seq(p - 1, s) + NT)
                sp.dma_start(x_sb[s][:, :, :], x_v[bass.ds(seq(p, s), 1)].rearrange("o p t d -> (o p) t d")
                             ).then_inc(x_ld[s], 16)
                ga_load(p, s)

            @step
            def load_gb(p, s):
                need(sp, res_rdy, NT * (p - 1) + 2 * (s + 1))
                sp.dma_start(gb_row[s][:, :, :].rearrange("p a d -> p (a d)"),
                             gate_row(seq(p, s), 1, 2)).then_inc(gb_ld[s], 16)

            @step
            def send(p, s):
                sp.wait_ge(res_rdy, NT * p + 2 * (s + 1))
                sp.dma_start(out_v[bass.ds(seq(p, s), 1)].rearrange("o p t d -> (o p) t d"),
                             res[:, NT * s:NT * (s + 1), :]).then_inc(sent[s], 16)

            def superstep(k):
                for i in range(0, 2):
                    load_x(k - 1, i)
                load_gb(k - 2, 0)
                for i in range(0, 2):
                    send(k - 3, i)
                load_gb(k - 2, 1)

            pipeline(sp, superstep)
            for s in range(2):
                sp.wait_ge(sent[s], 16 * PAIRS)

        @block.tensor
        def _(pe):
            mm, tr = nc.tensor.matmul, nc.tensor.transpose
            pe.wait_ge(id_ready, 1)
            pe.wait_ge(in_sig, 16)
            for c in range(KC):
                last = tr(banks[7][:, c * NTILES:(c + 1) * NTILES], sraw[:, c * P:(c + 1) * P], ident[0:NTILES, 0:NTILES])
            last.then_inc(s_pe, 1)
            pe.wait_ge(s_dve, SILU_READY)
            for c in range(KC):
                last = tr(banks[5][:, c * B:(c + 1) * B], c_sb[:, c * P:(c + 1) * P], ident[0:B, 0:B])
            last.then_inc(s_pe, 1)
            pe.wait_ge(in_qk, 32)
            for m in range(KC):
                for c in range(KC):
                    last = mm(banks[0][:, m * D:(m + 1) * D], wq[:, c, m * P:(m + 1) * P], wk[:, c, :],
                              start=(c == 0), stop=(c == KC - 1))
            last.then_inc(s_pe, 1)
            pe.wait_ge(in_ov, 32)
            for v in range(KC):
                for o in range(KC):
                    last = tr(banks[1][:, v * D + o * P:v * D + (o + 1) * P], wo[:, o, v * P:(v + 1) * P], ident[:, :])
            last.then_inc(s_pe, 1)
            pe.wait_ge(in_mod, 16)
            pe.wait_ge(s_dve, CT_READY)
            for i, j in enumerate((2, 5)):
                for c in range(KC):
                    last = mm(banks[5][0:B, i * D:(i + 1) * D], c_T[:, c, :], wmod_sb[:, c, j * D:(j + 1) * D],
                              start=(c == 0), stop=(c == KC - 1))
            last.then_inc(s_pe, 1)
            for i, j in enumerate((0, 1, 3, 4)):
                for m in range(KC):
                    o = (i * KC + m) * B
                    for c in range(KC):
                        last = mm(banks[6][:, o:o + B], wmod_sb[:, c, j * D + m * P:j * D + (m + 1) * P], c_T[:, c, :],
                                  start=(c == 0), stop=(c == KC - 1))
            last.then_inc(s_pe, 1)
            pe.wait_ge(in_bias, 64)
            for m in range(KC):
                for c in range(KC):
                    mm(banks[3][:, m:m + 1], wq[:, c, m * P:(m + 1) * P], bk[:, c:c + 1],
                       start=(c == 0), stop=(c == KC - 1))
                for c in range(KC):
                    last = mm(banks[3][:, KC + m:KC + m + 1], wk[:, c, m * P:(m + 1) * P], bq[:, c:c + 1],
                              start=(c == 0), stop=(c == KC - 1))
            last.then_inc(s_pe, 1)
            pe.wait_ge(s_act, WOT_READY)
            for m in range(KC):
                for v in range(KC):
                    last = mm(banks[2][:, m * D:(m + 1) * D], wv[:, v, m * P:(m + 1) * P], woT[:, v, :],
                              start=(v == 0), stop=(v == KC - 1))
            last.then_inc(s_pe, 1)
            for v in range(KC):
                mm(banks[4][0:2, 0:D], bv[:, v:v + 1].broadcast_to([P, 2]), woT[:, v, :],
                   start=(v == 0), stop=(v == KC - 1))
            for c in range(KC):
                last = mm(banks[4][0:2, D:D + 1], bq[:, c:c + 1].broadcast_to([P, 2]), bk[:, c:c + 1],
                          start=(c == 0), stop=(c == KC - 1))
            last.then_inc(s_pe, 1)
            reader = {}

            def free(name, p, reads, count):
                bank = TURN[name] if name in TURN else 2 + MIX[name]
                if bank in reader:
                    before, at, when = reader[bank]
                    for signal in before:
                        pe.wait_ge(signal, at(when))
                reader[bank] = (reads, count, p)
                return banks[bank]

            def split3(ps, lhs_hi, lhs_lo, rhs_hi, rhs_lo, start=True, stop=True):
                ops = [(a(c), b(c)) for c in range(KC)
                       for a, b in ((lhs_hi, rhs_hi), (lhs_hi, rhs_lo), (lhs_lo, rhs_hi))]
                for i, (a, b) in enumerate(ops):
                    last = mm(ps, a, b, start=start and i == 0, stop=stop and i == len(ops) - 1)
                return last

            @step
            def x_turn(p, s, c):
                ps = free(f"XT{s}{c}", p, (h_ready, h_hi_rdy), lambda q: KC * seq(q, s) + c + 1)
                pe.wait_ge(xhat_ready, NT * seq(p, s) + NT)
                for t in range(NT):
                    last = tr(ps[:, t * P:(t + 1) * P], xhat[:, t, c * P:(c + 1) * P], ident[:, :])
                last.then_inc(xt_done, 1)

            @step
            def project_g(p, s, m):
                ps = free(f"G{s}{m}", p, (g_lo_rdy,), lambda q: KC * seq(q, s) + m + 1)
                pe.wait_ge(h_lo_rdy, KC * seq(p, s) + KC)
                split3(ps[:, 0:S], lambda c: a_hi[:, c, m * P:(m + 1) * P], lambda c: a_lo[:, c, m * P:(m + 1) * P],
                       lambda c: h_hi[s][:, c, :], lambda c: h_lo[s][:, c, :]).then_inc(g_done, 1)

            @step
            def project_v(p, s, t):
                ps = free(f"V{s}{t}", p, (v_ready,), lambda q: NT * seq(q, s) + t + 1)
                pe.wait_ge(h_lo_rdy, KC * seq(p, s) + KC)
                mm(ps[:, 0:VW], ones2[:, :], vbias[:, :], start=True, stop=False)
                split3(ps[:, 0:VW], lambda c: h_hi[s][:, c, t * P:(t + 1) * P], lambda c: h_lo[s][:, c, t * P:(t + 1) * P],
                       lambda c: m_hi[:, c, :], lambda c: m_lo[:, c, :], start=False).then_inc(vproj_done, 1)

            @step
            def scores(p, s, t):
                b = seq(p, s)
                if t == 0:
                    pe.wait_ge(g_lo_rdy, KC * b + KC)
                need(pe, absc_ready, NT * b + t - 1)
                w = (t + 1) * P
                split3(score_ps[t % 2][:, 0:w], lambda c: g_hi[:, c, t * P:(t + 1) * P], lambda c: g_lo[:, c, t * P:(t + 1) * P],
                       lambda c: h_hi[s][:, c, 0:w], lambda c: h_lo[s][:, c, 0:w]).then_inc(scores_done, 1)

            @step
            def p_turn(p, s, t):
                b = seq(p, s)
                ps = free(f"PT{s}{t}", p, (pt_rdy,), lambda q: NT * seq(q, s) + t + 1)
                pe.wait_ge(probs_rdy, NT * b + t + 1)
                for j in range(t + 1):
                    last = tr(ps[:, j * P:(j + 1) * P], probs[t][:, j * P:(j + 1) * P], ident[:, :])
                last.then_inc(pt_done, 1)

            @step
            def attend(p, s, t):
                b = seq(p, s)
                need(pe, gated_rdy, NT * b + t)
                pe.wait_ge(pt_rdy, NT * b + t + 1)
                for j in range(t + 1):
                    last = mm(attn_ps[:, 0:D], probsT[t][:, j * P:(j + 1) * P],
                              v_sb[s][:, j, 0:D], start=(j == 0), stop=(j == t))
                last.then_inc(pv_done, 1)

            @step
            def h2_turn(p, u):
                s, m = u // KC, u % KC
                ps = free(f"H2T{u}", p, (h2_rdy,), lambda q: 2 * KC * q + u + 1)
                pe.wait_ge(xhat2_rdy, PT * p + NT * (s + 1))
                for t in range(NT):
                    last = tr(ps[:, t * P:(t + 1) * P], xhat2[:, NT * s + t, m * P:(m + 1) * P], ident[:, :])
                last.then_inc(h2t_done, 1)

            @step
            def ffn_scores(p, u):
                ps = free(f"FS{u}", p, (fs_rdy,), lambda q: 3 * q + u + 1)
                tiles = range(3 * u, min(3 * u + 3, PT))
                pe.wait_ge(h2_lo_rdy, 2 * KC * p + KC * (tiles[-1] // NT + 1))
                for i, t in enumerate(tiles):
                    s, q = t // NT, (t % NT) * P
                    last = split3(ps[:, i * FW:(i + 1) * FW], lambda m: h2_hi[:, s, m, q:q + P], lambda m: h2_lo[:, s, m, q:q + P],
                                  lambda m: f_hi[:, m, :], lambda m: f_lo[:, m, :])
                last.then_inc(fs_done, 1)

            @step
            def turn_back(p, u):
                ps = free(f"BT{u}", p, (h2_tok_rdy,), lambda q: NT * q + u + 1)
                pe.wait_ge(h2_rdy, 2 * KC * p + KC * (u // 2 + 1))
                for i in range(2):
                    t = 2 * u + i
                    for m in range(KC):
                        q = (t % NT) * P
                        last = tr(ps[:, i * D + m * P:i * D + (m + 1) * P], h2_full[:, t // NT, m, q:q + P], ident[:, :])
                last.then_inc(bt_done, 1)

            @step
            def onehot_turn(p, u):
                ps = free(f"OHT{u}", p, (oht_rdy,), lambda q: 2 * q + u + 1)[:, :].bitcast(BF16)
                pe.wait_ge(onehot_rdy, p + 1)
                for i in range(NT):
                    last = tr(ps[:, i * P:(i + 1) * P], onehot[:, NT * u + i, :], identb[:, :])
                last.then_inc(oht_done, 1)

            @step
            def gather(p, t):
                ps = free(f"GA{t}", p, (gath_rdy,), lambda q: PT * q + t + 1)
                pe.wait_ge(oht_rdy, 2 * p + t // NT + 1)
                mm(ps[:, 0:GW], onehotT[:, t * P:(t + 1) * P], table[:, :], start=True, stop=True).then_inc(ga_done, 1)

            pe.wait_ge(s_dve, ROWS_READY)
            for c in range(KC):
                run_ahead(x_turn, 0, 0, c)
            pe.wait_ge(s_dve, DVE_SETUP)

            def superstep(k):
                if not isinstance(k, int):
                    lags = {bank: LAG - p for bank, (_, _, p) in reader.items()}
                    for bank, (r, at, _) in list(reader.items()):
                        reader[bank] = (r, at, k - 1 - lags[bank])
                h2_turn(k - 3, 2)
                project_v(k - 2, 0, 0)
                h2_turn(k - 3, 3)
                for i in range(0, 2):
                    project_g(k - 2, 0, i)
                for i in range(0, 2):
                    x_turn(k - 2, 1, i)
                for i in range(0, 3):
                    ffn_scores(k - 3, i)
                for i in range(1, 3):
                    project_v(k - 2, 0, i)
                for i in range(0, 2):
                    scores(k - 2, 0, i)
                project_v(k - 2, 0, 3)
                turn_back(k - 3, 0)
                for i in range(2, 4):
                    scores(k - 2, 0, i)
                p_turn(k - 2, 0, 0)
                for i in range(0, 2):
                    project_g(k - 2, 1, i)
                attend(k - 2, 0, 0)
                project_v(k - 2, 1, 0)
                p_turn(k - 2, 0, 1)
                project_v(k - 2, 1, 1)
                p_turn(k - 2, 0, 2)
                for i in range(0, 2):
                    scores(k - 2, 1, i)
                attend(k - 2, 0, 1)
                project_v(k - 2, 1, 2)
                p_turn(k - 2, 0, 3)
                scores(k - 2, 1, 2)
                attend(k - 2, 0, 2)
                project_v(k - 2, 1, 3)
                turn_back(k - 3, 1)
                attend(k - 2, 0, 3)
                p_turn(k - 2, 1, 0)
                scores(k - 2, 1, 3)
                p_turn(k - 2, 1, 1)
                turn_back(k - 3, 2)
                p_turn(k - 2, 1, 2)
                attend(k - 2, 1, 0)
                turn_back(k - 3, 3)
                for i in range(0, 2):
                    onehot_turn(k - 3, i)
                attend(k - 2, 1, 1)
                for i in range(0, 3):
                    gather(k - 3, i)
                p_turn(k - 2, 1, 3)
                attend(k - 2, 1, 2)
                for i in range(3, 8):
                    gather(k - 3, i)
                attend(k - 2, 1, 3)
                for i in range(0, 2):
                    x_turn(k - 1, 0, i)
                for i in range(0, 2):
                    h2_turn(k - 2, i)
                if not isinstance(k, int):
                    for bank, (r, at, _) in list(reader.items()):
                        reader[bank] = (r, at, PAIRS - 1 - lags[bank])

            pipeline(pe, superstep)

        @block.scalar
        def _(act):
            A = nc.scalar.activation
            def load(loaded, dst, src):
                act.dma_start(dst, src).then_inc(loaded, 16)

            load(in_c, c_sb[:, :], ins["L0_c"])
            nc.scalar.preload_act_table_set("natural_log_exp_and_others")
            load(in_mod, wmod_sb[:, :, :], ins["L0_wmod"].rearrange("(c p) n -> p c n", p=P))
            load(in_rest, f_full[:, :, NCL + NTILES:FW], ins["L0_ffn_compress_w1"].rearrange("(c p) n -> p c n", p=P))
            load(in_rest, gamma_r[:, :], ins["L0_ffn_norm_gamma"].rearrange("(o d) -> o d", o=1).broadcast_to([B, D]))
            load(in_rest, beta_r[:, :], ins["L0_ffn_norm_beta"].rearrange("(o d) -> o d", o=1).broadcast_to([B, D]))
            act.wait_ge(in_c, 16)
            A(c_exp[:, :], c_sb[:, :], ACT.Exp, scale=-1.0).then_inc(s_act, 1)
            G = GRID
            for h in range(2):
                r = slice(h * NTILES, (h + 1) * NTILES)
                load(in_rest, t_full[r, 0:2 * G], ins["L0_ffn_spline_w1"].rearrange("n i g -> n (i g)"))
                load(in_rest, t_full[r, 2 * G:3 * G], ins["L0_ffn_spline_b1"])
                load(in_rest, t_full[r, 3 * G:4 * G], ins["L0_ffn_spline_w2"].rearrange("n g o -> n (g o)"))
                load(in_rest, t_full[r, 4 * G:4 * G + 1], ins["L0_ffn_spline_b2"])
                load(in_rest, t_full[r, PAR:GW], ins["L0_ffn_directions"])
            act.wait_ge(s_pe, 4)
            A(woT[:, :, :].rearrange("p c d -> p (c d)"), banks[1][:, :], ACT.Copy).then_inc(s_act, 1)

            def ln_guess(out_, var, ready, chain, i, signal):
                act.wait_ge(ready, i + 1)
                chain.link(act, A(out_, var, ACT.Ln))
                A(out_, out_, ACT.Exp, scale=-0.5).then_inc(signal, 1)

            @step
            def a_guess(p, s):
                b = seq(p, s)
                act_guess1.at(b)
                ln_guess(guess1[:, :], var1[:, :], ln1_var, act_guess1, b, ln1_guess)

            @step
            def a_xhat(p, s, t):
                b = seq(p, s)
                act.wait_ge(ln1_ready, b + 1)
                need(act, xt_done, KC * b)
                A(xhat[:, t, :], x_sb[s][:, t, :], ACT.Identity, bias=nmr1[:, t:t + 1],
                  scale=rstd1[:, t:t + 1]).then_inc(xhat_ready, 1)

            @step
            def a_evict(p, s, c):
                b = seq(p, s)
                act.wait_ge(xt_done, KC * b + c + 1)
                need(act, h_lo_rdy, KC * (b - 1) + c + 1)
                A(h_full[:, c, :], turn_ps[TURN[f"XT{s}{c}"]][:, :], ACT.Identity,
                  bias=sa_col[:, c, bass.ds(b, 1)], scale=ca_col[:, c, bass.ds(b, 1)]).then_inc(h_ready, 1)

            @step
            def a_hi(p, s, c):
                b = seq(p, s)
                act.wait_ge(xt_done, KC * b + c + 1)
                need(act, scores_done, NT * (b - 1))
                A(h_hi[s][:, c, :], turn_ps[TURN[f"XT{s}{c}"]][:, :], ACT.Identity,
                  bias=sa_col2[:, c, bass.ds(b, 1)], scale=ca_col2[:, c, bass.ds(b, 1)]).then_inc(h_hi_rdy, 1)

            @step
            def b_g(p, s, c):
                b = seq(p, s)
                act.wait_ge(g_done, KC * b + c + 1)
                need(act, scores_done, NT * b)
                A(g_hi[:, c, :], mix_ps[MIX[f"G{s}{c}"]][:, :], ACT.Identity,
                  bias=g_bias[:, c:c + 1]).then_inc(g_hi_rdy, 1)

            @step
            def b_v(p, s, t):
                b = seq(p, s)
                act.wait_ge(vproj_done, NT * b + t + 1)
                need(act, pv_done, NT * (b - 1))
                A(v_sb[s][:, t, :], mix_ps[MIX[f"V{s}{t}"]][:, 0:VW], ACT.Identity).then_inc(v_ready, 1)

            @step
            def b_abs(p, s, t):
                b, w = seq(p, s), (t + 1) * P
                act.wait_ge(scores_done, NT * b + t + 1)
                act.wait_ge(v_ready, NT * b + t + 1)
                need(act, probs_rdy, NT * (b - 1) + t + 1)
                A(absc[t][:, 0:w], score_ps[t % 2][:, 0:w], ACT.Abs, bias=v_sb[s][:, t, D:D + 1],
                  scale=SCALE).then_inc(absc_ready, 1)

            @step
            def b_exp(p, s, t):
                b, w = seq(p, s), (t + 1) * P
                act.wait_ge(rowmax, NT * b + t + 1)
                need(act, pt_done, NT * (b - 1) + t + 1)
                if t == 0:
                    need(act, gated_rdy, NT * (b - 1))
                A(probs[t][:, 0:w], absc[t][:, 0:w], ACT.Exp, bias=negmax[:, t:t + 1],
                  accum_out=rowsum[s][:, t:t + 1]).then_inc(probs_rdy, 1)

            @step
            def b_pt(p, s, t):
                b, w = seq(p, s), (t + 1) * P
                act.wait_ge(pt_done, NT * b + t + 1)
                need(act, pv_done, NT * (b - 1) + t + 1)
                A(probsT[t][:, 0:w], turn_ps[TURN[f"PT{s}{t}"]][:, 0:w], ACT.Identity).then_inc(pt_rdy, 1)

            @step
            def c_guess2(p):
                act_guess2.at(p)
                ln_guess(guess2[:, :], var2[:, :], ln2_var, act_guess2, p, ln2_guess)

            @step
            def c_h2(p, u):
                s, m = u // KC, u % KC
                b = seq(p, s)
                act.wait_ge(h2t_done, 2 * KC * p + u + 1)
                need(act, h2_lo_rdy, 2 * KC * (p - 1) + u + 1)
                need(act, bt_done, NT * (p - 1) + 2 * (s + 1))
                A(h2_full[:, s, m, :], turn_ps[TURN[f"H2T{u}"]][:, :], ACT.Identity,
                  bias=sb_col[:, m, bass.ds(b, 1)], scale=cb_col[:, m, bass.ds(b, 1)]).then_inc(h2_rdy, 1)

            @step
            def c_fs(p, u):
                n_ = min(3, PT - 3 * u)
                act.wait_ge(fs_done, 3 * p + u + 1)
                need(act, onehot_rdy, p)
                need(act, pregelu, p)
                A(fs[:, 3 * u:3 * u + n_, :].rearrange("p t f -> p (t f)"), mix_ps[MIX[f"FS{u}"]][:, 0:n_ * FW],
                  ACT.Identity).then_inc(fs_rdy, 1)

            @step
            def c_back(p, u):
                act.wait_ge(bt_done, NT * p + u + 1)
                need(act, y_sem, PT * (p - 1) + 2 * (u + 1))
                A(h2_tok[:, 2 * u:2 * u + 2, :].rearrange("p t d -> p (t d)"), mix_ps[MIX[f"BT{u}"]][:, :],
                  ACT.Identity).then_inc(h2_tok_rdy, 1)

            @step
            def c_exp_cl(p):
                act.wait_ge(zc_rdy, p + 1)
                A(z_cl[:, :], z_cl[:, :], ACT.Exp, scale=-1.0).then_inc(ec_rdy, 1)

            @step
            def c_exp_lo(p):
                act.wait_ge(zl_rdy, p + 1)
                A(z_lo[:, :], z_lo[:, :], ACT.Exp, scale=-1.0).then_inc(el_rdy, 1)

            @step
            def c_gelu(p):
                act.wait_ge(pregelu, p + 1)
                A(hid[:, :, :], hid[:, :, :], ACT.Gelu).then_inc(gelu_rdy, 1)

            @step
            def c_tanh(p):
                act.wait_ge(pretanh, p + 1)
                need(act, y_sem, PT * (p - 1) + 1)
                A(comp[:, :, :], cmp_t[:, :, :], ACT.Tanh).then_inc(tanh_rdy, 1)
                nc.scalar.preload_act_table_set("natural_log_exp_and_others")

            @step
            def c_onehot(p, u):
                act.wait_ge(oht_done, 2 * p + u + 1)
                need(act, ga_done, PT * (p - 1) + NT * (u + 1))
                A(onehotT[:, u * S:(u + 1) * S], turn_ps[TURN[f"OHT{u}"]][:, :].bitcast(BF16)[:, 0:S],
                  ACT.Identity).then_inc(oht_rdy, 1)

            @step
            def c_gath(p, t):
                act.wait_ge(ga_done, PT * p + t + 1)
                need(act, y_sem, PT * (p - 1) + t + 1)
                A(gath[:, t, :], mix_ps[MIX[f"GA{t}"]][:, 0:GW], ACT.Identity).then_inc(gath_rdy, 1)

            @step
            def c_guess3(p):
                act_guess3.at(p)
                ln_guess(guess3[:, :], var3[:, :], ln3_var, act_guess3, p, ln3_guess)

            @step
            def c_yhat(p, t):
                act.wait_ge(ln3_ready, p + 1)
                A(y[:, t, :], y[:, t, :], ACT.Identity, bias=nmr3[:, t:t + 1],
                  scale=rstd3[:, t:t + 1]).then_inc(yhat_rdy, 1)

            run_ahead(a_guess, 0, 0)
            for t in range(NT):
                run_ahead(a_xhat, 0, 0, t)
            act.wait_ge(s_dve, COLUMNS_READY)
            for c in range(KC):
                run_ahead(a_evict, 0, 0, c)
                run_ahead(a_hi, 0, 0, c)
            act.wait_ge(s_dve, DVE_SETUP)

            def superstep(k):
                b_exp(k - 2, 0, 1)
                b_g(k - 2, 1, 0)
                b_exp(k - 2, 0, 2)
                b_g(k - 2, 1, 1)
                b_v(k - 2, 1, 0)
                for i in range(1, 3):
                    b_pt(k - 2, 0, i)
                b_abs(k - 2, 1, 0)
                b_v(k - 2, 1, 1)
                b_exp(k - 2, 0, 3)
                c_exp_lo(k - 3)
                b_abs(k - 2, 1, 1)
                b_v(k - 2, 1, 2)
                b_exp(k - 2, 1, 0)
                b_pt(k - 2, 0, 3)
                b_abs(k - 2, 1, 2)
                c_gelu(k - 3)
                b_exp(k - 2, 1, 1)
                c_back(k - 3, 1)
                b_v(k - 2, 1, 3)
                b_pt(k - 2, 1, 0)
                b_exp(k - 2, 1, 2)
                b_abs(k - 2, 1, 3)
                for i in range(1, 3):
                    b_pt(k - 2, 1, i)
                for i in range(2, 4):
                    c_back(k - 3, i)
                c_onehot(k - 3, 0)
                b_exp(k - 2, 1, 3)
                c_onehot(k - 3, 1)
                for i in range(0, 3):
                    c_gath(k - 3, i)
                b_pt(k - 2, 1, 3)
                for i in range(3, 8):
                    c_gath(k - 3, i)
                c_tanh(k - 3)
                a_guess(k - 1, 0)
                c_guess2(k - 2)
                for i in range(0, 4):
                    a_xhat(k - 1, 0, i)
                a_hi(k - 1, 0, 0)
                for i in range(0, 2):
                    a_evict(k - 1, 0, i)
                a_hi(k - 1, 0, 1)
                c_h2(k - 2, 0)
                a_guess(k - 1, 1)
                for i in range(1, 3):
                    c_h2(k - 2, i)
                for i in range(0, 2):
                    a_xhat(k - 1, 1, i)
                b_v(k - 1, 0, 0)
                for i in range(2, 4):
                    a_xhat(k - 1, 1, i)
                c_h2(k - 2, 3)
                for i in range(0, 2):
                    b_g(k - 1, 0, i)
                a_hi(k - 1, 1, 0)
                c_guess3(k - 3)
                a_evict(k - 1, 1, 0)
                for i in range(0, 4):
                    c_yhat(k - 3, i)
                c_fs(k - 2, 0)
                a_hi(k - 1, 1, 1)
                for i in range(1, 3):
                    c_fs(k - 2, i)
                c_exp_cl(k - 2)
                a_evict(k - 1, 1, 1)
                b_v(k - 1, 0, 1)
                b_abs(k - 1, 0, 0)
                b_v(k - 1, 0, 2)
                c_yhat(k - 3, 4)
                b_abs(k - 1, 0, 1)
                for i in range(5, 7):
                    c_yhat(k - 3, i)
                b_v(k - 1, 0, 3)
                b_exp(k - 1, 0, 0)
                b_abs(k - 1, 0, 2)
                c_back(k - 2, 0)
                c_yhat(k - 3, 7)
                b_abs(k - 1, 0, 3)
                b_pt(k - 1, 0, 0)

            pipeline(act, superstep)

        @block.gpsimd
        def _(pool):
            gp = nc.gpsimd
            n = [0]

            def link(ins_):
                n[0] += 1
                ins_.then_inc(s_pool, 1)
                pool.wait_ge(s_pool, n[0])

            link(gp.memset(ident[:, :], 0.0))
            gp.affine_select(out=ident[:, :], in_=ident[:, :], compare_op=ALU.not_equal, fill=1.0, base=0,
                             pattern=[[-1, P]], channel_multiplier=1).then_inc(id_ready, 1)
            link(gp.memset(causal[:, :], 0.0))
            gp.affine_select(out=causal[:, :], in_=causal[:, :], compare_op=ALU.is_ge, fill=MASKED, base=0,
                             pattern=[[-1, P]], channel_multiplier=1)
            for j in range(K):
                gp.memset(steps[:, j:j + 1], float(j))
            for j in range(TPC):
                gp.memset(falling[:, j:j + 1], float(TPC - j))
            link(gp.memset(t_full[:, PAR - 1:PAR], 0.0))
            link(gp.memset(vb2[:, :], 0.0))
            assert n[0] == POOL_SETUP

            @step
            def split_h(p, s, c):
                pool.wait_ge(h_ready, KC * seq(p, s) + c + 1)
                pool.wait_ge(h_hi_rdy, KC * seq(p, s) + c + 1)
                gp.tensor_tensor(h_lo[s][:, c, :], h_full[:, c, :], h_hi[s][:, c, :].bitcast(F32),
                                 ALU.subtract).then_inc(h_lo_rdy, 1)

            @step
            def mask(p, s, t):
                pool.wait_ge(absc_ready, NT * seq(p, s) + t + 1)
                d = absc[t][:, t * P:(t + 1) * P]
                gp.tensor_tensor(d, d, causal[:, :], ALU.add).then_inc(masked, 1)

            @step
            def residual(p, s, t):
                pool.wait_ge(gated_rdy, NT * seq(p, s) + t + 1)
                if t == 0:
                    need(pool, xhat2_rdy, PT * (p - 1) + NT * (s + 1))
                    need(pool, base_rdy, NT * (p - 1) + 2 * (s + 1))
                gp.tensor_tensor(x2[s][:, t, :], gated[t % 2][:, :], x_sb[s][:, t, :], ALU.add).then_inc(x2_rdy, 1)

            @step
            def split_h2(p, u):
                s, m = u // KC, u % KC
                pool.wait_ge(h2_hi_rdy, 2 * KC * p + u + 1)
                gp.tensor_tensor(h2_lo[:, s, m, :], h2_full[:, s, m, :], h2_hi[:, s, m, :].bitcast(F32),
                                 ALU.subtract).then_inc(h2_lo_rdy, 1)

            @step
            def knot_product(p, local, i):
                pool.wait_ge(knot_sel, 2 * p + local + 1)
                row = (knots[:, 0:K - 1], knot_step[:, :])[i].unsqueeze(1).broadcast_to([P, E8, K - 1])
                gp.tensor_tensor(cal7[1 + i][:, :, :], cal7[0][:, :, :], row, ALU.mult).then_inc(knot_prod, 1)

            @step
            def w2_product(p, o):
                pool.wait_ge(gelu_rdy, p + 1)
                need(pool, pretanh, p)
                gp.tensor_tensor(w2prod[:, :, o, :], hid[:, :, :], w2_rows[:, :, o].unsqueeze(1).broadcast_to([P, PT, H]),
                                 ALU.mult).then_inc(w2_prod, 1)

            @step
            def base(p, u):
                s, t = u // 2, slice(2 * (u % 2), 2 * (u % 2) + 2)
                pool.wait_ge(gb_ld[s], 16 * (p + 1))
                pool.wait_ge(x2_rdy, NT * seq(p, s) + 2 * (u % 2) + 2)
                need(pool, sent[s], 16 * p)
                gp.tensor_tensor(res[:, 2 * u:2 * u + 2, :], x2[s][:, t, :],
                                 gb_row[s][:, 1:2, :].broadcast_to([P, 2, D]), ALU.add).then_inc(base_rdy, 1)

            @step
            def scale_y(p, u):
                pool.wait_ge(yhat_rdy, PT * p + 2 * (u + 1))
                ys = y[:, 2 * u:2 * u + 2, :]
                gp.tensor_tensor(ys, ys, gb_row[u // 2][:, 0:1, :].broadcast_to([P, 2, D]), ALU.mult).then_inc(scaled, 1)

            @step
            def finish(p, u):
                pool.wait_ge(scaled, NT * p + u + 1)
                pool.wait_ge(base_rdy, NT * p + u + 1)
                rs = res[:, 2 * u:2 * u + 2, :]
                gp.tensor_tensor(rs, rs, y[:, 2 * u:2 * u + 2, :], ALU.add).then_inc(res_rdy, 1)

            def superstep(k):
                for i in range(2, 4):
                    residual(k - 2, 0, i)
                w2_product(k - 3, 0)
                mask(k - 2, 1, 3)
                w2_product(k - 3, 1)
                for i in range(2, 4):
                    base(k - 3, i)
                for i in range(0, 4):
                    residual(k - 2, 1, i)
                for i in range(0, 2):
                    split_h(k - 1, 0, i)
                for i in range(0, 4):
                    split_h2(k - 2, i)
                split_h(k - 1, 1, 0)
                for i in range(0, 2):
                    scale_y(k - 3, i)
                for i in range(0, 2):
                    finish(k - 3, i)
                mask(k - 1, 0, 0)
                split_h(k - 1, 1, 1)
                mask(k - 1, 0, 1)
                knot_product(k - 2, local=False, i=0)
                mask(k - 1, 0, 2)
                knot_product(k - 2, local=False, i=1)
                scale_y(k - 3, 2)
                mask(k - 1, 0, 3)
                scale_y(k - 3, 3)
                for i in range(2, 4):
                    finish(k - 3, i)
                mask(k - 1, 1, 0)
                for i in range(0, 2):
                    base(k - 2, i)
                mask(k - 1, 1, 1)
                residual(k - 1, 0, 0)
                mask(k - 1, 1, 2)
                for i in range(0, 2):
                    knot_product(k - 2, local=True, i=i)
                residual(k - 1, 0, 1)

            pipeline(pool, superstep)

        @block.vector
        def _(dve):
            v = nc.vector
            tt, ts, stt, red = v.tensor_tensor, v.tensor_scalar, v.scalar_tensor_tensor, v.tensor_reduce
            n = [0]

            def mark(ins_):
                n[0] += 1
                ins_.then_inc(s_dve, 1)

            def link(ins_):
                mark(ins_)
                dve.wait_ge(s_dve, n[0])

            dve.wait_ge(id_ready, 1)
            dve.wait_ge(s_pool, POOL_SETUP)
            link(v.tensor_copy(identb[:, :], ident[:, :]))
            dve.wait_ge(s_act, 1)
            link(ts(c_exp[:, :], c_exp[:, :], 1.0, None, ALU.add))
            link(v.reciprocal(c_exp[:, :], c_exp[:, :]))
            link(tt(c_sb[:, :], c_sb[:, :], c_exp[:, :], ALU.mult))
            assert n[0] == SILU_READY, n
            dve.wait_ge(s_pe, 2)
            link(v.tensor_copy(c_T[:, :, :].rearrange("p c b -> p (c b)"), banks[5][:, 0:KC * B]))
            assert n[0] == CT_READY, n
            link(v.tensor_copy(raw_T, banks[7][:, 0:KC * NTILES]))
            mark(ts(sig_T, raw_T, 0.3, None, ALU.is_gt))
            link(ts(sig_tmp, raw_T, -0.3, None, ALU.is_lt))
            link(tt(sig_T, sig_T, sig_tmp, ALU.subtract))
            link(tt(sig_T, sig_T, raw_T, ALU.subtract))
            link(tt(sig_T, raw_T, sig_T, ALU.add))
            sig = sig_T.rearrange("p (c j) -> p c j", c=KC * NCL)
            link(tt(cl_sum[:, :], sig[:, :, 0], sig[:, :, 1], ALU.add))
            for j in range(2, TPC):
                link(tt(cl_sum[:, :], cl_sum[:, :], sig[:, :, j], ALU.add))
            link(ts(cl_neg[:, :], cl_sum[:, :], 0.0, None, ALU.is_lt))
            link(ts(cl_sum[:, :], cl_sum[:, :], 0.0, None, ALU.is_gt))
            mark(tt(f_full[:, :, 0:NCL], cl_sum[:, :].rearrange("p (c j) -> p c j", c=KC),
                    cl_neg[:, :].rearrange("p (c j) -> p c j", c=KC), ALU.subtract))
            mark(v.tensor_copy(f_full[:, :, NCL:NCL + NTILES], sig_T.rearrange("p (c j) -> p c j", c=KC)))
            flat = lambda a: a[:, :, :].rearrange("p c d -> p (c d)")
            dve.wait_ge(s_pe, 3)
            link(v.tensor_copy(flat(a_hi), banks[0][:, :]))
            mark(tt(flat(a_lo), banks[0][:, :], flat(a_hi).bitcast(F32), ALU.subtract))
            dve.wait_ge(s_pe, 5)
            g = mod[:, 0:2, :].rearrange("b a d -> b (a d)")
            r = rows[:, 0:2, :].rearrange("b a d -> b (a d)")
            link(v.tensor_copy(g, banks[5][0:B, :]))
            mark(stt(out=r, in0=g, scalar=-1.0, in1=g, op0=ALU.mult, op1=ALU.max))
            link(ts(mod2, g, 0.0, None, ALU.is_ge))
            link(ts(mod2, mod2, 2.0, -1.0, ALU.mult, ALU.add))
            link(stt(out=r, in0=r, scalar=GATE_MIN, in1=mod2, op0=ALU.max, op1=ALU.mult))
            dve.wait_ge(in_rest, 16 * LOADS_REST)
            link(tt(rows[:, 2, :], rows[:, 1, :], beta_r[:, :], ALU.mult))
            link(tt(rows[:, 1, :], rows[:, 1, :], gamma_r[:, :], ALU.mult))
            assert n[0] == ROWS_READY, n

            VAR_STEPS, NORM_STEPS = 4, 4

            def variance(i, chain, st, sums, dif, var, signal):
                if i in (1, 3):
                    chain.wait(dve)
                if i == 0:
                    chain.mark(tt(dif, st[:, :, 1], st[:, :, 4], ALU.subtract))
                    chain.mark(tt(var, st[:, :, 2], st[:, :, 5], ALU.add))
                elif i == 1:
                    chain.mark(tt(dif, dif, dif, ALU.mult))
                    chain.mark(ts(var, var, 1.0 / D, EPS, ALU.mult, ALU.add))
                elif i == 2:
                    chain.mark(tt(sums, st[:, :, 1], st[:, :, 4], ALU.add))
                else:
                    stt(out=var, in0=dif, scalar=0.25, in1=var, op0=ALU.mult, op1=ALU.add).then_inc(signal, 1)

            def newton(i, chain, var, guess, tmp, rstd, nmr, sums, signal):
                if i == 0:
                    chain.mark(tt(tmp, guess, guess, ALU.mult))
                    return
                chain.wait(dve)
                if i == 1:
                    chain.mark(stt(out=tmp, in0=tmp, scalar=-0.5, in1=var, op0=ALU.mult, op1=ALU.mult))
                elif i == 2:
                    chain.mark(stt(out=rstd, in0=tmp, scalar=1.5, in1=guess, op0=ALU.add, op1=ALU.mult))
                else:
                    stt(out=nmr, in0=sums, scalar=-0.5, in1=rstd, op0=ALU.mult, op1=ALU.mult).then_inc(signal, 1)

            @step
            def a_stats(p, s, t):
                dve_a.at(seq(p, s))
                if t == 0:
                    dve.wait_ge(x_ld[s], 16 * (p + 1))
                dve_a.mark(v.bn_stats(st1[:, t, :], x_sb[s][:, t, :]))

            @step
            def a_var(p, s, i):
                dve_a.at(seq(p, s))
                if i == 0:
                    dve_a.wait(dve)
                variance(i, dve_a, st1, sum1[:, :], dif1[:, :], var1[:, :], ln1_var)

            @step
            def a_norm(p, s, i):
                dve_a.at(seq(p, s))
                if i == 0:
                    dve.wait_ge(ln1_guess, seq(p, s) + 1)
                    need(dve, xhat_ready, NT * seq(p, s))
                newton(i, dve_a, var1[:, :], guess1[:, :], newt1[:, :], rstd1[:, :], nmr1[:, :], sum1[:, :], ln1_ready)

            @step
            def b_split(p, s, c):
                dve.wait_ge(g_hi_rdy, KC * seq(p, s) + c + 1)
                stt(out=g_lo[:, c, :], in0=mix_ps[MIX[f"G{s}{c}"]][:, :], scalar=g_bias[:, c:c + 1],
                    in1=g_hi[:, c, :].bitcast(F32), op0=ALU.add, op1=ALU.subtract).then_inc(g_lo_rdy, 1)

            @step
            def b_max(p, s, t):
                dve.wait_ge(masked, NT * seq(p, s) + t + 1)
                red(negmax[:, t:t + 1], absc[t][:, 0:(t + 1) * P], X, ALU.max, negate=True).then_inc(rowmax, 1)

            @step
            def b_rinv(p, s, t):
                b = seq(p, s)
                dve_b.at(b)
                dve.wait_ge(probs_rdy, NT * b + t + 1)
                dve_b.mark(v.reciprocal(rinv[:, t:t + 1], rowsum[s][:, t:t + 1]))

            @step
            def b_gate(p, s, t):
                b = seq(p, s)
                if t == 0:
                    dve.wait_ge(ga_ld[s], 16 * (p + 1))
                dve.wait_ge(pv_done, NT * b + t + 1)
                need(dve, x2_rdy, NT * b + t - 1)
                dve.wait_ge(dve_b.sem, NT * b + t + 1)
                stt(out=gated[t % 2][:, :], in0=attn_ps[:, 0:D], scalar=rinv[:, t:t + 1], in1=ga_row[s][:, :],
                    op0=ALU.mult, op1=ALU.mult).then_inc(gated_rdy, 1)

            @step
            def b_stats(p, s, t):
                dve.wait_ge(x2_rdy, NT * seq(p, s) + t + 1)
                v.bn_stats(st2[:, NT * s + t, :], x2[s][:, t, :]).then_inc(st2_rdy, 1)

            @step
            def c_var(p, i):
                dve_ln2.at(p)
                if i == 0:
                    dve.wait_ge(st2_rdy, PT * (p + 1))
                variance(i, dve_ln2, st2, sum2[:, :], dif2[:, :], var2[:, :], ln2_var)

            @step
            def c_norm(p, i):
                dve_ln2.at(p)
                if i == 0:
                    dve.wait_ge(ln2_guess, p + 1)
                    need(dve, xhat2_rdy, PT * p)
                newton(i, dve_ln2, var2[:, :], guess2[:, :], newt2[:, :], rstd2[:, :], nmr2[:, :], sum2[:, :], ln2_ready)

            @step
            def c_xhat2(p, t):
                dve.wait_ge(ln2_ready, p + 1)
                need(dve, h2t_done, 2 * KC * (p - 1) + KC * (t // NT + 1))
                ts(xhat2[:, t, :], x2[t // NT][:, t % NT, :], rstd2[:, t:t + 1], nmr2[:, t:t + 1],
                   ALU.mult, ALU.add).then_inc(xhat2_rdy, 1)

            @step
            def c_split(p, u):
                s, m = u // KC, u % KC
                dve.wait_ge(h2_rdy, 2 * KC * p + u + 1)
                need(dve, fs_done, 3 * p)
                v.tensor_copy(h2_hi[:, s, m, :], h2_full[:, s, m, :]).then_inc(h2_hi_rdy, 1)

            @step
            def c_z(p):
                dve.wait_ge(fs_rdy, 3 * (p + 1))
                ts_z(z_cl[:, :].rearrange("p (t j) -> p t j", t=PT), fs[:, :, 0:NCL]).then_inc(zc_rdy, 1)

            @step
            def c_hidden(p):
                dve.wait_ge(fs_rdy, 3 * (p + 1))
                need(dve, w2_prod, NCOMP * p)
                tt(hid[:, :, :], fs[:, :, NCL + NTILES:FW], b1_row[:, :].unsqueeze(1).broadcast_to([P, PT, H]),
                   ALU.add).then_inc(pregelu, 1)

            def ts_z(dst, src):
                return ts(dst, src, inv_temp[:, 0:1], Z_MIN, ALU.mult, ALU.max)

            K1 = K - 1
            ROUND = float(2 ** 23)
            row7 = lambda a: a.unsqueeze(1).broadcast_to([P, E8, K1])
            col7 = lambda a: a.unsqueeze(2).broadcast_to([P, E8, K1])
            ix, fl, vl, vd, gates = (a[:, :] for a in cal)

            @step
            def c_calibrate(p, local, i):
                e = z_lo[:, :] if local else z_cl[:, :]
                dve_route.at(p)
                if i == 0:
                    dve.wait_ge(el_rdy if local else ec_rdy, p + 1)
                    dve_route.mark(ts(e, e, 1.0, None, ALU.add))
                    return
                if i in (7, 8):
                    dve.wait_ge(knot_prod, 4 * p + 2 * local + i - 6)
                    dve_route.mark(red((vl, vd)[i - 7], cal7[i - 6][:, :, :], X, ALU.add))
                    return
                dve_route.wait(dve)
                if i == 1:
                    dve_route.mark(v.reciprocal(ix, e))
                elif i == 2:
                    dve_route.mark(ts(ix, ix, float(K1), None, ALU.mult))
                elif i == 3:
                    dve_route.mark(ts(vl, ix, K1 - 0.6, ROUND, ALU.min, ALU.add))
                elif i == 4:
                    dve_route.mark(stt(out=vd, in0=vl, scalar=-ROUND, in1=ix, op0=ALU.add, op1=ALU.is_gt))
                elif i == 5:
                    dve_route.mark(stt(out=fl, in0=vl, scalar=-ROUND, in1=vd, op0=ALU.add, op1=ALU.subtract))
                elif i == 6:
                    dve_route.mark(tt(ix, ix, fl, ALU.subtract))
                    tt(cal7[0][:, :, :], col7(fl), row7(steps[:, 0:K1]), ALU.is_equal).then_inc(knot_sel, 1)
                elif i == 9:
                    dve_route.mark(tt(ix, ix, vd, ALU.mult))
                else:
                    dve_route.mark(tt(gates, vl, ix, ALU.add))

            @step
            def c_best(p, local, i):
                onehot_ = oh_lo[:, :, :] if local else oh_cl[:, :, :]
                dve_route.at(p)
                dve_route.wait(dve)
                gate = gates.rearrange("p (t j) -> p t j", t=PT)
                rank = cal[0][:, :].rearrange("p (t j) -> p t j", t=PT)
                spread = best[:, :].unsqueeze(2).broadcast_to([P, PT, TPC])
                if i == 0:
                    dve_route.mark(red(best[:, :], gate, X, ALU.max))
                elif i == 1:
                    dve_route.mark(tt(rank, gate, spread, ALU.is_equal))
                elif i == 2:
                    dve_route.mark(tt(rank, rank, falling[:, :].unsqueeze(1).broadcast_to([P, PT, TPC]), ALU.mult))
                elif i == 3:
                    dve_route.mark(red(best[:, :], rank, X, ALU.max))
                else:
                    dve_route.mark(tt(onehot_, rank, spread, ALU.is_equal))

            @step
            def c_pick(p, i):
                dve_route.at(p)
                if i != 1:
                    dve_route.wait(dve)
                pick = picked[:, :, :].rearrange("p t (c j) -> p t c j", c=NCL)
                zl = z_lo[:, :].rearrange("p (t j) -> p t j", t=PT)
                if i < 2:
                    tiles = slice(NT * i, NT * (i + 1))
                    dve_route.mark(tt(pick[:, tiles], fs[:, tiles, NCL:NCL + NTILES].rearrange("p t (c j) -> p t c j", c=NCL),
                                      oh_cl[:, tiles, :].unsqueeze(3).broadcast_to([P, NT, NCL, TPC]), ALU.mult))
                elif i == 2:
                    dve_route.mark(red(zl, pick.rearrange("p t c j -> p t j c"), X, ALU.add))
                else:
                    ts_z(zl, zl).then_inc(zl_rdy, 1)

            @step
            def c_onehot(p, i):
                dve_route.at(p)
                if i != 1:
                    dve_route.wait(dve)
                if i < 2:
                    if i == 0:
                        need(dve, oht_done, 2 * p)
                    q = slice(NT * i, NT * (i + 1))
                    dve_route.mark(tt(onehot[:, q, 0:NTILES].rearrange("p t (c j) -> p t c j", c=NCL),
                                      oh_cl[:, q, :].unsqueeze(3).broadcast_to([P, NT, NCL, TPC]),
                                      oh_lo[:, q, :].unsqueeze(2).broadcast_to([P, NT, NCL, TPC]), ALU.mult))
                else:
                    v.tensor_copy(onehot[:, :, NTILES:P], onehot[:, :, 0:NTILES]).then_inc(onehot_rdy, 1)

            @step
            def c_comp(p, i):
                dve_comp.at(p)
                if i == 0:
                    dve.wait_ge(w2_prod, NCOMP * (p + 1))
                    need(dve, tanh_rdy, p)
                    dve_comp.mark(red(cmp_t[:, :, :], w2prod[:, :, :, :], X, ALU.add))
                else:
                    dve_comp.wait(dve)
                    tt(cmp_t[:, :, :], cmp_t[:, :, :], b2_row[:, :].unsqueeze(1).broadcast_to([P, PT, NCOMP]),
                       ALU.add).then_inc(pretanh, 1)

            @step
            def c_spline(p, i):
                G = GRID
                dve_spline.at(p)
                cb = lambda j: comp[:, :, j:j + 1].broadcast_to([P, PT, G])
                mark_s = dve_spline.mark
                if i == 0:
                    dve.wait_ge(tanh_rdy, p + 1)
                    dve.wait_ge(gath_rdy, PT * (p + 1))
                    mark_s(tt(sp0[:, :, :], gath[:, :, 0:G], cb(0), ALU.mult))
                    mark_s(tt(sp1[:, :, :], gath[:, :, G:2 * G], cb(1), ALU.mult))
                    return
                dve_spline.wait(dve)
                if i == 1:
                    mark_s(tt(sp0[:, :, :], sp0[:, :, :], sp1[:, :, :], ALU.add))
                elif i == 2:
                    mark_s(tt(sp0[:, :, :], sp0[:, :, :], gath[:, :, 2 * G:3 * G], ALU.add))
                elif i == 3:
                    mark_s(stt(out=sp0[:, :, :], in0=sp0[:, :, :], scalar=0.0, in1=gath[:, :, 3 * G:4 * G],
                               op0=ALU.max, op1=ALU.mult))
                elif i == 4:
                    mark_s(red(mag[:, :], sp0[:, :, :], X, ALU.add))
                elif i == 5:
                    mark_s(tt(mag[:, :], mag[:, :], gath[:, :, 4 * G], ALU.add))
                else:
                    mark_s(ts(mag[:, :], mag[:, :], out_scale[:, 0:1], None, ALU.mult))

            @step
            def c_y(p, t):
                dve_spline.at(p)
                dve_spline.wait(dve)
                dve.wait_ge(h2_tok_rdy, NT * p + t // 2 + 1)
                need(dve, res_rdy, NT * (p - 1) + t // 2 + 1)
                stt(out=y[:, t, :], in0=gath[:, t, PAR:GW], scalar=mag[:, t:t + 1], in1=h2_tok[:, t, :],
                    op0=ALU.mult, op1=ALU.add).then_inc(y_sem, 1)

            @step
            def c_stats(p, t):
                dve_ln3.at(p)
                dve.wait_ge(y_sem, PT * p + t + 1)
                dve_ln3.mark(v.bn_stats(st3[:, t, :], y[:, t, :]))

            @step
            def c_var3(p, i):
                dve_ln3.at(p)
                if i == 0:
                    dve_ln3.wait(dve)
                variance(i, dve_ln3, st3, sum3[:, :], dif3[:, :], var3[:, :], ln3_var)

            @step
            def c_norm3(p, i):
                dve_ln3.at(p)
                if i == 0:
                    dve.wait_ge(ln3_guess, p + 1)
                    need(dve, yhat_rdy, PT * p)
                newton(i, dve_ln3, var3[:, :], guess3[:, :], newt3[:, :], rstd3[:, :], nmr3[:, :], sum3[:, :], ln3_ready)

            for t in range(NT):
                run_ahead(a_stats, 0, 0, t)
            for i in range(VAR_STEPS):
                run_ahead(a_var, 0, 0, i)
            for i in range(NORM_STEPS):
                run_ahead(a_norm, 0, 0, i)
            dve.wait_ge(s_pe, 6)
            for i, dst, add in ((0, sa_col, 0.0), (0, sa_col2, 0.0), (1, ca_col, 1.0), (1, ca_col2, 1.0),
                                (2, sb_col, 0.0), (3, cb_col, 1.0)):
                mark(ts(flat(dst), banks[6][:, i * KC * B:(i + 1) * KC * B], add, None, ALU.add))
            assert n[0] == COLUMNS_READY, n
            link(v.tensor_copy(flat(f_hi), flat(f_full)))
            mark(tt(flat(f_lo), flat(f_full), flat(f_hi).bitcast(F32), ALU.subtract))
            lo = slice(NTILES, P)
            link(v.tensor_copy(table[:, :], t_full[:, :]))
            link(tt(t_full[lo, :], t_full[lo, :], table[lo, :].bitcast(F32), ALU.subtract))
            link(v.tensor_copy(table[lo, :], t_full[lo, :]))
            mark(tt(knot_step[:, :], knots[:, 1:K], knots[:, 0:K - 1], ALU.subtract))
            link(ts(inv_temp[:, :], inv_temp[:, :], TEMP_EPS, None, ALU.add))
            link(v.reciprocal(inv_temp[:, :], inv_temp[:, :]))
            dve.wait_ge(s_pe, 9)
            bank2 = banks[2][:, :].rearrange("p (c d) -> p c d", c=KC)
            mark(v.tensor_copy(m_hi[:, :, 0:D], bank2))
            link(v.tensor_copy(m_hi[:, :, D:VW], steps[:, 0:1].unsqueeze(1).broadcast_to([P, KC, 2])))
            mark(tt(m_lo[:, :, 0:D], bank2, m_hi[:, :, 0:D].bitcast(F32), ALU.subtract))
            mark(v.tensor_copy(m_lo[:, :, D:VW], steps[:, 0:1].unsqueeze(1).broadcast_to([P, KC, 2])))
            tcol = comp[:, 0:KC, 0]
            link(ts(tcol, banks[3][:, 0:KC], SCALE, None, ALU.mult))
            link(v.tensor_copy(m_hi[:, :, D], tcol))
            link(tt(m_lo[:, :, D], tcol, m_hi[:, :, D].bitcast(F32), ALU.subtract))
            mark(v.tensor_copy(g_bias[:, :], banks[3][:, KC:2 * KC]))
            mark(tt(vb2[:, 0:D], banks[4][0:2, 0:D], bo2[:, :], ALU.add))
            link(ts(vb2[:, D:D + 1], banks[4][0:2, D:D + 1], SCALE, None, ALU.mult))
            link(v.tensor_copy(vb2_hi[:, :], vb2[:, :]))
            link(tt(vb2_lo[:, :], vb2[:, :], vb2_hi[:, :].bitcast(F32), ALU.subtract))
            link(ts(vb2_lo[:, :], vb2_lo[:, :], ident[0:2, 1:2], None, ALU.mult))
            link(stt(out=vbias[:, :], in0=vb2_hi[:, :].bitcast(F32), scalar=ident[0:2, 0:1], in1=vb2_lo[:, :],
                     op0=ALU.mult, op1=ALU.add))
            mark(ts(ones2[:, :], ident[0:2, :], 0.0, 1.0, ALU.mult, ALU.add))
            assert n[0] == DVE_SETUP, n

            def superstep(k):
                for i in range(0, 4):
                    c_calibrate(k - 3, local=False, i=i)
                b_max(k - 2, 0, 0)
                for i in range(4, 7):
                    c_calibrate(k - 3, local=False, i=i)
                c_hidden(k - 3)
                b_rinv(k - 2, 0, 0)
                for i in range(1, 3):
                    b_max(k - 2, 0, i)
                for i in range(7, 10):
                    c_calibrate(k - 3, local=False, i=i)
                b_rinv(k - 2, 0, 1)
                b_split(k - 2, 1, 0)
                c_calibrate(k - 3, local=False, i=10)
                c_best(k - 3, local=False, i=0)
                b_gate(k - 2, 0, 0)
                c_best(k - 3, local=False, i=1)
                b_rinv(k - 2, 0, 2)
                b_split(k - 2, 1, 1)
                c_best(k - 3, local=False, i=2)
                b_max(k - 2, 0, 3)
                for i in range(3, 5):
                    c_best(k - 3, local=False, i=i)
                for i in range(0, 4):
                    c_pick(k - 3, i)
                b_gate(k - 2, 0, 1)
                b_max(k - 2, 1, 0)
                for i in range(0, 3):
                    c_calibrate(k - 3, local=True, i=i)
                b_rinv(k - 2, 0, 3)
                for i in range(3, 7):
                    c_calibrate(k - 3, local=True, i=i)
                b_rinv(k - 2, 1, 0)
                b_stats(k - 2, 0, 0)
                b_gate(k - 2, 0, 2)
                for i in range(1, 3):
                    b_max(k - 2, 1, i)
                for i in range(7, 10):
                    c_calibrate(k - 3, local=True, i=i)
                b_gate(k - 2, 0, 3)
                c_calibrate(k - 3, local=True, i=10)
                for i in range(0, 4):
                    c_best(k - 3, local=True, i=i)
                b_rinv(k - 2, 1, 1)
                c_best(k - 3, local=True, i=4)
                for i in range(0, 3):
                    c_onehot(k - 3, i)
                b_gate(k - 2, 1, 0)
                b_rinv(k - 2, 1, 2)
                b_max(k - 2, 1, 3)
                for i in range(1, 3):
                    b_stats(k - 2, 0, i)
                b_gate(k - 2, 1, 1)
                c_comp(k - 3, 0)
                b_stats(k - 2, 0, 3)
                b_rinv(k - 2, 1, 3)
                for i in range(0, 2):
                    a_stats(k - 1, 0, i)
                c_comp(k - 3, 1)
                b_gate(k - 2, 1, 2)
                for i in range(2, 4):
                    a_stats(k - 1, 0, i)
                b_stats(k - 2, 1, 0)
                a_var(k - 1, 0, 0)
                for i in range(1, 3):
                    b_stats(k - 2, 1, i)
                for i in range(1, 3):
                    a_var(k - 1, 0, i)
                b_gate(k - 2, 1, 3)
                for i in range(0, 2):
                    c_spline(k - 3, i)
                a_var(k - 1, 0, 3)
                b_stats(k - 2, 1, 3)
                c_spline(k - 3, 2)
                c_var(k - 2, 0)
                a_norm(k - 1, 0, 0)
                for i in range(1, 3):
                    c_var(k - 2, i)
                a_norm(k - 1, 0, 1)
                c_var(k - 2, 3)
                for i in range(2, 4):
                    a_norm(k - 1, 0, i)
                for i in range(3, 5):
                    c_spline(k - 3, i)
                c_norm(k - 2, 0)
                c_spline(k - 3, 5)
                c_norm(k - 2, 1)
                c_spline(k - 3, 6)
                for i in range(2, 4):
                    c_norm(k - 2, i)
                c_y(k - 3, 0)
                c_xhat2(k - 2, 0)
                c_y(k - 3, 1)
                for i in range(1, 5):
                    c_xhat2(k - 2, i)
                c_y(k - 3, 2)
                a_stats(k - 1, 1, 0)
                c_stats(k - 3, 0)
                for i in range(1, 3):
                    a_stats(k - 1, 1, i)
                c_xhat2(k - 2, 5)
                a_stats(k - 1, 1, 3)
                c_xhat2(k - 2, 6)
                a_var(k - 1, 1, 0)
                c_xhat2(k - 2, 7)
                for i in range(1, 3):
                    a_var(k - 1, 1, i)
                c_stats(k - 3, 1)
                a_var(k - 1, 1, 3)
                c_y(k - 3, 3)
                c_stats(k - 3, 2)
                a_norm(k - 1, 1, 0)
                c_split(k - 2, 0)
                for i in range(1, 3):
                    a_norm(k - 1, 1, i)
                c_stats(k - 3, 3)
                a_norm(k - 1, 1, 3)
                c_split(k - 2, 1)
                for i in range(4, 7):
                    c_y(k - 3, i)
                c_stats(k - 3, 4)
                c_y(k - 3, 7)
                c_split(k - 2, 2)
                for i in range(5, 8):
                    c_stats(k - 3, i)
                c_split(k - 2, 3)
                for i in range(0, 4):
                    c_var3(k - 3, i)
                b_split(k - 1, 0, 0)
                for i in range(0, 4):
                    c_norm3(k - 3, i)
                b_split(k - 1, 0, 1)
                c_z(k - 2)

            pipeline(dve, superstep)


_INS = ['L0_attn_x', 'L0_attn_Wq', 'L0_attn_bq', 'L0_attn_Wk', 'L0_attn_bk', 'L0_attn_Wv', 'L0_attn_bv', 'L0_attn_Wo',
        'L0_attn_bo', 'L0_ffn_signatures_raw', 'L0_ffn_knot_values', 'L0_ffn_temperature', 'L0_ffn_compress_w1',
        'L0_ffn_compress_b1', 'L0_ffn_compress_w2', 'L0_ffn_compress_b2', 'L0_ffn_spline_w1', 'L0_ffn_spline_b1',
        'L0_ffn_spline_w2', 'L0_ffn_spline_b2', 'L0_ffn_directions', 'L0_ffn_norm_gamma', 'L0_ffn_norm_beta',
        'L0_ffn_output_scale', 'L0_c', 'L0_wmod']


def kernel(**inputs):
    import numpy as np
    import concourse.bacc as bacc
    from concourse.bass_utils import run_bass_kernel_spmd

    nc = bacc.Bacc("TRN2", target_bir_lowering=False, num_devices=1)
    arrays, args = {}, {}
    for name in _INS:
        a = np.ascontiguousarray(inputs[name])
        arrays[f"in_{name}"] = a
        args[name] = nc.dram_tensor(f"in_{name}", a.shape, mybir.dt.from_np(a.dtype), kind="ExternalInput").ap()
    shape = arrays["in_L0_attn_x"].shape
    out = nc.dram_tensor("out", shape, F32, kind="ExternalOutput").ap()
    adaln_kernel(nc, args, out)
    r = run_bass_kernel_spmd(nc, [arrays], core_ids=[0])
    return r.results[0]["out"]
```
